# Optimizing a Trainium2 kernel written in Bass

```python
import numpy as np
import jax
import jax.numpy as jnp

def _softmax(x, axis=-1):
    return jax.nn.softmax(x, axis=axis)

def _gelu(x):
    return jax.nn.gelu(x, approximate=True)

def _silu(x):
    return jax.nn.silu(x)

def _sigmoid(x):
    return jax.nn.sigmoid(x)

def _layernorm(x, axis=-1, eps=1e-05):
    m = jnp.mean(x, axis=axis, keepdims=True)
    v = jnp.var(x, axis=axis, keepdims=True)
    return (x - m) / jnp.sqrt(v + eps)

def _scatter_add(tgt, idx, src, axis=0):
    return tgt.at[idx].add(src)

def _segment_sum(src, seg, n):
    return jax.ops.segment_sum(src, seg, n)
kernel_name = 'mk_perceiver_d4_seqx_r8_5e0c7f'

def setup_inputs(seed: int=0):
    np.random.seed(seed)
    _w = jnp.asarray

    def _rec_inputs():
        import jax
        import jax.numpy as jnp
        _rk = jax.random.key(seed)
        x = -0.0003929 + 0.9999 * jax.random.normal(jax.random.fold_in(_rk, 1), (128, 32, 128), jnp.float32)
        _lenS = 32 - jax.random.randint(jax.random.fold_in(_rk, 7), (128,), 0, max(1, 32 // 4) + 1, jnp.int32)
        _lenS2 = 257 - jax.random.randint(jax.random.fold_in(_rk, 8), (128,), 0, max(1, 257 // 4) + 1, jnp.int32)
        _ctx_2048P = jax.random.normal(jax.random.fold_in(_rk, 11), (128, 16, 256), jnp.float32)
        _ctx_2048c = jax.random.dirichlet(jax.random.fold_in(_rk, 511), 0.3 * jnp.ones((16,), jnp.float32), (128, 257))
        _ctx_2048t = jnp.einsum('bsk,bkd->bsd', _ctx_2048c, _ctx_2048P)
        _ctx_2048t = _ctx_2048t * jax.lax.rsqrt(jnp.mean(jnp.square(_ctx_2048t)) + 1e-12) * 0.953939
        ctx_2048 = 4.13588e-05 + 0.999923 * (_ctx_2048t + 0.3 * jax.random.normal(jax.random.fold_in(_rk, 611), (128, 257, 256), jnp.float32))
        _validS = jnp.arange(32)[None, :] < _lenS[:, None]
        _validS2 = jnp.arange(257)[None, :] < _lenS2[:, None]
        _causal = jnp.tril(jnp.ones((32, 32), dtype=bool))
        mask_BxS2_if0 = jnp.where(jnp.ones((128, 257), dtype=bool), 4, 0).astype(jnp.int32)
        return (x, ctx_2048, mask_BxS2_if0)
    x, ctx_2048, mask_BxS2_if0 = _rec_inputs()

    def _L0_xattn_setup():
        import jax, jax.numpy as jnp
        import numpy as np
        B, L, P = (4, 512, 128)
        D_MODEL = 128
        D_GLOBAL = 256
        HEADDIM = 32
        EPSILON = 0.001
        RMS_EPS = 1e-05

        def rmsnorm(x, g, eps=RMS_EPS):
            var = jnp.mean(jnp.square(x), axis=-1, keepdims=True)
            return x * jax.lax.rsqrt(var + eps) * g

        def _hnet_depool(h, h_patch_full, patch_lens):
            h_patch = h_patch_full[..., :D_MODEL]
            bsz, plen = (h_patch.shape[0], h_patch.shape[1])
            seqlen = h.shape[1]
            logp = jnp.full((bsz, plen), -EPSILON, dtype=jnp.float32)
            bidx = jnp.cumsum(patch_lens, axis=1) - 1
            boundary_mask = jnp.zeros((bsz, seqlen), dtype=jnp.int32)
            boundary_mask = boundary_mask.at[jnp.arange(bsz)[:, None], bidx].set(1)
            dt = (-jnp.log(-jnp.expm1(logp))).astype(h_patch.dtype)
            x = h_patch / dt[..., None]
            n_heads = D_MODEL // HEADDIM
            A = -jnp.ones((n_heads,), dtype=jnp.float32)
            bcoef = jnp.exp(logp).astype(h_patch.dtype)
            x4 = x.reshape(bsz, plen, n_heads, HEADDIM)
            a = jnp.exp(dt[:, :, None] * A[None, None, :])
            u = (dt * bcoef)[:, :, None, None] * x4
            a_b = jnp.broadcast_to(a[..., None], u.shape)

            def comb(lft, rgt):
                aL, uL = lft
                aR, uR = rgt
                return (aL * aR, uL * aR + uR)
            _, s = jax.lax.associative_scan(comb, (a_b, u), axis=1)
            depool = s.reshape(bsz, plen, D_MODEL)
            plug = jnp.clip(jnp.cumsum(boundary_mask, axis=1) - 1, 0, plen - 1)
            depool_out = depool[jnp.arange(bsz)[:, None], plug]
            return depool_out + h
        key = jax.random.key(seed)
        k1, k2, k3, k4 = jax.random.split(key, 4)
        embeds = jax.random.normal(k1, (B, L, D_MODEL), dtype=jnp.float32)
        patch_embeds = jax.random.normal(k2, (B, P, D_GLOBAL), dtype=jnp.float32)
        patch_lens = jnp.full((B, P), L // P, dtype=jnp.int64)
        W_in = jax.random.normal(k3, (D_MODEL, D_MODEL), dtype=jnp.float32) * 0.02
        b_in = jnp.zeros((D_MODEL,), dtype=jnp.float32)
        g_res = jnp.ones((D_MODEL,), dtype=jnp.float32)
        g_init = jnp.ones((D_GLOBAL,), dtype=jnp.float32)
        return {'embeds': embeds, 'patch_embeds': patch_embeds, 'patch_lens': patch_lens, 'W_in': W_in, 'b_in': b_in, 'g_res': g_res, 'g_init': g_init}
    _L0_xattn_all = _L0_xattn_setup()
    _L0_xattn_in = {k: v for k, v in _L0_xattn_all.items() if k in ('W_in', 'b_in', 'g_res', 'g_init')}
    del _L0_xattn_all

    def _L0_attn_setup():
        import jax, jax.numpy as jnp
        import numpy as np
        import math
        B, S, D = (2, 256, 128)
        HQ, HKV = (16, 4)
        HD = D // HQ
        N_REP = HQ // HKV
        WINDOW = 32
        ROPE_BASE = 10000.0

        def _rope(x):
            s, hd = (x.shape[1], x.shape[-1])
            inv_freq = 1.0 / ROPE_BASE ** (jnp.arange(0, hd, 2, dtype=jnp.float32) / hd)
            ang = jnp.arange(s, dtype=jnp.float32)[:, None] * inv_freq
            cos = jnp.cos(ang)[None, :, None, :].astype(x.dtype)
            sin = jnp.sin(ang)[None, :, None, :].astype(x.dtype)
            x1, x2 = (x[..., ::2], x[..., 1::2])
            out = jnp.stack([x1 * cos - x2 * sin, x1 * sin + x2 * cos], axis=-1)
            return out.reshape(x.shape)
        key = jax.random.key(seed)
        ks = jax.random.split(key, 5)
        sc = 0.02
        return {'x': jax.random.normal(ks[0], (B, S, D), dtype=jnp.float32), 'Wq': jax.random.normal(ks[1], (D, HQ * HD), dtype=jnp.float32) * sc, 'Wk': jax.random.normal(ks[2], (D, HKV * HD), dtype=jnp.float32) * sc, 'Wv': jax.random.normal(ks[3], (D, HKV * HD), dtype=jnp.float32) * sc, 'Wo': jax.random.normal(ks[4], (HQ * HD, D), dtype=jnp.float32) * sc}
    _L0_attn_all = _L0_attn_setup()
    _L0_attn_in = {k: v for k, v in _L0_attn_all.items() if k in ('Wq', 'Wk', 'Wv', 'Wo')}
    del _L0_attn_all

    def _L0_ffn_setup():
        import jax, jax.numpy as jnp
        import numpy as np
        H = 8
        KD = 128
        TOPK = 8
        NUM_KEYS = 32
        N_EXPERTS = NUM_KEYS * NUM_KEYS
        N_DIM = 128
        BN_EPS = 1e-05

        def gelu_new(x):
            c = jnp.sqrt(jnp.asarray(2.0 / jnp.pi, x.dtype))
            return 0.5 * x * (1.0 + jnp.tanh(c * (x + 0.044715 * x * x * x)))
        key = jax.random.key(seed)
        ks = jax.random.split(key, 5)
        b, s = (2, 128)
        x = jax.random.normal(ks[0], (b, s, N_DIM), dtype=jnp.float32)
        w_q = jax.random.normal(ks[1], (N_DIM, 2 * H * KD), dtype=jnp.float32) * 0.02
        bn_gamma = jnp.ones((2 * H * KD,), dtype=jnp.float32)
        bn_beta = jnp.zeros((2 * H * KD,), dtype=jnp.float32)
        keys = jax.random.normal(ks[2], (H, NUM_KEYS, 2, KD), dtype=jnp.float32) * 0.02
        down_embed = jax.random.normal(ks[3], (N_EXPERTS, N_DIM), dtype=jnp.float32) * 0.02
        up_embed = jax.random.normal(ks[4], (N_EXPERTS, N_DIM), dtype=jnp.float32) * 0.02
        return {'x': x, 'w_q': w_q, 'bn_gamma': bn_gamma, 'bn_beta': bn_beta, 'keys': keys, 'down_embed': down_embed, 'up_embed': up_embed}
    _L0_ffn_all = _L0_ffn_setup()
    _L0_ffn_in = {k: v for k, v in _L0_ffn_all.items() if k in ('w_q', 'bn_gamma', 'bn_beta', 'keys', 'down_embed', 'up_embed')}
    del _L0_ffn_all

    def _L1_xattn_setup():
        import jax, jax.numpy as jnp
        import numpy as np
        NUM_HEADS = 16
        key = jax.random.key(seed)
        ks = jax.random.split(key, 5)
        dim = 128
        B, N, N_c = (4, 128, 32)
        x = jax.random.normal(ks[0], (B, N, dim), dtype=jnp.float32)
        context = jax.random.normal(ks[1], (B, N_c, 2 * dim), dtype=jnp.float32)
        w_qkv = jax.random.normal(ks[2], (3 * dim, dim), dtype=jnp.float32) * 0.02
        w_proj = jax.random.normal(ks[3], (dim, dim), dtype=jnp.float32) * 0.02
        b_proj = jax.random.normal(ks[4], (dim,), dtype=jnp.float32) * 0.02
        return {'x': x, 'context': context, 'w_qkv': w_qkv, 'w_proj': w_proj, 'b_proj': b_proj}
    _L1_xattn_all = _L1_xattn_setup()
    _L1_xattn_in = {k: v for k, v in _L1_xattn_all.items() if k in ('w_qkv', 'w_proj', 'b_proj')}
    del _L1_xattn_all

    def _L1_attn_setup():
        import jax, jax.numpy as jnp
        import numpy as np
        D_MODEL, D_STATE, D_CONV, D_INNER = (128, 16, 4, 256)
        BATCH, SEQLEN = (4, 256)

        def _mamba_fwd(x, W_in, conv_w, W_x, W_dt, b_dt, W_Bp, D_param, W_out):
            B, L, _ = x.shape
            xz = x @ W_in
            xc, z = jnp.split(xz, 2, axis=-1)
            xt = jnp.transpose(xc, (0, 2, 1))
            xt = jax.lax.conv_general_dilated(xt, conv_w, window_strides=(1,), padding=[(D_CONV - 1, 0)], dimension_numbers=('NCH', 'OIH', 'NCH'), feature_group_count=D_INNER)
            u = jax.nn.silu(jnp.transpose(xt, (0, 2, 1)))
            xp = u @ W_x
            dt_raw, B_raw = jnp.split(xp, 2, axis=-1)
            dt = jax.nn.softplus(dt_raw @ W_dt + b_dt)
            Bp = B_raw @ W_Bp
            dt = jnp.clip(dt, 0.0001, 1.0)
            ub = u * Bp

            def step(h, inp):
                d_t, ub_t = inp
                h = h * (1.0 - d_t) + ub_t
                return (h, h)
            _, ys = jax.lax.scan(step, jnp.zeros((B, D_INNER), x.dtype), (jnp.transpose(dt, (1, 0, 2)), jnp.transpose(ub, (1, 0, 2))))
            y = jnp.transpose(ys, (1, 0, 2)) + D_param * u
            y = y * jax.nn.silu(z)
            return y @ W_out
        key = jax.random.key(seed)
        ks = jax.random.split(key, 8)
        x = jax.random.normal(ks[0], (BATCH, SEQLEN, D_MODEL), jnp.float32)
        W_in = jax.random.normal(ks[1], (D_MODEL, 2 * D_INNER), jnp.float32) / np.float32(np.sqrt(D_MODEL))
        conv_w = jax.random.normal(ks[2], (D_INNER, 1, D_CONV), jnp.float32) * np.float32(0.3)
        W_x = jax.random.normal(ks[3], (D_INNER, 2 * D_STATE), jnp.float32) / np.float32(np.sqrt(D_INNER))
        W_dt = jax.random.normal(ks[4], (D_STATE, D_INNER), jnp.float32) / np.float32(np.sqrt(D_STATE))
        b_dt = jax.random.normal(ks[5], (D_INNER,), jnp.float32) * np.float32(0.1)
        W_Bp = jax.random.normal(ks[6], (D_STATE, D_INNER), jnp.float32) / np.float32(np.sqrt(D_STATE))
        D_param = jnp.ones((D_INNER,), jnp.float32)
        W_out = jax.random.normal(ks[7], (D_INNER, D_MODEL), jnp.float32) / np.float32(np.sqrt(D_INNER))
        return {'x': x, 'W_in': W_in, 'conv_w': conv_w, 'W_x': W_x, 'W_dt': W_dt, 'b_dt': b_dt, 'W_Bp': W_Bp, 'D_param': D_param, 'W_out': W_out}
    _L1_attn_all = _L1_attn_setup()
    _L1_attn_in = {k: v for k, v in _L1_attn_all.items() if k in ('W_in', 'conv_w', 'W_x', 'W_dt', 'b_dt', 'W_Bp', 'D_param', 'W_out')}
    del _L1_attn_all

    def _L1_ffn_setup():
        import jax, jax.numpy as jnp
        import numpy as np
        EPS = 1e-06
        LN_EPS = 1e-05

        def _absmean_core(W):
            gamma = jnp.mean(jnp.abs(W)) + EPS
            Ws = W / gamma
            Wq = jnp.sign(Ws) * jnp.minimum(jnp.round(jnp.abs(Ws)), 1.0)
            return (Wq, gamma)

        @jax.custom_vjp
        def absmean(W):
            return _absmean_core(W)[0]

        def _absmean_fwd(W):
            Wq, gamma = _absmean_core(W)
            return (Wq, gamma)

        def _absmean_bwd(gamma, g):
            return (g / gamma,)
        absmean.defvjp(_absmean_fwd, _absmean_bwd)

        def layernorm(x, w, b, eps=LN_EPS):
            mu = jnp.mean(x, axis=-1, keepdims=True)
            var = jnp.mean((x - mu) ** 2, axis=-1, keepdims=True)
            return (x - mu) * jax.lax.rsqrt(var + eps) * w + b
        key = jax.random.key(seed)
        k1, k2, k3 = jax.random.split(key, 3)
        d, h = (128, 512)
        B, T = (8, 256)
        return {'x': jax.random.normal(k1, (B, T, d), jnp.float32), 'W_fc': jax.random.normal(k2, (h, d), jnp.float32), 'ln_w': jnp.ones((h,), jnp.float32), 'ln_b': jnp.zeros((h,), jnp.float32), 'W_proj': jax.random.normal(k3, (d, h), jnp.float32)}
    _L1_ffn_all = _L1_ffn_setup()
    _L1_ffn_in = {k: v for k, v in _L1_ffn_all.items() if k in ('W_fc', 'ln_w', 'ln_b', 'W_proj')}
    del _L1_ffn_all

    def _L2_xattn_setup():
        import jax, jax.numpy as jnp
        import numpy as np
        B, N, DIM = (8, 512, 128)
        M, CTX = (32, 256)
        HEADS, DH = (16, 64)
        INNER = HEADS * DH
        EPS = 1e-06

        def _split_heads(t):
            b, n, _ = t.shape
            return t.reshape(b, n, HEADS, DH).transpose(0, 2, 1, 3)
        key = jax.random.key(seed)
        ks = jax.random.split(key, 6)
        x = jax.random.normal(ks[0], (B, N, DIM), dtype=jnp.float32)
        context = jax.random.normal(ks[1], (B, M, CTX), dtype=jnp.float32)
        Wq = jax.random.normal(ks[2], (DIM, INNER), dtype=jnp.float32) / np.sqrt(DIM)
        Wkv = jax.random.normal(ks[3], (CTX, 2 * INNER), dtype=jnp.float32) / np.sqrt(CTX)
        null_kv = jax.random.normal(ks[4], (2, DH), dtype=jnp.float32) / np.sqrt(2.0)
        Wout = jax.random.normal(ks[5], (INNER, DIM), dtype=jnp.float32) / np.sqrt(INNER)
        ln_scale = jnp.ones((DIM,), dtype=jnp.float32)
        ln_bias = jnp.zeros((DIM,), dtype=jnp.float32)
        return {'x': x, 'context': context, 'Wq': Wq, 'Wkv': Wkv, 'null_kv': null_kv, 'Wout': Wout, 'ln_scale': ln_scale, 'ln_bias': ln_bias}
    _L2_xattn_all = _L2_xattn_setup()
    _L2_xattn_in = {k: v for k, v in _L2_xattn_all.items() if k in ('Wq', 'Wkv', 'null_kv', 'Wout', 'ln_scale', 'ln_bias')}
    del _L2_xattn_all

    def _L2_attn_setup():
        import jax, jax.numpy as jnp
        import numpy as np
        B, T, D, H = (4, 128, 128, 16)
        key = jax.random.key(seed)
        ks = jax.random.split(key, 7)
        x = jax.random.normal(ks[0], (B, T, D), dtype=jnp.float32)
        scale = 0.02
        Wq = jax.random.normal(ks[1], (D, D), dtype=jnp.float32) * scale
        Wk = jax.random.normal(ks[2], (D, D), dtype=jnp.float32) * scale
        Wv = jax.random.normal(ks[3], (D, D), dtype=jnp.float32) * scale
        bq = jax.random.normal(ks[4], (D,), dtype=jnp.float32) * scale
        bk = jax.random.normal(ks[5], (D,), dtype=jnp.float32) * scale
        bv = jax.random.normal(ks[6], (D,), dtype=jnp.float32) * scale
        temperature = jnp.ones((H, 1, 1), dtype=jnp.float32)
        return {'x': x, 'Wq': Wq, 'bq': bq, 'Wk': Wk, 'bk': bk, 'Wv': Wv, 'bv': bv, 'temperature': temperature}
    _L2_attn_all = _L2_attn_setup()
    _L2_attn_in = {k: v for k, v in _L2_attn_all.items() if k in ('Wq', 'bq', 'Wk', 'bk', 'Wv', 'bv', 'temperature')}
    del _L2_attn_all

    def _L2_ffn_setup():
        import jax, jax.numpy as jnp
        import numpy as np
        QP = 127.0
        MIN_RANGE = 1e-06

        def _ste_round(x):
            return x + jax.lax.stop_gradient(jnp.round(x) - x)

        def _quant_per_tensor(x):
            scale = jnp.maximum(jnp.max(jnp.abs(x)), MIN_RANGE) / QP
            return (_ste_round(x / scale), scale)

        def _qlinear(x2d, w, b):
            xq, sx = _quant_per_tensor(x2d)
            wq, sw = _quant_per_tensor(w)
            out = jnp.matmul(xq, wq.T) + b[None, :]
            return out * (sw * sx)
        key = jax.random.key(seed)
        k = jax.random.split(key, 5)
        B, N, D, H = (8, 128, 128, 512)
        return {'x': jax.random.normal(k[0], (B, N, D), dtype=jnp.float32), 'w1': jax.random.normal(k[1], (H, D), dtype=jnp.float32) * 0.02, 'b1': jax.random.normal(k[2], (H,), dtype=jnp.float32) * 0.02, 'w2': jax.random.normal(k[3], (D, H), dtype=jnp.float32) * 0.02, 'b2': jax.random.normal(k[4], (D,), dtype=jnp.float32) * 0.02}
    _L2_ffn_all = _L2_ffn_setup()
    _L2_ffn_in = {k: v for k, v in _L2_ffn_all.items() if k in ('w1', 'b1', 'w2', 'b2')}
    del _L2_ffn_all

    def _L3_xattn_setup():
        import jax, jax.numpy as jnp
        import numpy as np
        B, L, P = (4, 512, 128)
        D_MODEL = 128
        D_GLOBAL = 256
        HEADDIM = 32
        EPSILON = 0.001
        RMS_EPS = 1e-05

        def rmsnorm(x, g, eps=RMS_EPS):
            var = jnp.mean(jnp.square(x), axis=-1, keepdims=True)
            return x * jax.lax.rsqrt(var + eps) * g

        def _hnet_depool(h, h_patch_full, patch_lens):
            h_patch = h_patch_full[..., :D_MODEL]
            bsz, plen = (h_patch.shape[0], h_patch.shape[1])
            seqlen = h.shape[1]
            logp = jnp.full((bsz, plen), -EPSILON, dtype=jnp.float32)
            bidx = jnp.cumsum(patch_lens, axis=1) - 1
            boundary_mask = jnp.zeros((bsz, seqlen), dtype=jnp.int32)
            boundary_mask = boundary_mask.at[jnp.arange(bsz)[:, None], bidx].set(1)
            dt = (-jnp.log(-jnp.expm1(logp))).astype(h_patch.dtype)
            x = h_patch / dt[..., None]
            n_heads = D_MODEL // HEADDIM
            A = -jnp.ones((n_heads,), dtype=jnp.float32)
            bcoef = jnp.exp(logp).astype(h_patch.dtype)
            x4 = x.reshape(bsz, plen, n_heads, HEADDIM)
            a = jnp.exp(dt[:, :, None] * A[None, None, :])
            u = (dt * bcoef)[:, :, None, None] * x4
            a_b = jnp.broadcast_to(a[..., None], u.shape)

            def comb(lft, rgt):
                aL, uL = lft
                aR, uR = rgt
                return (aL * aR, uL * aR + uR)
            _, s = jax.lax.associative_scan(comb, (a_b, u), axis=1)
            depool = s.reshape(bsz, plen, D_MODEL)
            plug = jnp.clip(jnp.cumsum(boundary_mask, axis=1) - 1, 0, plen - 1)
            depool_out = depool[jnp.arange(bsz)[:, None], plug]
            return depool_out + h
        key = jax.random.key(seed)
        k1, k2, k3, k4 = jax.random.split(key, 4)
        embeds = jax.random.normal(k1, (B, L, D_MODEL), dtype=jnp.float32)
        patch_embeds = jax.random.normal(k2, (B, P, D_GLOBAL), dtype=jnp.float32)
        patch_lens = jnp.full((B, P), L // P, dtype=jnp.int64)
        W_in = jax.random.normal(k3, (D_MODEL, D_MODEL), dtype=jnp.float32) * 0.02
        b_in = jnp.zeros((D_MODEL,), dtype=jnp.float32)
        g_res = jnp.ones((D_MODEL,), dtype=jnp.float32)
        g_init = jnp.ones((D_GLOBAL,), dtype=jnp.float32)
        return {'embeds': embeds, 'patch_embeds': patch_embeds, 'patch_lens': patch_lens, 'W_in': W_in, 'b_in': b_in, 'g_res': g_res, 'g_init': g_init}
    _L3_xattn_all = _L3_xattn_setup()
    _L3_xattn_in = {k: v for k, v in _L3_xattn_all.items() if k in ('W_in', 'b_in', 'g_res', 'g_init')}
    del _L3_xattn_all

    def _L3_attn_setup():
        import jax, jax.numpy as jnp
        import numpy as np
        EPS = 1e-08
        GROUPS = 128

        def log_g(x):
            return jnp.where(x >= 0, jnp.log(jax.nn.relu(x) + 0.5 + EPS), -jax.nn.softplus(-x) + EPS)

        def grouped_linear(x, W):
            B, S, D = x.shape
            G = W.shape[0]
            xg = x.reshape(B, S, G, D // G)
            y = jnp.einsum('bsgi,goi->bsgo', xg, W)
            return y.reshape(B, S, -1)

        def parallel_scan_log(log_coeffs, log_values):
            a_star = jnp.cumsum(log_coeffs + EPS, axis=1)
            log_h0_plus_b_star = jax.lax.cumlogsumexp(log_values - a_star, axis=1)
            return jnp.exp(a_star + log_h0_plus_b_star)
        key = jax.random.key(seed)
        k_x, k_f, k_i, k_h = jax.random.split(key, 4)
        B, S, D, H = (4, 1024, 128, 128)
        din_g, dout_g = (D // GROUPS, H // GROUPS)
        fan_in = din_g
        bound = 1.0 / np.sqrt(fan_in)
        x_t = jax.random.normal(k_x, (B, S, D), dtype=jnp.float32)
        Wf = jax.random.uniform(k_f, (GROUPS, dout_g, din_g), jnp.float32, -bound, bound)
        Wi = jax.random.uniform(k_i, (GROUPS, dout_g, din_g), jnp.float32, -bound, bound)
        Wh = jax.random.uniform(k_h, (GROUPS, dout_g, din_g), jnp.float32, -bound, bound)
        return {'x_t': x_t, 'Wf': Wf, 'Wi': Wi, 'Wh': Wh}
    _L3_attn_all = _L3_attn_setup()
    _L3_attn_in = {k: v for k, v in _L3_attn_all.items() if k in ('Wf', 'Wi', 'Wh')}
    del _L3_attn_all

    def _L3_ffn_setup():
        import jax, jax.numpy as jnp
        import numpy as np
        B, S, D, O, E, R = (8, 256, 128, 128, 8, 4)
        TOP_K = 2
        SCALING = 4.0 / 4.0
        key = jax.random.key(seed)
        k0, k1, k2, k3, k4 = jax.random.split(key, 5)
        hidden_states = jax.random.normal(k0, (B, S, D), dtype=jnp.float32)
        W_lin = jax.random.normal(k1, (O, D), dtype=jnp.float32) * 0.02
        b_lin = jnp.zeros((O,), dtype=jnp.float32)
        gate_w = jax.random.normal(k2, (E, D), dtype=jnp.float32) * 0.02
        left = jax.random.normal(k3, (E, D, R), dtype=jnp.float32) * 0.02
        right = jax.random.normal(k4, (E, R, O), dtype=jnp.float32) * 0.02
        return {'hidden_states': hidden_states, 'W_lin': W_lin, 'b_lin': b_lin, 'gate_w': gate_w, 'left': left, 'right': right}
    _L3_ffn_all = _L3_ffn_setup()
    _L3_ffn_in = {k: v for k, v in _L3_ffn_all.items() if k in ('W_lin', 'b_lin', 'gate_w', 'left', 'right')}
    del _L3_ffn_all
    return {'x': x, 'ctx_2048': ctx_2048, 'mask_BxS2_if0': mask_BxS2_if0, 'L0_xattn_W_in': _L0_xattn_in['W_in'], 'L0_xattn_b_in': _L0_xattn_in['b_in'], 'L0_xattn_g_res': _L0_xattn_in['g_res'], 'L0_xattn_g_init': _L0_xattn_in['g_init'], 'L0_attn_Wq': _L0_attn_in['Wq'], 'L0_attn_Wk': _L0_attn_in['Wk'], 'L0_attn_Wv': _L0_attn_in['Wv'], 'L0_attn_Wo': _L0_attn_in['Wo'], 'L0_ffn_w_q': _L0_ffn_in['w_q'], 'L0_ffn_bn_gamma': _L0_ffn_in['bn_gamma'], 'L0_ffn_bn_beta': _L0_ffn_in['bn_beta'], 'L0_ffn_keys': _L0_ffn_in['keys'], 'L0_ffn_down_embed': _L0_ffn_in['down_embed'], 'L0_ffn_up_embed': _L0_ffn_in['up_embed'], 'L1_xattn_w_qkv': _L1_xattn_in['w_qkv'], 'L1_xattn_w_proj': _L1_xattn_in['w_proj'], 'L1_xattn_b_proj': _L1_xattn_in['b_proj'], 'L1_attn_W_in': _L1_attn_in['W_in'], 'L1_attn_conv_w': _L1_attn_in['conv_w'], 'L1_attn_W_x': _L1_attn_in['W_x'], 'L1_attn_W_dt': _L1_attn_in['W_dt'], 'L1_attn_b_dt': _L1_attn_in['b_dt'], 'L1_attn_W_Bp': _L1_attn_in['W_Bp'], 'L1_attn_D_param': _L1_attn_in['D_param'], 'L1_attn_W_out': _L1_attn_in['W_out'], 'L1_ffn_W_fc': _L1_ffn_in['W_fc'], 'L1_ffn_ln_w': _L1_ffn_in['ln_w'], 'L1_ffn_ln_b': _L1_ffn_in['ln_b'], 'L1_ffn_W_proj': _L1_ffn_in['W_proj'], 'L2_xattn_Wq': _L2_xattn_in['Wq'], 'L2_xattn_Wkv': _L2_xattn_in['Wkv'], 'L2_xattn_null_kv': _L2_xattn_in['null_kv'], 'L2_xattn_Wout': _L2_xattn_in['Wout'], 'L2_xattn_ln_scale': _L2_xattn_in['ln_scale'], 'L2_xattn_ln_bias': _L2_xattn_in['ln_bias'], 'L2_attn_Wq': _L2_attn_in['Wq'], 'L2_attn_bq': _L2_attn_in['bq'], 'L2_attn_Wk': _L2_attn_in['Wk'], 'L2_attn_bk': _L2_attn_in['bk'], 'L2_attn_Wv': _L2_attn_in['Wv'], 'L2_attn_bv': _L2_attn_in['bv'], 'L2_attn_temperature': _L2_attn_in['temperature'], 'L2_ffn_w1': _L2_ffn_in['w1'], 'L2_ffn_b1': _L2_ffn_in['b1'], 'L2_ffn_w2': _L2_ffn_in['w2'], 'L2_ffn_b2': _L2_ffn_in['b2'], 'L3_xattn_W_in': _L3_xattn_in['W_in'], 'L3_xattn_b_in': _L3_xattn_in['b_in'], 'L3_xattn_g_res': _L3_xattn_in['g_res'], 'L3_xattn_g_init': _L3_xattn_in['g_init'], 'L3_attn_Wf': _L3_attn_in['Wf'], 'L3_attn_Wi': _L3_attn_in['Wi'], 'L3_attn_Wh': _L3_attn_in['Wh'], 'L3_ffn_W_lin': _L3_ffn_in['W_lin'], 'L3_ffn_b_lin': _L3_ffn_in['b_lin'], 'L3_ffn_gate_w': _L3_ffn_in['gate_w'], 'L3_ffn_left': _L3_ffn_in['left'], 'L3_ffn_right': _L3_ffn_in['right']}

def reference(x, ctx_2048, mask_BxS2_if0, L0_xattn_W_in, L0_xattn_b_in, L0_xattn_g_res, L0_xattn_g_init, L0_attn_Wq, L0_attn_Wk, L0_attn_Wv, L0_attn_Wo, L0_ffn_w_q, L0_ffn_bn_gamma, L0_ffn_bn_beta, L0_ffn_keys, L0_ffn_down_embed, L0_ffn_up_embed, L1_xattn_w_qkv, L1_xattn_w_proj, L1_xattn_b_proj, L1_attn_W_in, L1_attn_conv_w, L1_attn_W_x, L1_attn_W_dt, L1_attn_b_dt, L1_attn_W_Bp, L1_attn_D_param, L1_attn_W_out, L1_ffn_W_fc, L1_ffn_ln_w, L1_ffn_ln_b, L1_ffn_W_proj, L2_xattn_Wq, L2_xattn_Wkv, L2_xattn_null_kv, L2_xattn_Wout, L2_xattn_ln_scale, L2_xattn_ln_bias, L2_attn_Wq, L2_attn_bq, L2_attn_Wk, L2_attn_bk, L2_attn_Wv, L2_attn_bv, L2_attn_temperature, L2_ffn_w1, L2_ffn_b1, L2_ffn_w2, L2_ffn_b2, L3_xattn_W_in, L3_xattn_b_in, L3_xattn_g_res, L3_xattn_g_init, L3_attn_Wf, L3_attn_Wi, L3_attn_Wh, L3_ffn_W_lin, L3_ffn_b_lin, L3_ffn_gate_w, L3_ffn_left, L3_ffn_right):
    import jax
    import jax.numpy as jnp

    def _L0_xattn_ref(embeds, patch_embeds, patch_lens, W_in, b_in, g_res, g_init):
        import jax, jax.numpy as jnp
        import numpy as np
        B, L, P = (4, 512, 128)
        D_MODEL = 128
        D_GLOBAL = 256
        HEADDIM = 32
        EPSILON = 0.001
        RMS_EPS = 1e-05

        def rmsnorm(x, g, eps=RMS_EPS):
            var = jnp.mean(jnp.square(x), axis=-1, keepdims=True)
            return x * jax.lax.rsqrt(var + eps) * g

        def _hnet_depool(h, h_patch_full, patch_lens):
            h_patch = h_patch_full[..., :D_MODEL]
            bsz, plen = (h_patch.shape[0], h_patch.shape[1])
            seqlen = h.shape[1]
            logp = jnp.full((bsz, plen), -EPSILON, dtype=jnp.float32)
            bidx = jnp.cumsum(patch_lens, axis=1) - 1
            boundary_mask = jnp.zeros((bsz, seqlen), dtype=jnp.int32)
            boundary_mask = boundary_mask.at[jnp.arange(bsz)[:, None], bidx].set(1)
            dt = (-jnp.log(-jnp.expm1(logp))).astype(h_patch.dtype)
            x = h_patch / dt[..., None]
            n_heads = D_MODEL // HEADDIM
            A = -jnp.ones((n_heads,), dtype=jnp.float32)
            bcoef = jnp.exp(logp).astype(h_patch.dtype)
            x4 = x.reshape(bsz, plen, n_heads, HEADDIM)
            a = jnp.exp(dt[:, :, None] * A[None, None, :])
            u = (dt * bcoef)[:, :, None, None] * x4
            a_b = jnp.broadcast_to(a[..., None], u.shape)

            def comb(lft, rgt):
                aL, uL = lft
                aR, uR = rgt
                return (aL * aR, uL * aR + uR)
            _, s = jax.lax.associative_scan(comb, (a_b, u), axis=1)
            depool = s.reshape(bsz, plen, D_MODEL)
            plug = jnp.clip(jnp.cumsum(boundary_mask, axis=1) - 1, 0, plen - 1)
            depool_out = depool[jnp.arange(bsz)[:, None], plug]
            return depool_out + h
        h = rmsnorm(embeds, g_res)
        h = jnp.einsum('bld,ed->ble', h, W_in) + b_in
        h_patch = rmsnorm(patch_embeds, g_init)
        return _hnet_depool(h, h_patch, patch_lens)

    def _L0_attn_ref(x, Wq, Wk, Wv, Wo):
        import jax, jax.numpy as jnp
        import numpy as np
        import math
        B, S, D = (2, 256, 128)
        HQ, HKV = (16, 4)
        HD = D // HQ
        N_REP = HQ // HKV
        WINDOW = 32
        ROPE_BASE = 10000.0

        def _rope(x):
            s, hd = (x.shape[1], x.shape[-1])
            inv_freq = 1.0 / ROPE_BASE ** (jnp.arange(0, hd, 2, dtype=jnp.float32) / hd)
            ang = jnp.arange(s, dtype=jnp.float32)[:, None] * inv_freq
            cos = jnp.cos(ang)[None, :, None, :].astype(x.dtype)
            sin = jnp.sin(ang)[None, :, None, :].astype(x.dtype)
            x1, x2 = (x[..., ::2], x[..., 1::2])
            out = jnp.stack([x1 * cos - x2 * sin, x1 * sin + x2 * cos], axis=-1)
            return out.reshape(x.shape)
        b, s, _ = x.shape
        xq = (x @ Wq).reshape(b, s, HQ, HD)
        xk = (x @ Wk).reshape(b, s, HKV, HD)
        xv = (x @ Wv).reshape(b, s, HKV, HD)
        xq = _rope(xq)
        xk = _rope(xk)
        keys = jnp.repeat(xk, N_REP, axis=2)
        values = jnp.repeat(xv, N_REP, axis=2)
        scores = jnp.einsum('bqhd,bkhd->bhqk', xq, keys) / math.sqrt(HD)
        idx = jnp.arange(s)
        mask = jnp.abs(idx[:, None] - idx[None, :]) <= WINDOW // 2
        scores = jnp.where(mask[None, None], scores, -jnp.inf)
        attn = jax.nn.softmax(scores.astype(jnp.float32), axis=-1).astype(xq.dtype)
        ctx = jnp.einsum('bhqk,bkhd->bqhd', attn, values).reshape(b, s, HQ * HD)
        return ctx @ Wo

    def _L0_ffn_ref(x, w_q, bn_gamma, bn_beta, keys, down_embed, up_embed):
        import jax, jax.numpy as jnp
        import numpy as np
        H = 8
        KD = 128
        TOPK = 8
        NUM_KEYS = 32
        N_EXPERTS = NUM_KEYS * NUM_KEYS
        N_DIM = 128
        BN_EPS = 1e-05

        def gelu_new(x):
            c = jnp.sqrt(jnp.asarray(2.0 / jnp.pi, x.dtype))
            return 0.5 * x * (1.0 + jnp.tanh(c * (x + 0.044715 * x * x * x)))
        b, n, d = x.shape
        q = jnp.einsum('bnd,de->bne', x, w_q)
        mean = jnp.mean(q, axis=(0, 1))
        var = jnp.var(q, axis=(0, 1))
        q = (q - mean) * jax.lax.rsqrt(var + BN_EPS) * bn_gamma + bn_beta
        q = q.reshape(b, n, 2, H, KD).transpose(2, 0, 1, 3, 4)
        sim = jnp.einsum('pbnhd,hkpd->pbnhk', q, keys)
        sx, ix = jax.lax.top_k(sim[0], TOPK)
        sy, iy = jax.lax.top_k(sim[1], TOPK)
        all_scores = (sx[..., :, None] + sy[..., None, :]).reshape(b, n, H, TOPK * TOPK)
        all_indices = (ix[..., :, None] * NUM_KEYS + iy[..., None, :]).reshape(b, n, H, TOPK * TOPK)
        scores, pk = jax.lax.top_k(all_scores, TOPK)
        indices = jnp.take_along_axis(all_indices, pk, axis=-1)
        wd = down_embed[indices]
        wu = up_embed[indices]
        h = jnp.einsum('bnd,bnhkd->bnhk', x, wd)
        h = gelu_new(h)
        h = jax.nn.softmax(scores, axis=-1) * h
        out = jnp.einsum('bnhk,bnhkd->bnd', h, wu)
        return out

    def _L1_xattn_ref(x, context, w_qkv, w_proj, b_proj):
        import jax, jax.numpy as jnp
        import numpy as np
        NUM_HEADS = 16
        B, N, C = x.shape
        H = NUM_HEADS
        D = C // H
        scale = D ** (-0.5)
        qkv = (x @ w_qkv.T).reshape(B, N, 3, H, D).transpose(2, 0, 3, 1, 4)
        q, k, v = (qkv[0], qkv[1], qkv[2])
        N_c = context.shape[1]
        kv = context.reshape(B, N_c, 2, H, D).transpose(2, 0, 3, 1, 4)
        extra_k, extra_v = (kv[0], kv[1])
        k = jnp.concatenate([extra_k, k], axis=2)
        v = jnp.concatenate([extra_v, v], axis=2)
        dtype = q.dtype
        attn = jnp.einsum('bhnd,bhmd->bhnm', q * scale, k).astype(jnp.float32)
        attn = jax.nn.softmax(attn, axis=-1).astype(dtype)
        out = jnp.einsum('bhnm,bhmd->bhnd', attn, v)
        out = out.transpose(0, 2, 1, 3).reshape(B, N, C)
        return out @ w_proj.T + b_proj

    def _L1_attn_ref(x, W_in, conv_w, W_x, W_dt, b_dt, W_Bp, D_param, W_out):
        import jax, jax.numpy as jnp
        import numpy as np
        D_MODEL, D_STATE, D_CONV, D_INNER = (128, 16, 4, 256)
        BATCH, SEQLEN = (4, 256)

        def _mamba_fwd(x, W_in, conv_w, W_x, W_dt, b_dt, W_Bp, D_param, W_out):
            B, L, _ = x.shape
            xz = x @ W_in
            xc, z = jnp.split(xz, 2, axis=-1)
            xt = jnp.transpose(xc, (0, 2, 1))
            xt = jax.lax.conv_general_dilated(xt, conv_w, window_strides=(1,), padding=[(D_CONV - 1, 0)], dimension_numbers=('NCH', 'OIH', 'NCH'), feature_group_count=D_INNER)
            u = jax.nn.silu(jnp.transpose(xt, (0, 2, 1)))
            xp = u @ W_x
            dt_raw, B_raw = jnp.split(xp, 2, axis=-1)
            dt = jax.nn.softplus(dt_raw @ W_dt + b_dt)
            Bp = B_raw @ W_Bp
            dt = jnp.clip(dt, 0.0001, 1.0)
            ub = u * Bp

            def step(h, inp):
                d_t, ub_t = inp
                h = h * (1.0 - d_t) + ub_t
                return (h, h)
            _, ys = jax.lax.scan(step, jnp.zeros((B, D_INNER), x.dtype), (jnp.transpose(dt, (1, 0, 2)), jnp.transpose(ub, (1, 0, 2))))
            y = jnp.transpose(ys, (1, 0, 2)) + D_param * u
            y = y * jax.nn.silu(z)
            return y @ W_out
        return _mamba_fwd(x, W_in, conv_w, W_x, W_dt, b_dt, W_Bp, D_param, W_out)

    def _L1_ffn_ref(x, W_fc, ln_w, ln_b, W_proj):
        import jax, jax.numpy as jnp
        import numpy as np
        EPS = 1e-06
        LN_EPS = 1e-05

        def _absmean_core(W):
            gamma = jnp.mean(jnp.abs(W)) + EPS
            Ws = W / gamma
            Wq = jnp.sign(Ws) * jnp.minimum(jnp.round(jnp.abs(Ws)), 1.0)
            return (Wq, gamma)

        @jax.custom_vjp
        def absmean(W):
            return _absmean_core(W)[0]

        def _absmean_fwd(W):
            Wq, gamma = _absmean_core(W)
            return (Wq, gamma)

        def _absmean_bwd(gamma, g):
            return (g / gamma,)
        absmean.defvjp(_absmean_fwd, _absmean_bwd)

        def layernorm(x, w, b, eps=LN_EPS):
            mu = jnp.mean(x, axis=-1, keepdims=True)
            var = jnp.mean((x - mu) ** 2, axis=-1, keepdims=True)
            return (x - mu) * jax.lax.rsqrt(var + eps) * w + b
        h = jnp.einsum('btd,hd->bth', x, absmean(W_fc))
        h = jax.nn.gelu(h, approximate=False)
        h = layernorm(h, ln_w, ln_b)
        return jnp.einsum('bth,dh->btd', h, absmean(W_proj))

    def _L2_xattn_ref(x, context, Wq, Wkv, null_kv, Wout, ln_scale, ln_bias):
        import jax, jax.numpy as jnp
        import numpy as np
        B, N, DIM = (8, 512, 128)
        M, CTX = (32, 256)
        HEADS, DH = (16, 64)
        INNER = HEADS * DH
        EPS = 1e-06

        def _split_heads(t):
            b, n, _ = t.shape
            return t.reshape(b, n, HEADS, DH).transpose(0, 2, 1, 3)
        scale = DH ** (-0.5)
        b = x.shape[0]
        q = _split_heads(jnp.einsum('bnd,df->bnf', x, Wq))
        kv = jnp.einsum('bmc,cf->bmf', context, Wkv)
        k, v = jnp.split(kv, 2, axis=-1)
        k, v = (_split_heads(k), _split_heads(v))
        nk = jnp.broadcast_to(null_kv[0], (b, HEADS, 1, DH))
        nv = jnp.broadcast_to(null_kv[1], (b, HEADS, 1, DH))
        k = jnp.concatenate((nk, k), axis=-2)
        v = jnp.concatenate((nv, v), axis=-2)
        q = q * scale
        sim = jnp.einsum('bhid,bhjd->bhij', q, k)
        attn = jax.nn.softmax(sim, axis=-1)
        out = jnp.einsum('bhij,bhjd->bhid', attn, v)
        out = out.transpose(0, 2, 1, 3).reshape(b, -1, INNER)
        out = jnp.einsum('bnf,fd->bnd', out, Wout)
        mu = jnp.mean(out, axis=-1, keepdims=True)
        var = jnp.var(out, axis=-1, keepdims=True)
        out = (out - mu) * jax.lax.rsqrt(var + EPS) * ln_scale + ln_bias
        return out

    def _L2_attn_ref(x, Wq, bq, Wk, bk, Wv, bv, temperature):
        import jax, jax.numpy as jnp
        import numpy as np
        B, T, D, H = (4, 128, 128, 16)
        b, t, d = x.shape
        h = temperature.shape[0]
        dh = d // h
        q = (x @ Wq + bq).reshape(b, h, dh, t)
        k = (x @ Wk + bk).reshape(b, h, dh, t)
        v = (x @ Wv + bv).reshape(b, h, dh, t)
        attn = jnp.einsum('bhdt,bhds->bhts', k, v) * temperature
        attn = jax.nn.softmax(attn, axis=-1)
        out = jnp.einsum('bhdt,bhts->bhds', q, attn)
        return out.reshape(b, t, d)

    def _L2_ffn_ref(x, w1, b1, w2, b2):
        import jax, jax.numpy as jnp
        import numpy as np
        QP = 127.0
        MIN_RANGE = 1e-06

        def _ste_round(x):
            return x + jax.lax.stop_gradient(jnp.round(x) - x)

        def _quant_per_tensor(x):
            scale = jnp.maximum(jnp.max(jnp.abs(x)), MIN_RANGE) / QP
            return (_ste_round(x / scale), scale)

        def _qlinear(x2d, w, b):
            xq, sx = _quant_per_tensor(x2d)
            wq, sw = _quant_per_tensor(w)
            out = jnp.matmul(xq, wq.T) + b[None, :]
            return out * (sw * sx)
        B, N, D = x.shape
        h = _qlinear(x.reshape(-1, D), w1, b1)
        h = jax.nn.gelu(h, approximate=False)
        o = _qlinear(h, w2, b2)
        return o.reshape(B, N, -1)

    def _L3_xattn_ref(embeds, patch_embeds, patch_lens, W_in, b_in, g_res, g_init):
        import jax, jax.numpy as jnp
        import numpy as np
        B, L, P = (4, 512, 128)
        D_MODEL = 128
        D_GLOBAL = 256
        HEADDIM = 32
        EPSILON = 0.001
        RMS_EPS = 1e-05

        def rmsnorm(x, g, eps=RMS_EPS):
            var = jnp.mean(jnp.square(x), axis=-1, keepdims=True)
            return x * jax.lax.rsqrt(var + eps) * g

        def _hnet_depool(h, h_patch_full, patch_lens):
            h_patch = h_patch_full[..., :D_MODEL]
            bsz, plen = (h_patch.shape[0], h_patch.shape[1])
            seqlen = h.shape[1]
            logp = jnp.full((bsz, plen), -EPSILON, dtype=jnp.float32)
            bidx = jnp.cumsum(patch_lens, axis=1) - 1
            boundary_mask = jnp.zeros((bsz, seqlen), dtype=jnp.int32)
            boundary_mask = boundary_mask.at[jnp.arange(bsz)[:, None], bidx].set(1)
            dt = (-jnp.log(-jnp.expm1(logp))).astype(h_patch.dtype)
            x = h_patch / dt[..., None]
            n_heads = D_MODEL // HEADDIM
            A = -jnp.ones((n_heads,), dtype=jnp.float32)
            bcoef = jnp.exp(logp).astype(h_patch.dtype)
            x4 = x.reshape(bsz, plen, n_heads, HEADDIM)
            a = jnp.exp(dt[:, :, None] * A[None, None, :])
            u = (dt * bcoef)[:, :, None, None] * x4
            a_b = jnp.broadcast_to(a[..., None], u.shape)

            def comb(lft, rgt):
                aL, uL = lft
                aR, uR = rgt
                return (aL * aR, uL * aR + uR)
            _, s = jax.lax.associative_scan(comb, (a_b, u), axis=1)
            depool = s.reshape(bsz, plen, D_MODEL)
            plug = jnp.clip(jnp.cumsum(boundary_mask, axis=1) - 1, 0, plen - 1)
            depool_out = depool[jnp.arange(bsz)[:, None], plug]
            return depool_out + h
        h = rmsnorm(embeds, g_res)
        h = jnp.einsum('bld,ed->ble', h, W_in) + b_in
        h_patch = rmsnorm(patch_embeds, g_init)
        return _hnet_depool(h, h_patch, patch_lens)

    def _L3_attn_ref(x_t, Wf, Wi, Wh):
        import jax, jax.numpy as jnp
        import numpy as np
        EPS = 1e-08
        GROUPS = 128

        def log_g(x):
            return jnp.where(x >= 0, jnp.log(jax.nn.relu(x) + 0.5 + EPS), -jax.nn.softplus(-x) + EPS)

        def grouped_linear(x, W):
            B, S, D = x.shape
            G = W.shape[0]
            xg = x.reshape(B, S, G, D // G)
            y = jnp.einsum('bsgi,goi->bsgo', xg, W)
            return y.reshape(B, S, -1)

        def parallel_scan_log(log_coeffs, log_values):
            a_star = jnp.cumsum(log_coeffs + EPS, axis=1)
            log_h0_plus_b_star = jax.lax.cumlogsumexp(log_values - a_star, axis=1)
            return jnp.exp(a_star + log_h0_plus_b_star)
        f_gate = grouped_linear(x_t, Wf)
        i_gate = grouped_linear(x_t, Wi)
        hidden = grouped_linear(x_t, Wh)
        diff = jax.nn.softplus(-f_gate) - jax.nn.softplus(-i_gate)
        log_f = -jax.nn.softplus(diff)
        log_i = -jax.nn.softplus(-diff)
        log_values = log_i + log_g(hidden)
        h_t = parallel_scan_log(log_f, log_values)
        return h_t

    def _L3_ffn_ref(hidden_states, W_lin, b_lin, gate_w, left, right):
        import jax, jax.numpy as jnp
        import numpy as np
        B, S, D, O, E, R = (8, 256, 128, 128, 8, 4)
        TOP_K = 2
        SCALING = 4.0 / 4.0
        bsz, seq, d_in = hidden_states.shape
        x = hidden_states.reshape(-1, d_in)
        logits = x @ gate_w.T
        scores = jax.nn.softmax(logits, axis=-1)
        weights, idx = jax.lax.top_k(scores, TOP_K)
        base = x @ W_lin.T + b_lin
        left_sel = left[idx]
        right_sel = right[idx]
        t = jnp.einsum('nd,nkdr->nkr', x, left_sel)
        out_k = jnp.einsum('nkr,nkro->nko', t, right_sel)
        lora = jnp.sum(weights[..., None] * out_k, axis=1) * SCALING
        return (base + lora).reshape(bsz, seq, -1)
    x = x + _L0_xattn_ref(_layernorm(x, axis=-1), ctx_2048, mask_BxS2_if0, L0_xattn_W_in, L0_xattn_b_in, L0_xattn_g_res, L0_xattn_g_init)
    x = x + _L0_attn_ref(_layernorm(x, axis=-1), L0_attn_Wq, L0_attn_Wk, L0_attn_Wv, L0_attn_Wo)
    x = x + _L0_ffn_ref(_layernorm(x, axis=-1), L0_ffn_w_q, L0_ffn_bn_gamma, L0_ffn_bn_beta, L0_ffn_keys, L0_ffn_down_embed, L0_ffn_up_embed)
    x = x + _L1_xattn_ref(_layernorm(x, axis=-1), ctx_2048, L1_xattn_w_qkv, L1_xattn_w_proj, L1_xattn_b_proj)
    x = x + _L1_attn_ref(_layernorm(x, axis=-1), L1_attn_W_in, L1_attn_conv_w, L1_attn_W_x, L1_attn_W_dt, L1_attn_b_dt, L1_attn_W_Bp, L1_attn_D_param, L1_attn_W_out)
    x = x + _L1_ffn_ref(_layernorm(x, axis=-1), L1_ffn_W_fc, L1_ffn_ln_w, L1_ffn_ln_b, L1_ffn_W_proj)
    x = x + _L2_xattn_ref(_layernorm(x, axis=-1), ctx_2048, L2_xattn_Wq, L2_xattn_Wkv, L2_xattn_null_kv, L2_xattn_Wout, L2_xattn_ln_scale, L2_xattn_ln_bias)
    x = x + _L2_attn_ref(_layernorm(x, axis=-1), L2_attn_Wq, L2_attn_bq, L2_attn_Wk, L2_attn_bk, L2_attn_Wv, L2_attn_bv, L2_attn_temperature)
    x = x + _L2_ffn_ref(_layernorm(x, axis=-1), L2_ffn_w1, L2_ffn_b1, L2_ffn_w2, L2_ffn_b2)
    x = x + _L3_xattn_ref(_layernorm(x, axis=-1), ctx_2048, mask_BxS2_if0, L3_xattn_W_in, L3_xattn_b_in, L3_xattn_g_res, L3_xattn_g_init)
    x = x + _L3_attn_ref(_layernorm(x, axis=-1), L3_attn_Wf, L3_attn_Wi, L3_attn_Wh)
    x = x + _L3_ffn_ref(_layernorm(x, axis=-1), L3_ffn_W_lin, L3_ffn_b_lin, L3_ffn_gate_w, L3_ffn_left, L3_ffn_right)
    return x

_drawn_inputs = setup_inputs


def setup_inputs(seed=0):
    import zlib

    import numpy as np

    out = dict(_drawn_inputs(seed))
    spreads = {'L0_xattn_b_in': (0.0, 0.1),
     'L0_xattn_g_res': (1.0, 0.2),
     'L0_xattn_g_init': (1.0, 0.2),
     'L0_ffn_bn_gamma': (1.0, 0.6),
     'L0_ffn_bn_beta': (0.0, 0.8),
     'L1_attn_D_param': (1.0, 0.2),
     'L1_ffn_ln_w': (1.0, 0.2),
     'L1_ffn_ln_b': (0.0, 0.1),
     'L2_xattn_ln_scale': (1.0, 0.6),
     'L2_xattn_ln_bias': (0.0, 0.8),
     'L2_attn_temperature': (1.0, 0.6),
     'L3_xattn_b_in': (0.0, 0.8),
     'L3_xattn_g_res': (1.0, 0.6),
     'L3_xattn_g_init': (1.0, 0.6),
     'L3_ffn_b_lin': (0.0, 0.8)}
    factors = {'L0_attn_Wq': 8.0,
     'L0_attn_Wk': 8.0,
     'L0_attn_Wv': 2.766,
     'L0_attn_Wo': 2.746,
     'L0_ffn_w_q': 8.0,
     'L0_ffn_keys': 8.0,
     'L0_ffn_down_embed': 8.0,
     'L0_ffn_up_embed': 8.0,
     'L1_xattn_w_qkv': 7.898,
     'L1_xattn_b_proj': 3.452,
     'L1_attn_W_dt': 4.184,
     'L1_attn_b_dt': 8.0,
     'L2_xattn_Wq': 2.775,
     'L2_xattn_null_kv': 8.0,
     'L2_attn_Wq': 8.0,
     'L2_attn_bq': 58.341,
     'L2_attn_Wk': 8.0,
     'L2_attn_bk': 8.0,
     'L2_attn_Wv': 8.0,
     'L2_attn_bv': 21.334,
     'L2_ffn_w1': 8.0,
     'L2_ffn_b1': 64.0,
     'L2_ffn_w2': 8.0,
     'L2_ffn_b2': 64.0,
     'L3_xattn_W_in': 4.902,
     'L3_attn_Wf': 8.0,
     'L3_attn_Wi': 8.0,
     'L3_attn_Wh': 4.168,
     'L3_ffn_W_lin': 4.955,
     'L3_ffn_gate_w': 29.852,
     'L3_ffn_left': 27.087,
     'L3_ffn_right': 27.135}
    for name, (base, spread) in spreads.items():
        noise = np.random.default_rng([zlib.crc32(name.encode()), seed]).standard_normal(out[name].shape)
        drawn = base * np.exp(spread * noise) if base else spread * noise
        out[name] = jnp.asarray(drawn.astype(out[name].dtype))
    for name, factor in factors.items():
        out[name] = (out[name] * factor).astype(out[name].dtype)
    return out
```

```python
from contextlib import ExitStack

import concourse.bass as bass
import numpy as np
from concourse import mybir

F32 = mybir.dt.float32
BF16 = mybir.dt.bfloat16
I32 = mybir.dt.int32
U32 = mybir.dt.uint32
ALU = mybir.AluOpType
ACT = mybir.ActivationFunctionType
X = mybir.AxisListType.X
XY = mybir.AxisListType.XY
ds = bass.ds

B, SEQ, D = 128, 32, 128
CTX, CD = 257, 256
P = 128
BT = P // SEQ
TILES = B * SEQ // P
HEADS = 16
G = 4
LN_EPS = 1e-5

CONST_WIDTHS = dict(ident=P, group=G, head4=G, head=HEADS, sel=SEQ, band=SEQ, rope=4 * SEQ, decay=P, iota8=8)
CONST_AT = {}
for _name, _w in CONST_WIDTHS.items():
    CONST_AT[_name] = sum(CONST_WIDTHS[k] for k in list(CONST_WIDTHS)[:len(CONST_AT)])
N_CONST = sum(CONST_WIDTHS.values())


def constants():
    p = np.arange(P)
    c = {}
    c["ident"] = np.eye(P)
    c["group"] = (p[:, None] // 32 == np.arange(G))
    c["head4"] = (p[:, None] // 8 % 4 == np.arange(G))
    c["head"] = (p[:, None] // 8 == np.arange(HEADS))
    c["sel"] = (p[:, None] % SEQ == np.arange(SEQ))
    c["band"] = np.where(abs(p[:, None] % SEQ - np.arange(SEQ)) <= 16, 0.0, -1e30)
    hd = 8
    inv = (np.float32(1.0) / np.float32(10000.0) ** (np.arange(0, hd, 2, dtype=np.float32) / np.float32(hd)))
    ang = np.arange(SEQ, dtype=np.float32)[None, :] * inv[(p % hd) // 2][:, None]
    cos, sin = np.cos(ang), np.sin(ang) * np.where(p % 2 == 0, -1.0, 1.0)[:, None]
    scale = 1.0 / np.sqrt(hd)
    c["rope"] = np.concatenate([cos * scale, sin * scale, cos, sin], axis=1)
    logp = np.float32(-0.001)
    dt = -np.log(-np.expm1(logp))
    k, j = p[:, None], p[None, :]
    lag = np.where((k >= j) & (k // SEQ == j // SEQ), k - j, 0)
    c["decay"] = np.where((k >= j) & (k // SEQ == j // SEQ), np.exp(np.float64(logp)) * np.exp(-np.float64(dt) * lag), 0.0)
    c["iota8"] = np.broadcast_to(np.arange(8), (P, 8))
    return np.concatenate([c[n].astype(np.float32) for n in CONST_WIDTHS], axis=1)


class Core:

    def __init__(self, nc, dram, ctx):
        self.nc, self.dram, self.sems = nc, dram, []
        self.x = ctx.enter_context(nc.sbuf_tensor("x_sb", [P, TILES, D], F32))
        self.ctx_n = ctx.enter_context(nc.sbuf_tensor("ctx_n", [P, TILES, D], F32))
        self.depool = ctx.enter_context(nc.sbuf_tensor("depool", [P, TILES, P], F32))
        self.const = ctx.enter_context(nc.sbuf_tensor("const", [P, N_CONST], F32))
        self.ones = ctx.enter_context(nc.sbuf_tensor("ones", [P, P], F32))
        self.eps = ctx.enter_context(nc.sbuf_tensor("eps", [P, 1], F32))
        self.half = ctx.enter_context(nc.sbuf_tensor("minus_half", [P, 1], F32))
        self.psum = ctx.enter_context(nc.psum_tensor("psum", [P, 8, 512], F32))

    def c(self, name):
        return self.const[:, CONST_AT[name]:CONST_AT[name] + CONST_WIDTHS[name]]

    def sem(self, name):
        handle = self.nc.alloc_semaphore(name=name)
        self.sems.append(handle)
        return handle

    def clear_sems(self):
        self.nc.clear_and_free_semaphores(self.sems)
        self.nc.all_engine_barrier()
        self.sems = []


class Front:

    def __init__(self, core, stage, name, S, bank, transposed=True, rms=False, pack=1):
        nc = core.nc
        self.core, self.nc, self.S, self.bank, self.rms, self.pack = core, nc, S, bank, rms, pack
        sb = lambda n, w: stage.enter_context(nc.sbuf_tensor(f"{name}_front_{n}_sb", [P, S, w], F32))
        self.stats, self.mv, self.var, self.rstd = sb("stats", 6), sb("mv", 2), sb("var", 2), sb("rstd", 1)
        self.xn = sb("xn", D)
        if transposed:
            self.xnT = sb("xnT", P)
        self.moments, self.rstd_done, self.normed, self.turned, self.xnT_done = (
            core.sem(f"{name}_front_{n}") for n in ("moments", "rstd_done", "normed", "turned", "xnT_done"))

    def dve_moments(self, dve, n):
        dve.drain()
        for s in range(self.S):
            self.nc.vector.bn_stats(self.stats[:, s, :], self.core.x[:, ds(n + s, 1), :])
        dve.drain()
        for s in range(self.S):
            self.nc.vector.bn_aggr(self.mv[:, s, :], self.stats[:, s, :]).then_inc(self.moments, 1)

    def pool_rstd(self, pool, n):
        S, mv = self.S, self.mv[:, :, 1:2]
        column = lambda k: self.var[:, :, k:k + 1]
        eps = self.core.eps[:, :].rearrange("p (s a) -> p s a", a=1).to_broadcast([P, S, 1])
        half = self.core.half[:, :].rearrange("p (s a) -> p s a", a=1).to_broadcast([P, S, 1])
        pool.wait_ge(self.moments, n + S)
        self.nc.gpsimd.tensor_tensor(column(0), mv, eps, ALU.add)
        if self.rms:
            pool.drain()
            self.nc.gpsimd.tensor_tensor(column(1), column(0), eps, ALU.mult)
            pool.drain()
            self.nc.gpsimd.tensor_tensor(column(0), column(1), mv, ALU.add)
        pool.drain()
        self.nc.gpsimd.tensor_tensor(self.rstd[:, :, :], column(0), half, ALU.pow).then_inc(self.rstd_done, S)

    def dve_normalise(self, dve, n):
        for s in range(self.S):
            dve.wait_ge(self.rstd_done, n + s + 1)
            self.nc.vector.tensor_scalar(self.xn[:, s, :], self.core.x[:, ds(n + s, 1), :], self.mv[:, s, 0:1],
                                         self.rstd[:, s, :], ALU.subtract, ALU.mult).then_inc(self.normed, 1)

    def pe_transpose(self, pe, n):
        for s in range(self.S):
            pe.wait_ge(self.normed, n + s + 1)
            self.nc.tensor.transpose(self.bank(s)[:, 0:P], self.xn[:, s, :],
                                     self.core.c("ident")).then_inc(self.turned, 1)

    def act_copy(self, act, n):
        for s in range(0, self.S, self.pack):
            act.wait_ge(self.turned, n + s + self.pack)
            src = self.core.psum[:, s // self.pack, 0:self.pack * P] if self.pack > 1 else self.bank(s)[:, 0:P]
            self.nc.scalar.copy(self.xnT[:, s:s + self.pack, :],
                                src.rearrange("p (s w) -> p s w", w=P)).then_inc(self.xnT_done, self.pack)


def load(eng, items, sem):
    for dst, src in items:
        eng.dma_start(dst, src).then_inc(sem, 16)
    return 16 * len(items)


def add_to_x(core, t, update):
    return core.nc.vector.tensor_tensor(core.x[:, ds(t, 1), :], core.x[:, ds(t, 1), :], update, ALU.add)


def start(core):
    nc, dram = core.nc, core.dram
    LOADS = 4
    with ExitStack() as st:
        sb = lambda n, shape, dt=F32: st.enter_context(nc.sbuf_tensor(f"start_{n}", shape, dt))
        lens_i = sb("lens_i", [B, CTX], I32)
        lens = sb("lens", [B, CTX])
        ends = sb("ends", [B, CTX])
        wrap = sb("wrap", [B, CTX])
        hit = sb("hit", [B, SEQ, CTX])
        steps = sb("steps", [B, SEQ])
        bound = sb("bound", [B, SEQ])
        plug = sb("plug", [B, SEQ])
        plug_all = sb("plug_all", [P, TILES * P])
        pick = sb("pick", [P, TILES, BT, SEQ])
        rowpos = sb("rowpos", [P, 1])
        raw = sb("raw", [P, TILES, CD])
        sq = sb("sq", [P, 2, TILES // LOADS, CD])
        ms = sb("ms", [P, 3, TILES])
        halves = sb("halves", [P, TILES])
        const_in, x_in, lens_in, plug_out, plug_in = (
            core.sem(n) for n in ("const_in", "x_in", "lens_in", "plug_out", "plug_in"))
        plug_done, pos_done, pick_done, scanned, mat_done = (
            core.sem(n) for n in ("plug_done", "pos_done", "pick_done", "scanned", "mat_done"))
        ctx_in = [core.sem(f"ctx_in{q}") for q in range(LOADS)]
        squared, summed_part, summed, rs_done = (core.sem(n) for n in (
            "ctx_squared", "ctx_summed_part", "ctx_summed", "ctx_rs"))
        scratch = nc.dram_tensor("plug_scratch", (B, SEQ), F32).ap()
        block = st.enter_context(nc.Block())

        @block.sync
        def _(sp):
            sp.dma_start(lens_i[:, :], dram["mask_BxS2_if0"]).then_inc(lens_in, 16)
            sp.dma_start(core.const[:, :], dram["constants"]).then_inc(const_in, 16)
            sp.dma_start(core.x[:, :, :], dram["x"].rearrange("(t p) d -> p t d", p=P)).then_inc(x_in, 16)
            sp.wait_ge(plug_done, 1)
            sp.dma_start(scratch, plug[:, :]).then_inc(plug_out, 16)
            sp.wait_ge(plug_out, 16)
            flat = scratch.rearrange("b s -> (b s)").rearrange("(a n) -> a n", a=1)
            sp.dma_start(plug_all[:, :], flat.to_broadcast([P, B * SEQ])).then_inc(plug_in, 16)

        @block.gpsimd
        def _(pool):
            pool.wait_ge(const_in, 16)
            nc.gpsimd.memset(core.ones[:, :], 1.0)
            nc.gpsimd.memset(core.half[:, :], -0.5)
            nc.gpsimd.memset(core.eps[:, :], LN_EPS)
            nc.gpsimd.memset(halves[:, :], -0.5)
            pool.drain()
            nc.gpsimd.iota(rowpos[:, :], [[0, 1]], base=0, channel_multiplier=1,
                           allow_small_or_imprecise_dtypes=True).then_inc(pos_done, 1)
            pool.wait_ge(summed, 1)
            nc.gpsimd.tensor_tensor(ms[:, 2, :], ms[:, 1, :], halves[:, :], ALU.pow).then_inc(rs_done, 1)

        @block.scalar
        def _(act):
            part = TILES // LOADS
            for q in range(LOADS):
                for b in range(BT):
                    first = q * part * BT + b
                    act.dma_start(raw[b * SEQ:(b + 1) * SEQ, q * part:(q + 1) * part, :],
                                  dram["ctx_2048"][first:(q + 1) * part * BT:BT, 0:SEQ, :].rearrange(
                                      "t k c -> k t c")).then_inc(ctx_in[q], 16)
            for q in range(LOADS):
                act.wait_ge(ctx_in[q], 16 * BT)
                if q >= 2:
                    act.wait_ge(summed_part, q - 1)
                nc.scalar.activation(sq[:, q % 2, :, :], raw[:, q * part:(q + 1) * part, :],
                                     ACT.Square).then_inc(squared, 1)

        @block.vector
        def _(dve):
            def then_wait(ins):
                dve.drain()

            dve.wait_ge(lens_in, 16)
            then_wait(nc.vector.tensor_copy(lens[:, :], lens_i[:, :]))
            then_wait(nc.vector.memset(wrap[:, :], 1.0))
            then_wait(nc.vector.tensor_tensor_scan(ends[:, :], wrap[:, :], lens[:, :], -1.0, ALU.mult, ALU.add))
            then_wait(nc.vector.tensor_scalar(wrap[:, :], ends[:, :], 0.0, float(SEQ), ALU.is_lt, ALU.mult))
            then_wait(nc.vector.tensor_tensor(ends[:, :], ends[:, :], wrap[:, :], ALU.add))
            for t in range(SEQ):
                ins = nc.vector.tensor_scalar(hit[:, t, :], ends[:, :], float(t), None, ALU.is_equal)
            then_wait(ins)
            then_wait(nc.vector.tensor_reduce(bound[:, :], hit[:, :, :], X, ALU.max))
            then_wait(nc.vector.memset(steps[:, :], 1.0))
            then_wait(nc.vector.tensor_tensor_scan(plug[:, :], steps[:, :], bound[:, :], -1.0, ALU.mult, ALU.add))
            nc.vector.tensor_scalar(plug[:, :], plug[:, :], 0.0, float(CTX - 1), ALU.max,
                                    ALU.min).then_inc(plug_done, 1)
            dve.wait_ge(pos_done, 1)
            for g in range(1, G):
                then_wait(nc.vector.scalar_tensor_tensor(rowpos[:, :], core.c("group")[:, g:g + 1], -32.0 * g,
                                                         rowpos[:, :], ALU.mult, ALU.add))
            dve.wait_ge(plug_in, 16)
            then_wait(nc.vector.tensor_scalar(plug_all[:, :], plug_all[:, :], rowpos[:, :], None, ALU.is_equal))
            nc.vector.tensor_tensor(
                pick[:, :, :, :], plug_all[:, :].rearrange("p (t b s) -> p t b s", t=TILES, b=BT),
                core.c("group").rearrange("p (a b c) -> p a b c", a=1, c=1).to_broadcast([P, TILES, BT, SEQ]),
                ALU.mult).then_inc(pick_done, 1)
            part = TILES // LOADS
            for q in range(LOADS):
                dve.wait_ge(squared, q + 1)
                nc.vector.tensor_reduce(ms[:, 0, q * part:(q + 1) * part], sq[:, q % 2, :, :], X,
                                        ALU.add).then_inc(summed_part, 1)
            dve.drain()
            nc.vector.tensor_scalar(ms[:, 1, :], ms[:, 0, :], 1.0 / CD, LN_EPS, ALU.mult, ALU.add).then_inc(summed, 1)
            for q in range(TILES * P // 512):
                dve.wait_ge(scanned, q + 1)
                nc.vector.tensor_copy(core.depool[:, q * 4:q * 4 + 4, :],
                                      core.psum[:, q, :].rearrange("p (t s) -> p t s", s=P)).then_inc(mat_done, 1)
            dve.wait_ge(rs_done, 1)
            nc.vector.tensor_tensor(core.ctx_n[:, :, :], raw[:, :, 0:D],
                                    ms[:, 2, :].rearrange("p (t c) -> p t c", c=1).to_broadcast([P, TILES, D]), ALU.mult)
            dve.wait_ge(x_in, 16)

        @block.tensor
        def _(pe):
            pe.wait_ge(pick_done, 1)
            pe.wait_ge(const_in, 16)
            for q in range(TILES * P // 512):
                nc.tensor.matmul(core.psum[:, q, :], core.c("decay"),
                                 pick[:, :, :, :].rearrange("p t b s -> p (t b s)")[:, q * 512:q * 512 + 512],
                                 start=True, stop=True).then_inc(scanned, 1)


def depool_cross(core, name):
    nc, dram = core.nc, core.dram
    S, PACK = 8, 4
    with ExitStack() as st:
        sb = lambda n, shape, dt=F32: st.enter_context(nc.sbuf_tensor(f"{name}_{n}", shape, dt))
        w = sb("w", [D, D])
        g_res = sb("g_res", [D, 1])
        b_in = sb("b_in", [1, D])
        g_init = sb("g_init", [P, D])
        mat = sb("mat", [P, S, P])
        patch = sb("patch", [P, S, D])
        front = Front(core, st, name, S, lambda s: core.psum[:, s // PACK, s % PACK * P:s % PACK * P + P], rms=True,
                      pack=PACK)
        out = lambda u: core.psum[:, 2 + u, :].rearrange("p (s d) -> p s d", d=D)
        w_in, w_done, copied, patch_done, out_done, added = (core.sem(f"{name}_{n}") for n in (
            "w_in", "w_done", "copied", "patch_done", "out_done", "added"))
        block = st.enter_context(nc.Block())
        U = S // PACK

        @block.sync
        def _(sp):
            load(sp, [(w[:, :], dram[f"{name}_W_in_T"]), (g_res[:, :], dram[f"{name}_g_res"]),
                      (b_in[:, :], dram[f"{name}_b_in"]),
                      (g_init[:, :], dram[f"{name}_g_init"][:, 0:D].to_broadcast([P, D]))], w_in)

        @block.gpsimd
        def _(pool):
            pool.wait_ge(w_in, 64)
            g4 = g_init[:, :].rearrange("p (s d) -> p s d", s=1).to_broadcast([P, PACK, D])
            with pool.Fori(0, TILES // S) as it:
                front.pool_rstd(pool, it * S)
                for u in range(U):
                    pool.wait_ge(out_done, it * U + u + 1)
                    nc.gpsimd.tensor_tensor(patch[:, 4 * u:4 * u + 4, :], core.ctx_n[:, ds(it * S + 4 * u, PACK), :], g4,
                                            ALU.mult).then_inc(patch_done, 1)

        @block.scalar
        def _(act):
            with act.Fori(0, TILES // S) as it:
                for u in range(U):
                    act.wait_ge(out_done, it * U + u + 1)
                    nc.scalar.copy(mat[:, 4 * u:4 * u + 4, :], core.depool[:, ds(it * S + 4 * u, PACK), :]).then_inc(copied, 1)
                front.act_copy(act, it * S)

        @block.vector
        def _(dve):
            dve.wait_ge(w_in, 64)
            nc.vector.tensor_scalar(w[:, :], w[:, :], g_res[:, :], None, ALU.mult).then_inc(w_done, 1)
            with dve.Fori(0, TILES // S) as it:
                front.dve_moments(dve, it * S)
                front.dve_normalise(dve, it * S)
                for u in range(U):
                    dve.wait_ge(out_done, (it + 1) * U + u + 1)
                    x = core.x[:, ds(it * S + 4 * u, PACK), :]
                    nc.vector.tensor_tensor(x, x, out(u), ALU.add).then_inc(added, 1)

        @block.tensor
        def _(pe):
            pe.sem_inc(out_done, U)
            pe.sem_inc(added, U)
            pe.wait_ge(w_done, 1)
            with pe.Fori(0, TILES // S) as it:
                front.pe_transpose(pe, it * S)
                for u in range(U):
                    pe.wait_ge(added, it * U + u + 1)
                    pe.wait_ge(copied, it * U + u + 1)
                    pe.wait_ge(patch_done, it * U + u + 1)
                    pe.wait_ge(front.xnT_done, it * S + 4 * u + 4)
                    for s in range(4 * u, 4 * u + 4):
                        nc.tensor.matmul(out(u)[:, s % 4, :], mat[:, s, :], patch[:, s, :], start=True, stop=False)
                        nc.tensor.matmul(out(u)[:, s % 4, :], core.ones[0:1, :], b_in[:, :], start=False, stop=False)
                        last = nc.tensor.matmul(out(u)[:, s % 4, :], front.xnT[:, s, :], w[:, :], start=False, stop=True)
                    last.then_inc(out_done, 1)


def spread(t, block, width):
    return (t.rearrange("p b (a w) -> p b a w", a=1).to_broadcast([P, BT, G, width]),
            block.rearrange("p (b j w) -> p b j w", b=1, w=1).to_broadcast([P, BT, G, width]))


def per_row(t):
    return t.rearrange("p (r w) -> p r w", w=1).to_broadcast([P, t.shape[1], SEQ])


def rotary_attention(core, name):
    nc, dram = core.nc, core.dram
    S = 4
    with ExitStack() as st:
        sb = lambda n, shape, dt=F32: st.enter_context(nc.sbuf_tensor(f"{name}_{n}", shape, dt))
        w_qk = sb("w_qk", [D, 4, D])
        w_v = sb("w_v", [D, G * 8])
        w_o = sb("w_o", [D, D])
        prod = sb("prod", [P, S, 4, P])
        qk = sb("qk", [P, S, 2, P])
        q4 = sb("q4", [P, S, BT, G, SEQ])
        kbd = sb("kbd", [P, S, BT, G, SEQ])
        vbd = sb("vbd", [P, S, BT, G, 8])
        prob = sb("prob", [P, S, HEADS, SEQ])
        top = sb("top", [P, S, HEADS])
        total = sb("total", [P, S, HEADS])
        probT = sb("probT", [P, S, BT, P])
        heads = sb("heads", [P, S, BT, G, G * 8])
        attnT = sb("attnT", [P, S, P])
        xnT4 = sb("xnT4", [P, S, BT, G, SEQ])
        bank_a = lambda s: core.psum[:, 2 * s, :]
        bank_b = lambda s: core.psum[:, 2 * s + 1, :]
        by_group = lambda t: t.rearrange("p (b j w) -> p b j w", b=BT, j=G)
        front = Front(core, st, name, S, bank_a)
        (w_in, tile_done, projected, roped, masked, scored, shifted, exped, normal, turned, probT_done, mixed,
         split, joined, attnT_done, out_done, copied) = (core.sem(f"{name}_{n}") for n in (
             "w_in", "tile_done", "projected", "roped", "masked", "scored", "shifted", "exped", "normal", "turned",
             "probT_done", "mixed", "split", "joined", "attnT_done", "out_done", "copied"))
        block = st.enter_context(nc.Block())

        @block.sync
        def _(sp):
            load(sp, [(w_qk[:, :, :], dram[f"{name}_Wqk"]), (w_v[:, :], dram[f"{name}_Wv"]),
                      (w_o[:, :], dram[f"{name}_Wo"])], w_in)

        @block.gpsimd
        def _(pool):
            with pool.Fori(0, TILES // S) as it:
                n = it * S
                front.pool_rstd(pool, n)
                for s in range(S):
                    pool.wait_ge(roped, n + s + 1)
                    a, m = spread(qk[:, s, 0, :].rearrange("p (b w) -> p b w", b=BT), core.c("head4"), SEQ)
                    nc.gpsimd.tensor_tensor(q4[:, s, :, :, :], a, m, ALU.mult)
                    a, m = spread(qk[:, s, 1, :].rearrange("p (b w) -> p b w", b=BT), core.c("group"), SEQ)
                    nc.gpsimd.tensor_tensor(kbd[:, s, :, :, :], a, m, ALU.mult).then_inc(masked, 1)

        @block.scalar
        def _(act):
            with act.Fori(0, TILES // S) as it:
                n = it * S
                front.act_copy(act, n)
                for s in range(S):
                    act.drain() if s == 0 else None
                    cols = front.xnT[:, s, :].rearrange("p (b a w) -> p b a w", b=BT, a=1)
                    nc.scalar.copy(xnT4[:, s, :, :, :], cols.to_broadcast([P, BT, G, SEQ])).then_inc(copied, 1)
                for s in range(S):
                    act.wait_ge(shifted, n + s + 1)
                    nc.scalar.activation(prob[:, s, :, :], prob[:, s, :, :], ACT.Exp).then_inc(exped, 1)
                for s in range(S):
                    act.wait_ge(turned, n + s + 1)
                    nc.scalar.copy(probT[:, s, :, :], bank_a(s).rearrange("p (b w) -> p b w", b=BT)).then_inc(probT_done, 1)
                for s in range(S):
                    act.wait_ge(joined, n + s + 1)
                    nc.scalar.copy(attnT[:, s, :], bank_a(s)[:, 0:P]).then_inc(attnT_done, 1)

        @block.vector
        def _(dve):
            with dve.Fori(0, TILES // S) as it:
                n = it * S
                front.dve_moments(dve, n)
                front.dve_normalise(dve, n)
                rope = core.c("rope").rearrange("p (f a w) -> p f a w", f=4, a=1).to_broadcast([P, 4, BT, SEQ])
                for s in range(S):
                    dve.wait_ge(projected, n + s + 1)
                    nc.vector.tensor_tensor(prod[:, s, :, :].rearrange("p f (b w) -> p f b w", b=BT),
                                            bank_b(s).rearrange("p (f b w) -> p f b w", f=4, b=BT), rope, ALU.mult)
                dve.drain()
                for s in range(S):
                    v = prod[:, s, :, :].rearrange("p (a f) w -> p a f w", a=2)
                    nc.vector.tensor_tensor(qk[:, s, :, :], v[:, :, 0, :], v[:, :, 1, :], ALU.add).then_inc(roped, 1)
                m = core.c("group").rearrange("p (b j w) -> p b j w", b=1, w=1).to_broadcast([P, BT, G, 8])
                for s in range(S):
                    nc.vector.tensor_tensor(vbd[:, s, :, :, :],
                                            bank_a(s)[:, 0:P].rearrange("p (b j w) -> p b j w", b=BT, j=G), m,
                                            ALU.mult)
                band = core.c("band").rearrange("p (a w) -> p a w", a=1).to_broadcast([P, HEADS, SEQ])
                for s in range(S):
                    dve.wait_ge(scored, n + s + 1)
                    nc.vector.tensor_tensor(prob[:, s, :, :], bank_b(s).rearrange("p (a w) -> p a w", w=SEQ), band,
                                            ALU.add)
                dve.drain()
                for s in range(S):
                    nc.vector.tensor_reduce(top[:, s, :], prob[:, s, :, :], X, ALU.max)
                dve.drain()
                for s in range(S):
                    nc.vector.tensor_tensor(prob[:, s, :, :], prob[:, s, :, :], per_row(top[:, s, :]),
                                            ALU.subtract).then_inc(shifted, 1)
                for s in range(S):
                    dve.wait_ge(exped, n + s + 1)
                    nc.vector.tensor_reduce(total[:, s, :], prob[:, s, :, :], X, ALU.add)
                dve.drain()
                for s in range(S):
                    nc.vector.reciprocal(total[:, s, :], total[:, s, :])
                dve.drain()
                for s in range(S):
                    nc.vector.tensor_tensor(prob[:, s, :, :], prob[:, s, :, :], per_row(total[:, s, :]),
                                            ALU.mult).then_inc(normal, 1)
                for s in range(S):
                    dve.wait_ge(mixed, n + s + 1)
                    a, m = spread(bank_b(s)[:, 0:P].rearrange("p (b w) -> p b w", b=BT), core.c("group"), G * 8)
                    nc.vector.tensor_tensor(heads[:, s, :, :, :], a, m, ALU.mult).then_inc(split, 1)
                for s in range(S):
                    dve.wait_ge(out_done, n + s + 1)
                    add_to_x(core, n + s, bank_b(s)[:, 0:D]).then_inc(tile_done, 1)

        @block.tensor
        def _(pe):
            pe.wait_ge(w_in, 48)
            with pe.Fori(0, TILES // S) as it:
                n = it * S
                front.pe_transpose(pe, n)
                for s in range(S):
                    pe.wait_ge(front.xnT_done, n + s + 1)
                    for f in range(4):
                        nc.tensor.matmul(bank_b(s)[:, f * P:(f + 1) * P], w_qk[:, f, :], front.xnT[:, s, :],
                                         start=True, stop=True)
                    pe.wait_ge(copied, n + s + 1)
                    for b in range(BT):
                        last = nc.tensor.matmul(bank_a(s)[:, b * 32:(b + 1) * 32],
                                                xnT4[:, s, b, :, :].rearrange("p a w -> p (a w)"), w_v[:, :],
                                                start=True, stop=True)
                    last.then_inc(projected, 1)
                for s in range(S):
                    pe.wait_ge(masked, n + s + 1)
                    for b in range(BT):
                        last = nc.tensor.matmul(bank_b(s)[:, b * P:(b + 1) * P],
                                                q4[:, s, b, :, :].rearrange("p j w -> p (j w)"),
                                                kbd[:, s, b, :, :].rearrange("p j w -> p (j w)"), start=True, stop=True)
                    last.then_inc(scored, 1)
                for s in range(S):
                    pe.wait_ge(normal, n + s + 1)
                    for b in range(BT):
                        last = nc.tensor.transpose(bank_a(s)[:, b * P:(b + 1) * P],
                                                   prob[:, s, b * G:(b + 1) * G, :].rearrange("p g k -> p (g k)"),
                                                   core.c("ident"))
                    last.then_inc(turned, 1)
                for s in range(S):
                    pe.wait_ge(probT_done, n + s + 1)
                    for b in range(BT):
                        last = nc.tensor.matmul(bank_b(s)[:, b * 32:(b + 1) * 32], probT[:, s, b, :],
                                                vbd[:, s, b, :, :].rearrange("p j w -> p (j w)"), start=True, stop=True)
                    last.then_inc(mixed, 1)
                for s in range(S):
                    pe.wait_ge(split, n + s + 1)
                    for b in range(BT):
                        last = nc.tensor.matmul(bank_a(s)[:, b * 32:(b + 1) * 32],
                                                heads[:, s, b, :, :].rearrange("p j w -> p (j w)"), core.c("sel"),
                                                start=True, stop=True)
                    last.then_inc(joined, 1)
                for s in range(S):
                    pe.wait_ge(attnT_done, n + s + 1)
                    nc.tensor.matmul(bank_b(s)[:, 0:D], attnT[:, s, :], w_o[:, :], start=True,
                                     stop=True).then_inc(out_done, 1)


def product_key_experts(core, name):
    nc, dram = core.nc, core.dram
    H, K, TOP, KG = 8, 32, 8, 16
    E = K * K
    with ExitStack() as outer:
        keep = lambda n, shape, dt=F32: outer.enter_context(nc.sbuf_tensor(f"{name}_{n}", shape, dt))
        w_sim = keep("w_sim", [D, KG * K])
        b_sim = keep("b_sim", [P, KG * K])
        down = keep("down", [D, E])
        up = keep("up", [P, E // P, D])
        experts_in = core.sem(f"{name}_experts_in")
        query_keys(core, name, w_sim, b_sim, down, up, experts_in)

        S = 2
        sb = keep
        sims = sb("sims", [P, S, KG, K])
        top = sb("top", [P, S, KG, TOP])
        pairs = sb("pairs", [P, S, H, TOP * TOP])
        best = sb("best", [P, S, H, TOP])
        shift = sb("shift", [P, S, H, TOP])
        total = sb("total", [P, S, H])
        bias = sb("bias", [P, S, H])
        sums = sb("sums", [P, S, 2, K, K])
        prob = sb("prob", [P, S, 2, E])
        weight = sb("weight", [P, S, E])
        value = sb("value", [P, S, E])
        mixT = sb("mixT", [P, S, E // P, P])
        bank = lambda s, k: core.psum[:, 4 * s + k, :]
        pair = lambda s, k=2: core.psum[:, 4 * s + k:4 * s + k + 2, :].rearrange("p a w -> p (a w)")
        front = Front(core, outer, f"{name}2", S, lambda s: bank(s, 0))
        (simmed, valued, cut, exped, logged, biased, summed, probs, used, kept, weighted, mixed, turned, mixT_done,
         out_done) = (core.sem(f"{name}_{n}") for n in (
             "simmed", "valued", "cut", "exped", "logged", "biased", "summed", "probs", "used", "kept", "weighted", "mixed", "turned",
             "mixT_done", "out_done"))
        block = outer.enter_context(nc.Block())

        @block.gpsimd
        def _(pool):
            with pool.Fori(0, TILES // S) as it:
                n = it * S
                front.pool_rstd(pool, n)
                for h in range(H):
                    for s in range(S):
                        if h == 0:
                            pool.wait_ge(biased, n + s + 1)
                        pool.wait_ge(kept, n * H + h * S + s + 1)
                        sx = sims[:, s, h, :].rearrange("p (i j) -> p i j", j=1).to_broadcast([P, K, K])
                        sy = sims[:, s, H + h, :].rearrange("p (i j) -> p i j", i=1).to_broadcast([P, K, K])
                        nc.gpsimd.tensor_tensor(sums[:, s, h % 2, :, :], sx, sy, ALU.add).then_inc(summed, 1)

        @block.scalar
        def _(act):
            with act.Fori(0, TILES // S) as it:
                n = it * S
                front.act_copy(act, n)
                for s in range(S):
                    act.wait_ge(valued, n + s + 1)
                    nc.scalar.activation(value[:, s, :], pair(s), ACT.Gelu_apprx_tanh)
                for s in range(S):
                    act.wait_ge(cut, n + s + 1)
                    nc.scalar.activation(shift[:, s, :, :], shift[:, s, :, :], ACT.Exp).then_inc(exped, 1)
                for s in range(S):
                    act.wait_ge(logged, n + s + 1)
                    nc.scalar.activation(total[:, s, :], total[:, s, :], ACT.Ln).then_inc(biased, 1)
                for h in range(H):
                    for s in range(S):
                        if h == 0:
                            act.wait_ge(weighted, n + s + 1)
                        act.wait_ge(used, n * H + h * S + s + 1)
                        act.wait_ge(summed, n * H + h * S + s + 1)
                        nc.scalar.activation(prob[:, s, h % 2, :], sums[:, s, h % 2, :, :].rearrange("p i j -> p (i j)"),
                                             ACT.Exp, bias=bias[:, s, h:h + 1]).then_inc(probs, 1)
                for s in range(S):
                    act.wait_ge(turned, n + s + 1)
                    nc.scalar.copy(mixT[:, s, :, :], pair(s, 0).rearrange("p (c w) -> p c w", w=P)).then_inc(mixT_done, 1)

        @block.vector
        def _(dve):
            dve.sem_inc(used, 2 * S)
            dve.sem_inc(kept, 2 * S)
            with dve.Fori(0, TILES // S) as it:
                n = it * S
                front.dve_moments(dve, n)
                front.dve_normalise(dve, n)
                for s in range(S):
                    dve.wait_ge(simmed, n + s + 1)
                    nc.vector.tensor_tensor(sims[:, s, :, :].rearrange("p g k -> p (g k)"), bank(s, 1), b_sim[:, :],
                                            ALU.add)
                dve.drain()
                for s in range(S):
                    for g in range(KG):
                        nc.vector.max(top[:, s, g, :], sims[:, s, g, :])
                dve.drain()
                for s in range(S):
                    for h in range(H):
                        sx = top[:, s, h, :].rearrange("p (i j) -> p i j", j=1).to_broadcast([P, TOP, TOP])
                        sy = top[:, s, H + h, :].rearrange("p (i j) -> p i j", i=1).to_broadcast([P, TOP, TOP])
                        nc.vector.tensor_tensor(pairs[:, s, h, :].rearrange("p (i j) -> p i j", j=TOP), sx, sy, ALU.add)
                dve.drain()
                for s in range(S):
                    for h in range(H):
                        nc.vector.max(best[:, s, h, :], pairs[:, s, h, :])
                dve.drain()
                for s in range(S):
                    nc.vector.tensor_tensor(shift[:, s, :, :], best[:, s, :, :],
                                            best[:, s, :, 0:1].to_broadcast([P, H, TOP]), ALU.subtract).then_inc(cut, 1)
                for s in range(S):
                    dve.wait_ge(exped, n + s + 1)
                    nc.vector.tensor_reduce(total[:, s, :], shift[:, s, :, :], X, ALU.add).then_inc(logged, 1)
                for s in range(S):
                    dve.wait_ge(biased, n + s + 1)
                    nc.vector.scalar_tensor_tensor(bias[:, s, :], total[:, s, :], -1.0,
                                                   best[:, s, :, 0:1].rearrange("p h a -> p (h a)"), ALU.mult,
                                                   ALU.subtract).then_inc(weighted, 1)
                for h in range(H):
                    for s in range(S):
                        dve.wait_ge(probs, n * H + h * S + s + 1)
                        nc.vector.scalar_tensor_tensor(
                            prob[:, s, h % 2, :], sums[:, s, h % 2, :, :].rearrange("p i j -> p (i j)"),
                            best[:, s, h, TOP - 1:TOP], prob[:, s, h % 2, :], ALU.is_ge, ALU.mult).then_inc(kept, 1)
                for s in range(S):
                    dve.wait_ge(used, n * H + (H + 1) * S + s + 1)
                    nc.vector.tensor_tensor(weight[:, s, :], pair(s), value[:, s, :], ALU.mult).then_inc(mixed, 1)
                for s in range(S):
                    dve.wait_ge(out_done, n + s + 1)
                    add_to_x(core, n + s, bank(s, 2)[:, 0:D])

        @block.tensor
        def _(pe):
            pe.wait_ge(experts_in, 32)
            with pe.Fori(0, TILES // S) as it:
                n = it * S
                front.pe_transpose(pe, n)
                for s in range(S):
                    pe.wait_ge(front.xnT_done, n + s + 1)
                    nc.tensor.matmul(bank(s, 1), front.xnT[:, s, :], w_sim[:, :], start=True, stop=True).then_inc(simmed, 1)
                    for k in range(2):
                        last = nc.tensor.matmul(bank(s, 2 + k), front.xnT[:, s, :], down[:, k * 512:(k + 1) * 512],
                                                start=True, stop=True)
                    last.then_inc(valued, 1)
                for h in range(H):
                    for s in range(S):
                        pe.wait_ge(kept, n * H + (h + 2) * S + s + 1)
                        for k in range(2):
                            last = nc.tensor.matmul(bank(s, 2 + k), core.c("ident"),
                                                    prob[:, s, h % 2, k * 512:(k + 1) * 512],
                                                    start=(h == 0), stop=(h == H - 1))
                        last.then_inc(used, 1)
                for s in range(S):
                    pe.wait_ge(mixed, n + s + 1)
                    for c in range(E // P):
                        last = nc.tensor.transpose(pair(s, 0)[:, c * P:(c + 1) * P], weight[:, s, c * P:(c + 1) * P],
                                                   core.c("ident"))
                    last.then_inc(turned, 1)
                for s in range(S):
                    pe.wait_ge(mixT_done, n + s + 1)
                    for c in range(E // P):
                        last = nc.tensor.matmul(bank(s, 2)[:, 0:D], mixT[:, s, c, :], up[:, c, :], start=(c == 0),
                                                stop=(c == E // P - 1))
                    last.then_inc(out_done, 1)


def query_keys(core, name, w_sim, b_sim, down, up, experts_in):
    nc, dram = core.nc, core.dram
    S, KG, K = 4, 16, 32
    TOKENS = B * SEQ
    with ExitStack() as st:
        sb = lambda n, shape, dt=F32: st.enter_context(nc.sbuf_tensor(f"{name}_keys_{n}", shape, dt))
        w_q = sb("w_q", [D, KG * P])
        w_qT = sb("w_qT", [P, KG, D])
        keys = sb("keys", [P, KG, K])
        keys_s = sb("keys_s", [P, KG, K])
        gamma = sb("gamma", [P, KG])
        beta = sb("beta", [P, KG])
        zeros = sb("zeros", [P, P])
        gram = sb("gram", [D, D])
        mean = sb("mean", [D, 1])
        mean_row = sb("mean_row", [1, D])
        spread_w = sb("spread_w", [D, KG * P])
        var = sb("var", [P, KG])
        rstd = sb("rstd", [P, KG])
        shift = sb("shift", [P, KG])
        halves = sb("halves", [P, KG])
        front = Front(core, st, f"{name}1", S, None, transposed=False)
        names = ("wq_in", "zeroed", "added", "gram_done", "mean_done", "row_made", "row_done", "outer_made", "cov_done",
                 "cov_w", "cov_w_done", "stats_made", "var_done", "rstd_q", "keys_done", "sim_made")
        (wq_in, zeroed, added, gram_done, mean_done, row_made, row_done, outer_made, cov_done, cov_w, cov_w_done,
         stats_made, var_done, rstd_q, keys_done, sim_made) = (core.sem(f"{name}_{n}") for n in names)
        GRAM, MEAN = core.psum[:, 6, 0:D], core.psum[:, 7, 0:1]
        block = st.enter_context(nc.Block())

        @block.sync
        def _(sp):
            load(sp, [(w_q[:, :], dram[f"{name}_w_q"]), (w_qT[:, :, :], dram[f"{name}_w_q_T"]),
                      (keys[:, :, :], dram[f"{name}_keys"]), (gamma[:, :], dram[f"{name}_gamma"]),
                      (beta[:, :], dram[f"{name}_beta"])], wq_in)
            load(sp, [(down[:, :], dram[f"{name}_down_T"]), (up[:, :, :], dram[f"{name}_up"])], experts_in)

        @block.gpsimd
        def _(pool):
            nc.gpsimd.memset(zeros[:, :], 0.0).then_inc(zeroed, 1)
            nc.gpsimd.memset(halves[:, :], -0.5)
            with pool.Fori(0, TILES // S) as it:
                front.pool_rstd(pool, it * S)
            pool.wait_ge(var_done, 1)
            nc.gpsimd.tensor_tensor(rstd[:, :], var[:, :], halves[:, :], ALU.pow).then_inc(rstd_q, 1)

        @block.vector
        def _(dve):
            dve.sem_inc(added, S)
            with dve.Fori(0, TILES // S) as it:
                n = it * S
                front.dve_moments(dve, n)
                dve.wait_ge(added, n + S)
                front.dve_normalise(dve, n)
            dve.wait_ge(gram_done, 1)
            nc.vector.tensor_scalar(gram[:, :], GRAM, 1.0 / TOKENS, None, ALU.mult)
            nc.vector.tensor_scalar(mean[:, :], MEAN, 1.0 / TOKENS, None, ALU.mult).then_inc(mean_done, 1)
            dve.wait_ge(row_made, 1)
            nc.vector.tensor_copy(mean_row[:, :], core.psum[0:1, 0, 0:D]).then_inc(row_done, 1)
            dve.wait_ge(outer_made, 1)
            nc.vector.tensor_tensor(gram[:, :], gram[:, :], core.psum[:, 1, 0:D], ALU.subtract).then_inc(cov_done, 1)
            dve.wait_ge(cov_w, 1)
            for k in range(4):
                ins = nc.vector.tensor_tensor(spread_w[:, k * 512:(k + 1) * 512], w_q[:, k * 512:(k + 1) * 512],
                                              core.psum[:, k, :], ALU.mult)
            ins.then_inc(cov_w_done, 1)
            dve.wait_ge(stats_made, 1)
            nc.vector.tensor_scalar(var[:, :], core.psum[:, 4, 0:KG], LN_EPS, None, ALU.add).then_inc(var_done, 1)
            dve.wait_ge(rstd_q, 1)
            nc.vector.tensor_tensor(gamma[:, :], gamma[:, :], rstd[:, :], ALU.mult)
            dve.drain()
            nc.vector.tensor_tensor(shift[:, :], core.psum[:, 4, KG:2 * KG], gamma[:, :], ALU.mult)
            nc.vector.tensor_tensor(keys_s[:, :, :], keys[:, :, :],
                                    gamma[:, :].rearrange("p (g k) -> p g k", k=1).to_broadcast([P, KG, K]), ALU.mult)
            dve.drain()
            nc.vector.tensor_tensor(shift[:, :], beta[:, :], shift[:, :], ALU.subtract).then_inc(keys_done, 1)
            dve.wait_ge(sim_made, 1)
            nc.vector.tensor_copy(w_sim[:, :], core.psum[:, 2, :])
            nc.vector.tensor_copy(b_sim[:, :], core.psum[:, 3, :])

        @block.tensor
        def _(pe):
            pe.wait_ge(zeroed, 1)
            nc.tensor.matmul(GRAM, zeros[:, :], zeros[:, :], start=True, stop=False)
            nc.tensor.matmul(MEAN, zeros[:, :], zeros[:, 0:1], start=True, stop=False)
            with pe.Fori(0, TILES // S) as it:
                for s in range(S):
                    pe.wait_ge(front.normed, it * S + s + 1)
                    nc.tensor.matmul(GRAM, front.xn[:, s, :], front.xn[:, s, :], start=False, stop=False)
                    nc.tensor.matmul(MEAN, front.xn[:, s, :], core.ones[:, 0:1], start=False, stop=False).then_inc(added, 1)
            nc.tensor.matmul(GRAM, zeros[:, :], zeros[:, :], start=False, stop=True)
            nc.tensor.matmul(MEAN, zeros[:, :], zeros[:, 0:1], start=False, stop=True).then_inc(gram_done, 1)
            pe.wait_ge(mean_done, 1)
            nc.tensor.transpose(core.psum[0:1, 0, 0:D], mean[:, :], core.c("ident")).then_inc(row_made, 1)
            pe.wait_ge(row_done, 1)
            nc.tensor.matmul(core.psum[:, 1, 0:D], mean_row[:, :], mean_row[:, :], start=True, stop=True).then_inc(outer_made, 1)
            pe.wait_ge(cov_done, 1)
            pe.wait_ge(wq_in, 80)
            for k in range(4):
                last = nc.tensor.matmul(core.psum[:, k, :], gram[:, :], w_q[:, k * 512:(k + 1) * 512], start=True, stop=True)
            last.then_inc(cov_w, 1)
            pe.wait_ge(cov_w_done, 1)
            for g in range(KG):
                nc.tensor.matmul(core.psum[:, 4, g:g + 1], spread_w[:, g * P:(g + 1) * P], core.ones[:, 0:1],
                                 start=True, stop=True)
            for g in range(KG):
                last = nc.tensor.matmul(core.psum[:, 4, KG + g:KG + g + 1], w_q[:, g * P:(g + 1) * P], mean[:, :],
                                        start=True, stop=True)
            last.then_inc(stats_made, 1)
            pe.wait_ge(keys_done, 1)
            for g in range(KG):
                nc.tensor.matmul(core.psum[:, 2, g * K:(g + 1) * K], w_qT[:, g, :], keys_s[:, g, :], start=True, stop=True)
            for g in range(KG):
                last = nc.tensor.matmul(core.psum[:, 3, g * K:(g + 1) * K], shift[:, g:g + 1].to_broadcast([P, P]),
                                        keys[:, g, :], start=True, stop=True)
            last.then_inc(sim_made, 1)


def context_attention(core, name):
    nc, dram = core.nc, core.dram
    KEYS = CTX + SEQ
    CHUNKS = [(0, P), (P, P), (2 * P, SEQ + 1)]
    scale = 8 ** -0.5
    with ExitStack() as outer:
        keep = lambda n, shape, dt=F32: outer.enter_context(nc.sbuf_tensor(f"{name}_{n}", shape, dt))
        qT = keep("qT", [P, TILES, P])
        kT = keep("kT", [P, TILES, P])
        v = keep("v", [P, TILES, D])
        w_proj = keep("w_proj", [D, D])
        b_proj = keep("b_proj", [1, D])
        w_in = core.sem(f"{name}_w_in")
        own_qkv(core, name, qT, kT, v, scale, w_in, w_proj, b_proj)

        k_all = keep("k_all", [P, BT, KEYS])
        v_all = keep("v_all", [P, BT, 3, D])
        q_bd = keep("q_bd", [P, BT, HEADS, SEQ])
        prob = keep("prob", [P, 2, 2, KEYS])
        nmax = keep("nmax", [P, 2, 2])
        total = keep("total", [P, 2, 2])
        own = keep("own", [P, 2, 2, G])
        probT = keep("probT", [P, 2, 3, 2, P])
        heads = keep("heads", [P, 2, 2 * G, 8])
        attnT = keep("attnT", [P, P])
        scores = lambda s: core.psum[:, 4 * s:4 * s + 2, 0:KEYS]
        turned_end = lambda s: core.psum[0:SEQ + 1, 4 * s + 3, 96:96 + 2 * P].rearrange("p (g w) -> p g w", g=2)
        turned_bank = lambda s: core.psum[:, 4 * s + 2, :].rearrange("p (k g w) -> p k g w", k=2, g=2)
        mix = lambda s: core.psum[:, 4 * s + 3, 0:64]
        join = lambda s: core.psum[64 * s:64 * s + 64, 4 * s + 3, 64:64 + SEQ]
        OUT = core.psum[:, 7, 352:352 + D]
        ctx_in = [core.sem(f"{name}_ctx_in{b}") for b in range(BT)]
        (prepared, scored, maxed, exped, turned, probT_done, endT_done, mixed, split, joined, joined_out,
         out_done, tile_done) = (core.sem(f"{name}_{n}") for n in (
             "prepared", "scored", "maxed", "exped", "turned", "probT_done", "endT_done", "mixed", "split",
             "joined", "joined_out", "out_done", "tile_done"))
        block = outer.enter_context(nc.Block())
        UNITS = 2 * BT

        def over_tiles(eng, tile):
            with eng.Fori(0, TILES - 1) as t:
                tile(t, False)
            tile(TILES - 1, True)

        def ahead(t, u, last, by):
            return (t, u + by) if u + by < UNITS else None if last else (t + 1, u + by - UNITS)

        @block.sync
        def _(sp):
            with sp.Fori(0, TILES) as t:
                for b in range(BT):
                    sp.wait_ge(mixed, t * UNITS + 2 * b + 2)
                    seq = t * BT + b
                    row = dram["ctx_2048"][ds(seq, 1), :, :].rearrange("a m c -> (a m) c")
                    for dst, src in ((k_all[:, b, 0:CTX], dram["ctx_T"][ds(seq, 1), 0:D, :].rearrange("a c m -> (a c) m")),
                                     (v_all[:, b, 0:2, :], row[0:2 * P, D:2 * D].rearrange("(k m) c -> m k c", m=P)),
                                     (v_all[0:1, b, 2, :], row[2 * P:CTX, D:2 * D]),
                                     (v_all[1:1 + SEQ, b, 2, :], v[b * SEQ:(b + 1) * SEQ, ds(t, 1), :])):
                        sp.dma_start(dst, src).then_inc(ctx_in[b], 16)

        @block.gpsimd
        def _(pool):
            with pool.Fori(0, TILES) as t:
                for b in range(BT):
                    pool.wait_ge(mixed, t * UNITS + 2 * b + 2)
                    cols = slice(b * SEQ, (b + 1) * SEQ)
                    a = qT[:, ds(t, 1), cols].to_broadcast([P, HEADS, SEQ])
                    m = core.c("head").rearrange("p (j w) -> p j w", w=1).to_broadcast([P, HEADS, SEQ])
                    nc.gpsimd.tensor_tensor(q_bd[:, b, :, :], a, m, ALU.mult)
                    nc.gpsimd.tensor_copy(k_all[:, b, CTX:KEYS], kT[:, ds(t, 1), cols]).then_inc(prepared, 1)

        @block.scalar
        def _(act):
            def exps(t, u):
                s = u % 2
                act.wait_ge(maxed, t * UNITS + u + 1)
                for g in range(2):
                    ins = nc.scalar.activation(prob[:, s, g, :], scores(s)[:, g, :], ACT.Exp,
                                               bias=nmax[:, s, g:g + 1], accum_out=total[:, s, g:g + 1])
                ins.then_inc(exped, 1)

            def join_out(t, u):
                b, s = u // 2, u % 2
                act.wait_ge(joined, t * UNITS + u + 1)
                nc.scalar.copy(attnT[64 * s:64 * s + 64, b * SEQ:(b + 1) * SEQ], join(s)).then_inc(joined_out, 1)

            def tile(t, last):
                for u in range(UNITS):
                    act.wait_ge(turned, t * UNITS + u + 1)
                    nc.scalar.copy(probT[0:SEQ + 1, u % 2, 2, :, :], turned_end(u % 2)).then_inc(endT_done, 1)
                    if ahead(t, u, last, 2):
                        exps(*ahead(t, u, last, 2))
                    if u:
                        join_out(t, u - 1)
                join_out(t, UNITS - 1)

            exps(0, 0)
            exps(0, 1)
            over_tiles(act, tile)

        @block.vector
        def _(dve):
            own_mask = core.c("group").rearrange("p (g j) -> p g j", g=1).to_broadcast([P, 2, G])

            def maxes(t, u):
                dve.wait_ge(scored, t * UNITS + u + 1)
                nc.vector.tensor_reduce(nmax[:, u % 2, :], scores(u % 2), X, ALU.max, negate=True).then_inc(maxed, 1)

            def shares(t, u):
                s = u % 2
                dve.wait_ge(exped, t * UNITS + u + 1)
                nc.vector.reciprocal(total[:, s, :], total[:, s, :])
                dve.drain()
                inv = total[:, s, :].rearrange("p (g j) -> p g j", j=1).to_broadcast([P, 2, G])
                nc.vector.tensor_tensor(own[:, s, :, :], inv, own_mask, ALU.mult)

            def tile(t, last):
                for u in range(UNITS):
                    s = u % 2
                    dve.wait_ge(turned, t * UNITS + u + 1)
                    nc.vector.tensor_copy(probT[:, s, 0:2, :, :], turned_bank(s)).then_inc(probT_done, 1)
                    if ahead(t, u, last, 2):
                        maxes(*ahead(t, u, last, 2))
                    dve.wait_ge(mixed, (t + 1) * UNITS + u + 1)
                    m = own[:, s, :, :].rearrange("p g j -> p (g j)").rearrange("p (a w) -> p a w", w=1)
                    nc.vector.tensor_tensor(heads[:, s, :, :], mix(s).rearrange("p (a w) -> p a w", w=8),
                                            m.to_broadcast([P, 2 * G, 8]), ALU.mult).then_inc(split, 1)
                    if ahead(t, u, last, 1):
                        shares(*ahead(t, u, last, 1))
                dve.wait_ge(out_done, t + 1)
                add_to_x(core, t, OUT).then_inc(tile_done, 1)

            maxes(0, 0)
            maxes(0, 1)
            shares(0, 0)
            over_tiles(dve, tile)

        @block.tensor
        def _(pe):
            def score(t, u):
                b, s = u // 2, u % 2
                if s == 0:
                    pe.wait_ge(ctx_in[b], (t + 1) * 16 * 4)
                    pe.wait_ge(prepared, t * BT + b + 1)
                for g in range(2):
                    h = 8 * s + 4 * g
                    ins = nc.tensor.matmul(scores(s)[:, g, :], q_bd[:, b, h:h + 4, :].rearrange("p j w -> p (j w)"),
                                           k_all[:, b, :], start=True, stop=True)
                ins.then_inc(scored, 1)

            def join_heads(t, u):
                pe.wait_ge(split, t * UNITS + u + 1)
                nc.tensor.matmul(join(u % 2), heads[:, u % 2, :, :].rearrange("p a w -> p (a w)"), core.c("sel"),
                                 start=True, stop=True).then_inc(joined, 1)

            def tile(t, last):
                n = t * UNITS
                for u in range(UNITS):
                    b, s = u // 2, u % 2
                    if u == 1:
                        pe.wait_ge(tile_done, t + 1)
                    if u >= 2:
                        pe.wait_ge(joined_out, n + u - 1)
                    pe.wait_ge(exped, n + u + 1)
                    for g in range(2):
                        for k, (at, size) in enumerate(CHUNKS):
                            dst = turned_end(s)[:, g, :] if k == 2 else turned_bank(s)[:, k, g, :]
                            ins = nc.tensor.transpose(dst, prob[:, s, g, at:at + size], core.c("ident"))
                    ins.then_inc(turned, 1)
                    if ahead(t, u, last, 2):
                        score(*ahead(t, u, last, 2))
                    pe.wait_ge(probT_done, n + u + 1)
                    pe.wait_ge(endT_done, n + u + 1)
                    for g in range(2):
                        for k, (at, size) in enumerate(CHUNKS):
                            ins = nc.tensor.matmul(mix(s)[:, g * 32:(g + 1) * 32], probT[0:size, s, k, g, :],
                                                   v_all[0:size, b, k, 32 * (2 * s + g):32 * (2 * s + g) + 32],
                                                   start=(k == 0), stop=(k == 2))
                    ins.then_inc(mixed, 1)
                    if u:
                        join_heads(t, u - 1)
                join_heads(t, UNITS - 1)
                pe.wait_ge(joined_out, n + UNITS)
                nc.tensor.matmul(OUT, attnT[:, :], w_proj[:, :], start=True, stop=False)
                nc.tensor.matmul(OUT, core.ones[0:1, :], b_proj[:, :], start=False, stop=True).then_inc(out_done, 1)

            pe.sem_inc(mixed, UNITS)
            pe.sem_inc(tile_done, 1)
            pe.wait_ge(w_in, 48)
            score(0, 0)
            score(0, 1)
            over_tiles(pe, tile)


def own_qkv(core, name, qT, kT, v, scale, w_in, w_proj, b_proj):
    nc, dram = core.nc, core.dram
    S, U = 8, 2
    with ExitStack() as st:
        w = st.enter_context(nc.sbuf_tensor(f"{name}_w", [D, 3 * D], F32))
        front = Front(core, st, name, S, lambda s: core.psum[:, s // 4, s % 4 * P:s % 4 * P + P], pack=4)
        made, q_done, kv_done = (core.sem(f"{name}_own_{n}") for n in ("made", "q_done", "kv_done"))
        block = st.enter_context(nc.Block())

        @block.sync
        def _(sp):
            load(sp, [(w[:, :], dram[f"{name}_w_qkv_T"]), (w_proj[:, :], dram[f"{name}_w_proj_T"]),
                      (b_proj[:, :], dram[f"{name}_b_proj"])], w_in)

        @block.gpsimd
        def _(pool):
            with pool.Fori(0, TILES // S) as it:
                front.pool_rstd(pool, it * S)

        tiles = lambda t: t.rearrange("p (t w) -> p t w", w=P)

        @block.scalar
        def _(act):
            with act.Fori(0, TILES // S) as it:
                front.act_copy(act, it * S)
                for u in range(U):
                    act.wait_ge(made, it * U + u + 1)
                    nc.scalar.activation(qT[:, ds(it * S + 4 * u, 4), :], tiles(core.psum[:, 2 + u, :]), ACT.Copy,
                                         scale=scale).then_inc(q_done, 1)

        @block.vector
        def _(dve):
            with dve.Fori(0, TILES // S) as it:
                front.dve_moments(dve, it * S)
                front.dve_normalise(dve, it * S)
                for u in range(U):
                    dve.wait_ge(made, it * U + u + 1)
                    nc.vector.tensor_copy(kT[:, ds(it * S + 4 * u, 4), :], tiles(core.psum[:, 4 + u, :]))
                    nc.vector.tensor_copy(v[:, ds(it * S + 4 * u, 4), :], tiles(core.psum[:, 6 + u, :])).then_inc(kv_done, 1)

        @block.tensor
        def _(pe):
            pe.wait_ge(w_in, 48)
            pe.sem_inc(q_done, U)
            with pe.Fori(0, TILES // S) as it:
                front.pe_transpose(pe, it * S)
                for u in range(U):
                    xnT = front.xnT[:, 4 * u:4 * u + 4, :].rearrange("p s w -> p (s w)")
                    pe.wait_ge(front.xnT_done, it * S + 4 * u + 4)
                    pe.wait_ge(q_done, it * U + u + 1)
                    nc.tensor.matmul(core.psum[:, 2 + u, :], w[:, 0:D], xnT, start=True, stop=True)
                    nc.tensor.matmul(core.psum[:, 4 + u, :], w[:, D:2 * D], xnT, start=True, stop=True)
                    for s in range(4):
                        last = nc.tensor.matmul(core.psum[:, 6 + u, s * P:(s + 1) * P], front.xnT[:, 4 * u + s, :],
                                                w[:, 2 * D:3 * D], start=True, stop=True)
                    last.then_inc(made, 1)


def gated_scan(core, name):
    nc, dram = core.nc, core.dram
    S, C, N = 4, 2, 512
    R = 16
    with ExitStack() as st:
        sb = lambda n, shape, dt=F32: st.enter_context(nc.sbuf_tensor(f"{name}_{n}", shape, dt))
        w_in = sb("w_in", [D, 2 * C, P])
        w_x = sb("w_x", [P, C, 2 * R])
        w_dt = sb("w_dt", [2 * R, C, P])
        w_bp = sb("w_bp", [2 * R, C, P])
        w_out = sb("w_out", [P, C, D])
        taps = sb("taps", [P, C, 4])
        b_dt = sb("b_dt", [P, C])
        skip = sb("skip", [P, C])
        conv = sb("conv", [P, C, N])
        u = sb("u", [P, C, N])
        z = sb("z", [P, C, N])
        low = sb("low", [2 * R, N])
        soft = sb("soft", [P, C, N])
        dt = sb("dt", [P, C, N])
        ub = sb("ub", [P, C, N])
        y = sb("y", [P, C, N])
        front = Front(core, st, name, S, lambda s: core.psum[:, 0, s * P:(s + 1) * P], pack=4)
        (wts_in, zeroed, in_done, conv_first, conv_done, u_done, low_made, low_done, dt_made, b_made, soft_done, y_done,
         out_done) = (core.sem(f"{name}_{n}") for n in (
             "wts_in", "zeroed", "in_done", "conv_first", "conv_done", "u_done", "low_made", "low_done", "dt_made",
             "b_made", "soft_done", "y_done", "out_done"))
        block = st.enter_context(nc.Block())
        seqs = lambda t: t.rearrange("p (b t) -> p b t", t=SEQ)
        STEPS = TILES // S

        @block.sync
        def _(sp):
            sp.wait_ge(zeroed, 1)
            load(sp, [(w_in[:, :, :], dram[f"{name}_W_in"]), (w_x[:, :, :], dram[f"{name}_W_x"]),
                      (w_dt[0:R, :, :], dram[f"{name}_W_dt"]), (w_bp[R:2 * R, :, :], dram[f"{name}_W_Bp"]),
                      (w_out[:, :, :], dram[f"{name}_W_out"]), (taps[:, :, :], dram[f"{name}_conv_w"]),
                      (b_dt[:, :], dram[f"{name}_b_dt"]), (skip[:, :], dram[f"{name}_D_param"])], wts_in)

        @block.gpsimd
        def _(pool):
            nc.gpsimd.memset(w_dt[:, :, :], 0.0)
            nc.gpsimd.memset(w_bp[:, :, :], 0.0).then_inc(zeroed, 1)
            with pool.Fori(0, STEPS) as it:
                front.pool_rstd(pool, it * S)

        @block.scalar
        def _(act):
            act.wait_ge(wts_in, 128)
            with act.Fori(0, STEPS) as it:
                front.act_copy(act, it * S)
                n = it * C
                for c in range(C):
                    act.wait_ge(in_done, n + c + 1)
                    nc.scalar.activation(conv[:, c, :], core.psum[:, 1 + c, :], ACT.Copy,
                                         scale=taps[:, c, 3:4]).then_inc(conv_first, 1)
                for c in range(C):
                    nc.scalar.activation(z[:, c, :], core.psum[:, 3 + c, :], ACT.Silu)
                for c in range(C):
                    act.wait_ge(conv_done, n + c + 1)
                    nc.scalar.activation(u[:, c, :], conv[:, c, :], ACT.Silu).then_inc(u_done, 1)
                act.wait_ge(low_made, it + 1)
                nc.scalar.copy(low[:, :], core.psum[0:2 * R, 5, :]).then_inc(low_done, 1)
                for c in range(C):
                    act.wait_ge(dt_made, n + c + 1)
                    nc.scalar.activation(soft[:, c, :], core.psum[:, 1 + c, :], ACT.Abs, bias=b_dt[:, c:c + 1])
                act.drain()
                nc.scalar.activation(soft[:, :, :], soft[:, :, :], ACT.Exp, scale=-1.0)
                act.drain()
                nc.scalar.activation(soft[:, :, :], soft[:, :, :], ACT.Ln, bias=1.0).then_inc(soft_done, 1)

        @block.vector
        def _(dve):
            dve.wait_ge(wts_in, 128)
            with dve.Fori(0, STEPS) as it:
                front.dve_moments(dve, it * S)
                front.dve_normalise(dve, it * S)
                n = it * C
                for tap in range(3):
                    lag = 3 - tap
                    for c in range(C):
                        if tap == 0:
                            dve.wait_ge(conv_first, n + c + 1)
                        nc.vector.scalar_tensor_tensor(
                            seqs(conv[:, c, :])[:, :, lag:], seqs(core.psum[:, 1 + c, :])[:, :, 0:SEQ - lag],
                            taps[:, c, tap:tap + 1], seqs(conv[:, c, :])[:, :, lag:], ALU.mult, ALU.add)
                    dve.drain()
                dve.sem_inc(conv_done, C)
                for c in range(C):
                    dve.wait_ge(dt_made, n + c + 1)
                    dve.wait_ge(soft_done, it + 1)
                    nc.vector.tensor_scalar(dt[:, c, :], core.psum[:, 1 + c, :], b_dt[:, c:c + 1], 0.0, ALU.add, ALU.max)
                dve.drain()
                nc.vector.tensor_tensor(dt[:, :, :], dt[:, :, :], soft[:, :, :], ALU.add)
                for c in range(C):
                    dve.wait_ge(b_made, n + c + 1)
                    nc.vector.tensor_tensor(ub[:, c, :], u[:, c, :], core.psum[:, 6 + c, :], ALU.mult)
                dve.drain()
                nc.vector.tensor_scalar(dt[:, :, :], dt[:, :, :], 1e-4, 1.0, ALU.max, ALU.min)
                dve.drain()
                nc.vector.tensor_scalar(dt[:, :, :], dt[:, :, :], -1.0, 1.0, ALU.mult, ALU.add)
                dve.drain()
                nc.vector.memset(dt[:, :, :].rearrange("p c (b t) -> p (c b) t", t=SEQ)[:, :, 0:1], 0.0)
                dve.drain()
                for c in range(C):
                    nc.vector.tensor_tensor_scan(y[:, c, :], dt[:, c, :], ub[:, c, :], 0.0, ALU.mult, ALU.add)
                dve.drain()
                for c in range(C):
                    nc.vector.scalar_tensor_tensor(y[:, c, :], u[:, c, :], skip[:, c:c + 1], y[:, c, :], ALU.mult,
                                                   ALU.add)
                dve.drain()
                nc.vector.tensor_tensor(y[:, :, :], y[:, :, :], z[:, :, :], ALU.mult).then_inc(y_done, 1)
                dve.wait_ge(out_done, it + 1)
                x = core.x[:, ds(it * S, S), :]
                nc.vector.tensor_tensor(x, x, core.psum[:, 0, :].rearrange("p (t w) -> p t w", w=D), ALU.add)

        @block.tensor
        def _(pe):
            pe.wait_ge(wts_in, 128)
            with pe.Fori(0, STEPS) as it:
                n = it * C
                front.pe_transpose(pe, it * S)
                xnT = front.xnT[:, :, :].rearrange("p s w -> p (s w)")
                pe.wait_ge(front.xnT_done, it * S + S)
                for m in (2, 3, 0, 1):
                    ins = nc.tensor.matmul(core.psum[:, 1 + m, :], w_in[:, m, :], xnT, start=True, stop=True)
                    if m < C:
                        ins.then_inc(in_done, 1)
                pe.wait_ge(u_done, n + C)
                for c in range(C):
                    last = nc.tensor.matmul(core.psum[0:2 * R, 5, :], w_x[:, c, :], u[:, c, :], start=(c == 0),
                                            stop=(c == C - 1))
                last.then_inc(low_made, 1)
                pe.wait_ge(low_done, it + 1)
                for c in range(C):
                    nc.tensor.matmul(core.psum[:, 1 + c, :], w_dt[:, c, :], low[:, :], start=True,
                                     stop=True).then_inc(dt_made, 1)
                for c in range(C):
                    nc.tensor.matmul(core.psum[:, 6 + c, :], w_bp[:, c, :], low[:, :], start=True,
                                     stop=True).then_inc(b_made, 1)
                pe.wait_ge(y_done, it + 1)
                for t in range(S):
                    for c in range(C):
                        last = nc.tensor.matmul(core.psum[:, 0, t * P:(t + 1) * P], y[:, c, t * P:(t + 1) * P],
                                                w_out[:, c, :], start=(c == 0), stop=(c == C - 1))
                last.then_inc(out_done, 1)


def ternary_ffn(core, name):
    nc, dram = core.nc, core.dram
    S, H = 4, 512
    C = H // P
    with ExitStack() as st:
        sb = lambda n, shape, dt=F32: st.enter_context(nc.sbuf_tensor(f"{name}_{n}", shape, dt))
        w_fc = sb("w_fc", [D, H])
        w_proj = sb("w_proj", [P, C, D])
        ln_w = sb("ln_w", [P, C])
        ln_b = sb("ln_b", [P, C])
        row = sb("row", [1, D])
        mass = sb("mass", [P, 2])
        limit = sb("limit", [P, 2, 2])
        low = sb("low", [P, H])
        h = sb("h", [P, S, H])
        hT = sb("hT", [P, S, C, P])
        h_stats, h_mv = sb("h_stats", [P, S, 6]), sb("h_mv", [P, S, 2])
        h_var, h_rstd = sb("h_var", [P, S, 1]), sb("h_rstd", [P, S, 1])
        bank_a = lambda s: core.psum[:, 2 * s, :]
        bank_b = lambda s: core.psum[:, 2 * s + 1, :]
        front = Front(core, st, name, S, bank_a)
        (w_in, masses, summed, w_done, row_made, row_done, wide, gelued, h_moments, h_rstd_done, h_normed, turned,
         hT_done, out_done) = (core.sem(f"{name}_{n}") for n in (
             "w_in", "masses", "summed", "w_done", "row_made", "row_done", "wide", "gelued", "h_moments",
             "h_rstd_done", "h_normed", "turned", "hT_done", "out_done"))
        block = st.enter_context(nc.Block())

        @block.sync
        def _(sp):
            load(sp, [(w_fc[:, :], dram[f"{name}_W_fc_T"]), (w_proj[:, :, :], dram[f"{name}_W_proj_T"]),
                      (ln_w[:, :], dram[f"{name}_ln_w"]), (ln_b[:, :], dram[f"{name}_ln_b"])], w_in)

        @block.gpsimd
        def _(pool):
            with pool.Fori(0, TILES // S) as it:
                n = it * S
                front.pool_rstd(pool, n)
                for s in range(S):
                    pool.wait_ge(h_moments, n + s + 1)
                    nc.gpsimd.tensor_tensor(h_var[:, s, :], h_mv[:, s, 1:2], core.eps[:, :], ALU.add)
                pool.drain()
                for s in range(S):
                    nc.gpsimd.tensor_tensor(h_rstd[:, s, :], h_var[:, s, :], core.half[:, :],
                                            ALU.pow).then_inc(h_rstd_done, 1)

        @block.scalar
        def _(act):
            act.wait_ge(row_made, 1)
            nc.scalar.copy(row[:, :], core.psum[0:1, 6, 0:D]).then_inc(row_done, 1)
            with act.Fori(0, TILES // S) as it:
                n = it * S
                front.act_copy(act, n)
                for s in range(S):
                    act.wait_ge(wide, n + s + 1)
                    nc.scalar.activation(h[:, s, :], bank_b(s), ACT.Gelu).then_inc(gelued, 1)
                for s in range(S):
                    act.wait_ge(turned, n + s + 1)
                    nc.scalar.copy(hT[:, s, :, :], bank_a(s).rearrange("p (c w) -> p c w", c=C)).then_inc(hT_done, 1)

        @block.vector
        def _(dve):
            dve.wait_ge(w_in, 64)
            nc.vector.tensor_reduce(mass[:, 0:1], w_fc[:, :], X, ALU.add, apply_absolute_value=True)
            nc.vector.tensor_reduce(mass[:, 1:2], w_proj[:, :, :], XY, ALU.add,
                                    apply_absolute_value=True).then_inc(masses, 1)
            dve.wait_ge(summed, 1)
            nc.vector.tensor_scalar(limit[:, 0, :], core.psum[:, 7, 0:2], 1.0 / (H * D), 1e-6, ALU.mult, ALU.add)
            dve.drain()
            nc.vector.tensor_scalar(limit[:, 1, :], limit[:, 0, :], -0.5, None, ALU.mult)
            dve.drain()
            nc.vector.tensor_scalar(limit[:, 0, :], limit[:, 0, :], 0.5, None, ALU.mult)
            for i, w in enumerate((w_fc[:, :], w_proj[:, :, :].rearrange("p c d -> p (c d)"))):
                dve.drain()
                nc.vector.tensor_scalar(low[:, :], w, limit[:, 1, i:i + 1], None, ALU.is_lt)
                dve.drain()
                nc.vector.scalar_tensor_tensor(w, w, limit[:, 0, i:i + 1], low[:, :], ALU.is_gt,
                                               ALU.subtract).then_inc(w_done, 1)
            dve.wait_ge(row_made, 1)
            for c in range(C):
                nc.vector.tensor_scalar(w_proj[:, c, :], w_proj[:, c, :], ln_w[:, c:c + 1], None,
                                        ALU.mult).then_inc(w_done, 1)
            with dve.Fori(0, TILES // S) as it:
                n = it * S
                front.dve_moments(dve, n)
                front.dve_normalise(dve, n)
                for s in range(S):
                    dve.wait_ge(gelued, n + s + 1)
                    nc.vector.bn_stats(h_stats[:, s, :], h[:, s, :])
                dve.drain()
                for s in range(S):
                    nc.vector.bn_aggr(h_mv[:, s, :], h_stats[:, s, :]).then_inc(h_moments, 1)
                for s in range(S):
                    dve.wait_ge(h_rstd_done, n + s + 1)
                    nc.vector.tensor_scalar(h[:, s, :], h[:, s, :], h_mv[:, s, 0:1], h_rstd[:, s, :], ALU.subtract,
                                            ALU.mult).then_inc(h_normed, 1)
                for s in range(S):
                    dve.wait_ge(out_done, n + s + 1)
                    add_to_x(core, n + s, bank_b(s)[:, 0:D])

        @block.tensor
        def _(pe):
            pe.wait_ge(masses, 1)
            nc.tensor.matmul(core.psum[:, 7, 0:2], core.ones[:, :], mass[:, :], start=True, stop=True).then_inc(summed, 1)
            pe.wait_ge(w_done, 2)
            for c in range(C):
                last = nc.tensor.matmul(core.psum[0:1, 6, 0:D], ln_b[:, c:c + 1], w_proj[:, c, :], start=(c == 0),
                                        stop=(c == C - 1))
            last.then_inc(row_made, 1)
            pe.wait_ge(w_done, 2 + C)
            pe.wait_ge(row_done, 1)
            with pe.Fori(0, TILES // S) as it:
                n = it * S
                front.pe_transpose(pe, n)
                for s in range(S):
                    pe.wait_ge(front.xnT_done, n + s + 1)
                    nc.tensor.matmul(bank_b(s), front.xnT[:, s, :], w_fc[:, :], start=True, stop=True).then_inc(wide, 1)
                for s in range(S):
                    pe.wait_ge(h_normed, n + s + 1)
                    for c in range(C):
                        last = nc.tensor.transpose(bank_a(s)[:, c * P:(c + 1) * P], h[:, s, c * P:(c + 1) * P],
                                                   core.c("ident"))
                    last.then_inc(turned, 1)
                for s in range(S):
                    pe.wait_ge(hT_done, n + s + 1)
                    for c in range(C):
                        nc.tensor.matmul(bank_b(s)[:, 0:D], hT[:, s, c, :], w_proj[:, c, :], start=(c == 0), stop=False)
                    nc.tensor.matmul(bank_b(s)[:, 0:D], core.ones[0:1, :], row[:, :], start=False,
                                     stop=True).then_inc(out_done, 1)


def wide_context_attention(core, name):
    with ExitStack() as outer:
        keep = lambda n, shape, dt=F32: outer.enter_context(core.nc.sbuf_tensor(f"{name}_{n}", shape, dt))
        m_h = keep("m_h", [D, HEADS, CD])
        u_h = keep("u_h", [P, 2, HEADS, D])
        w_null = keep("w_null", [D, HEADS])
        v_null = keep("v_null", [HEADS, D])
        xnT = keep("xnT", [D, TILES, P])
        s_null = keep("s_null", [HEADS, TILES, P])
        fold_weights(core, name, m_h, u_h, w_null, v_null)
        transposed_tokens(core, name, w_null, xnT, s_null)
        wide_attention(core, name, outer, m_h, u_h, v_null, xnT, s_null)


def fold_weights(core, name, m_h, u_h, w_null, v_null):
    nc, dram = core.nc, core.dram
    F = 64
    with ExitStack() as st:
        sb = lambda n, shape, dt=F32: st.enter_context(nc.sbuf_tensor(f"{name}_{n}", shape, dt))
        wq, wk, wv, wo = sb("wq", [F, HEADS, D]), sb("wk", [F, HEADS, CD]), sb("wv", [F, HEADS, CD]), sb("wo", [F, HEADS, D])
        null = sb("null", [F, 2])
        diag = sb("diag", [F, HEADS * HEADS])
        qk_in, vo_in, diag_done, m_made, m_out, u_made, u_out, null_made = (core.sem(f"{name}_{n}") for n in (
            "qk_in", "vo_in", "diag_done", "m_made", "m_out", "u_made", "u_out", "null_made"))
        block = st.enter_context(nc.Block())

        @block.sync
        def _(sp):
            load(sp, [(wq[:, :, :], dram[f"{name}_WqT"]), (wk[:, :, :], dram[f"{name}_WkT"]),
                      (null[:, :], dram[f"{name}_null_kv_T"])], qk_in)

        @block.scalar
        def _(act):
            load(act, [(wv[:, :, :], dram[f"{name}_WvT"]), (wo[:, :, :], dram[f"{name}_Wo"])], vo_in)
            for k in range(8):
                act.wait_ge(m_made, k + 1)
                nc.scalar.activation(m_h[:, 2 * k:2 * k + 2, :], core.psum[:, k, :].rearrange("p (h c) -> p h c", h=2),
                                     ACT.Copy, scale=F ** -0.5).then_inc(m_out, 1)
            act.wait_ge(null_made, 1)
            nc.scalar.activation(w_null[:, :], core.psum[:, 0, 0:HEADS], ACT.Copy, scale=F ** -0.5)
            nc.scalar.copy(v_null[:, :], core.psum[0:HEADS, 0, P:2 * P])

        @block.vector
        def _(dve):
            nc.vector.memset(diag[:, :], 0.0)
            dve.drain()
            dve.wait_ge(qk_in, 48)
            nc.vector.tensor_copy(diag[:, 0:HEADS * HEADS:HEADS + 1],
                                  null[:, 1:2].to_broadcast([F, HEADS])).then_inc(diag_done, 1)
            for k in range(8):
                dve.wait_ge(u_made, k + 1)
                nc.vector.tensor_copy(u_h[:, k // 4, k % 4 * 4:k % 4 * 4 + 4, :],
                                      core.psum[:, k, :].rearrange("p (h e) -> p h e", h=4)).then_inc(u_out, 1)

        @block.tensor
        def _(pe):
            pe.wait_ge(qk_in, 48)
            for k in range(8):
                for i in range(2):
                    last = nc.tensor.matmul(core.psum[:, k, i * CD:(i + 1) * CD], wq[:, 2 * k + i, :], wk[:, 2 * k + i, :],
                                            start=True, stop=True)
                last.then_inc(m_made, 1)
            pe.wait_ge(vo_in, 32)
            for k in range(8):
                c, h = k // 4, k % 4 * 4
                pe.wait_ge(m_out, k + 1)
                for i in range(4):
                    last = nc.tensor.matmul(core.psum[:, k, i * D:(i + 1) * D], wv[:, h + i, c * P:(c + 1) * P],
                                            wo[:, h + i, :], start=True, stop=True)
                last.then_inc(u_made, 1)
            pe.wait_ge(u_out, 1)
            for h in range(HEADS):
                nc.tensor.matmul(core.psum[:, 0, h:h + 1], wq[:, h, :], null[:, 0:1], start=True, stop=True)
            pe.wait_ge(diag_done, 1)
            for h in range(HEADS):
                last = nc.tensor.matmul(core.psum[0:HEADS, 0, P:2 * P], diag[:, h * HEADS:(h + 1) * HEADS], wo[:, h, :],
                                        start=(h == 0), stop=(h == HEADS - 1))
            last.then_inc(null_made, 1)


def transposed_tokens(core, name, w_null, xnT, s_null):
    nc = core.nc
    S, U = 8, 2
    with ExitStack() as st:
        front = Front(core, st, name, S, lambda s: core.psum[:, s // 4, s % 4 * P:s % 4 * P + P], transposed=False, pack=4)
        scored, score_out = core.sem(f"{name}_null_scored"), core.sem(f"{name}_null_score_out")
        block = st.enter_context(nc.Block())

        @block.gpsimd
        def _(pool):
            with pool.Fori(0, TILES // S) as it:
                front.pool_rstd(pool, it * S)

        @block.scalar
        def _(act):
            with act.Fori(0, TILES // S) as it:
                for u in range(U):
                    act.wait_ge(front.turned, it * S + 4 * u + 4)
                    nc.scalar.copy(xnT[:, ds(it * S + 4 * u, 4), :],
                                   core.psum[:, u, :].rearrange("p (s w) -> p s w", w=P)).then_inc(front.xnT_done, 1)

        @block.vector
        def _(dve):
            with dve.Fori(0, TILES // S) as it:
                front.dve_moments(dve, it * S)
                front.dve_normalise(dve, it * S)
                for u in range(U):
                    dve.wait_ge(scored, it * U + u + 1)
                    nc.vector.tensor_copy(s_null[:, ds(it * S + 4 * u, 4), :],
                                          core.psum[0:HEADS, 2 + u, :].rearrange("p (s w) -> p s w", w=P)).then_inc(score_out, 1)

        @block.tensor
        def _(pe):
            pe.sem_inc(score_out, U)
            with pe.Fori(0, TILES // S) as it:
                front.pe_transpose(pe, it * S)
                for u in range(U):
                    pe.wait_ge(score_out, it * U + u + 1)
                    pe.wait_ge(front.xnT_done, it * U + u + 1)
                    nc.tensor.matmul(core.psum[0:HEADS, 2 + u, :], w_null[:, :],
                                     xnT[:, ds(it * S + 4 * u, 4), :].rearrange("p s w -> p (s w)"),
                                     start=True, stop=True).then_inc(scored, 1)


def wide_attention(core, name, st, m_h, u_h, v_null, xnT, s_null):
    nc, dram = core.nc, core.dram
    KEYS = CTX + 1
    LN2_EPS = 1e-6
    UNITS = 2 * BT
    sb = lambda n, shape, dt=F32: st.enter_context(nc.sbuf_tensor(f"{name}_{n}", shape, dt))
    ctxT = sb("ctxT", [P, BT, 2, CTX])
    ctx = sb("ctx", [P, BT, 2, CD])
    ctx_last = sb("ctx_last", [1, BT, CD])
    q_ctx = sb("q_ctx", [P, 2, BT, HEADS, SEQ])
    null_bd = sb("null_bd", [HEADS, 2, HEADS, SEQ])
    prob = sb("prob", [P, 2, 2, KEYS])
    nmax = sb("nmax", [P, 2, 2])
    total = sb("total", [P, 2, 2])
    probT = sb("probT", [P, 2, 2, 2 * P])
    lastT = sb("lastT", [2, HEADS, P])
    nullT = sb("nullT", [HEADS, P])
    mixed_ctx = sb("mixed_ctx", [P, 2, HEADS, P])
    z = sb("z", [P, D])
    z_stats, z_mv, z_var = sb("z_stats", [P, 6]), sb("z_mv", [P, 2]), sb("z_var", [P, 2])
    z_eps = sb("z_eps", [P, 1])
    ln_scale, ln_bias = sb("ln_scale", [P, D]), sb("ln_bias", [P, D])
    scores = lambda s: core.psum[:, 4 * s:4 * s + 2, 0:KEYS]
    turned_last = lambda s: core.psum[0:2, 4 * s:4 * s + 2, KEYS:KEYS + P]
    turned_bank = lambda s: core.psum[:, 4 * s + 2, :]
    mix_bank = lambda s: core.psum[:, 4 * s + 3, :]
    OUT = core.psum[:, 3, 0:D]
    ctx_in = [core.sem(f"{name}_ctx_in{b}") for b in range(BT)]
    (ln_in, q_made, q_out, null_ready, scored, maxed, exped, scaled, turned, probT_done, lastT_done, mixed,
     mix_out, null_in, out_done, z_copied, z_done, z_used) = (core.sem(f"{name}_{n}") for n in (
         "ln_in", "q_made", "q_out", "null_ready", "scored", "maxed", "exped", "scaled", "turned", "probT_done",
         "lastT_done", "mixed", "mix_out", "null_in", "out_done", "z_copied", "z_done", "z_used"))
    block = st.enter_context(nc.Block())

    def q_bank(k):
        c, g = k // 4, k % 4
        return (q_ctx[:, c, :, 4 * g:4 * g + 4, :],
                core.psum[:, k, :].rearrange("p (h b n) -> p b h n", h=4, b=BT))

    @block.sync
    def _(sp):
        load(sp, [(ln_scale[:, :], dram[f"{name}_ln_scale"].to_broadcast([P, D])),
                  (ln_bias[:, :], dram[f"{name}_ln_bias"].to_broadcast([P, D]))], ln_in)
        with sp.Fori(0, TILES) as t:
            for b in range(BT):
                sp.wait_ge(mixed, t * UNITS + 2 * b + 2)
                seq = t * BT + b
                row = dram["ctx_2048"][ds(seq, 1), :, :].rearrange("a m c -> (a m) c")
                for dst, src in ((ctxT[:, b, :, :], dram["ctx_T"][ds(seq, 1), :, :].rearrange("a (k c) m -> c (a k) m", c=P)),
                                 (ctx[:, b, :, :], row[0:2 * P, :].rearrange("(k m) c -> m k c", m=P)),
                                 (ctx_last[:, b, :], row[2 * P:CTX, :])):
                    sp.dma_start(dst, src).then_inc(ctx_in[b], 16)

    @block.gpsimd
    def _(pool):
        nc.gpsimd.memset(z_eps[:, :], LN2_EPS)
        pool.drain()
        pool.wait_ge(ln_in, 32)
        with pool.Fori(0, TILES) as t:
            for b in range(BT):
                pool.wait_ge(scored, t * UNITS + 2 * b + 2)
                a = s_null[:, ds(t, 1), b * SEQ:(b + 1) * SEQ].to_broadcast([HEADS, HEADS, SEQ])
                m = core.c("ident")[0:HEADS, 0:HEADS].rearrange("p (h n) -> p h n", n=1).to_broadcast([HEADS, HEADS, SEQ])
                nc.gpsimd.tensor_tensor(null_bd[:, b % 2, :, :], a, m, ALU.mult).then_inc(null_ready, 1)
            pool.wait_ge(z_done, t + 1)
            nc.gpsimd.tensor_tensor(z_var[:, 0:1], z_mv[:, 1:2], z_eps[:, :], ALU.add)
            pool.drain()
            nc.gpsimd.tensor_tensor(z_var[:, 1:2], z_var[:, 0:1], core.half[:, :], ALU.pow)
            pool.drain()
            nc.gpsimd.tensor_scalar(z[:, :], z[:, :], z_mv[:, 0:1], z_var[:, 1:2], ALU.subtract, ALU.mult)
            pool.drain()
            nc.gpsimd.tensor_tensor(z[:, :], z[:, :], ln_scale[:, :], ALU.mult)
            pool.drain()
            nc.gpsimd.tensor_tensor(z[:, :], z[:, :], ln_bias[:, :], ALU.add)
            pool.drain()
            nc.gpsimd.tensor_tensor(core.x[:, ds(t, 1), :], core.x[:, ds(t, 1), :], z[:, :], ALU.add).then_inc(z_used, 1)

    @block.scalar
    def _(act):
        def exps(n, s):
            act.wait_ge(maxed, n + 1)
            for g in range(2):
                ins = nc.scalar.activation(prob[:, s, g, :], scores(s)[:, g, :], ACT.Exp,
                                           bias=nmax[:, s, g:g + 1], accum_out=total[:, s, g:g + 1])
            ins.then_inc(exped, 1)

        with act.Fori(0, TILES) as t:
            n = t * UNITS
            for k in range(0, 8, 2):
                act.wait_ge(q_made, t * 8 + k + 1)
                nc.scalar.copy(*q_bank(k)).then_inc(q_out, 1)
            exps(n, 0)
            for u in range(UNITS):
                b, s = u // 2, u % 2
                act.wait_ge(turned, n + u + 1)
                if u == 0:
                    act.wait_ge(null_in, t * 16 + 16)
                nc.scalar.copy(lastT[:, 8 * s:8 * s + 8, b * SEQ:(b + 1) * SEQ].rearrange("p (g h) n -> p g h n", g=2),
                               turned_last(s).rearrange("p g (h n) -> p g h n", h=G)).then_inc(lastT_done, 1)
                if u < UNITS - 1:
                    exps(n + u + 1, 1 - s)
                act.wait_ge(mixed, n + u + 1 + UNITS)
                nc.scalar.copy(mixed_ctx[:, :, 8 * s:8 * s + 8, b * SEQ:(b + 1) * SEQ],
                               mix_bank(s).rearrange("p (c h n) -> p c h n", c=2, h=8)).then_inc(mix_out, 1)
            act.drain()
            act.dma_start(nullT[:, :], lastT[1:2, :, :]).then_inc(null_in, 16)

    @block.vector
    def _(dve):
        def maxes(n, s):
            dve.wait_ge(scored, n + 4 + 1)
            nc.vector.tensor_reduce(nmax[:, s, :], scores(s), X, ALU.max, negate=True).then_inc(maxed, 1)

        def scales(n, s):
            dve.wait_ge(exped, n + 1)
            nc.vector.reciprocal(total[:, s, :], total[:, s, :])
            dve.drain()
            for g in range(2):
                ins = nc.vector.tensor_scalar(prob[:, s, g, :], prob[:, s, g, :], total[:, s, g:g + 1], None, ALU.mult)
            ins.then_inc(scaled, 1)

        with dve.Fori(0, TILES) as t:
            n = t * UNITS
            for k in range(1, 8, 2):
                dve.wait_ge(q_made, t * 8 + k + 1)
                nc.vector.tensor_copy(*q_bank(k)).then_inc(q_out, 1)
            maxes(n, 0)
            scales(n, 0)
            for u in range(UNITS):
                s = u % 2
                dve.wait_ge(turned, n + u + 1)
                nc.vector.tensor_copy(probT[:, s, :, :],
                                      turned_bank(s).rearrange("p (k w) -> p k w", k=2)).then_inc(probT_done, 1)
                if u < UNITS - 1:
                    maxes(n + u + 1, 1 - s)
                    scales(n + u + 1, 1 - s)
            dve.wait_ge(z_used, t + 1)
            dve.wait_ge(out_done, t + 1)
            nc.vector.tensor_copy(z[:, :], OUT).then_inc(z_copied, 1)
            dve.drain()
            nc.vector.bn_stats(z_stats[:, :], z[:, :])
            dve.drain()
            nc.vector.bn_aggr(z_mv[:, :], z_stats[:, :]).then_inc(z_done, 1)

    @block.tensor
    def _(pe):
        def score(t, u):
            b, s = u // 2, u % 2
            if s == 0:
                pe.wait_ge(ctx_in[b], (t + 1) * 16 * 3)
                pe.wait_ge(null_ready, t * BT + b + 1)
            for g in range(2):
                h = 8 * s + 4 * g
                for c in range(2):
                    nc.tensor.matmul(scores(s)[:, g, 0:CTX], q_ctx[:, c, b, h:h + 4, :].rearrange("p h n -> p (h n)"),
                                     ctxT[:, b, c, :], start=(c == 0), stop=(c == 1))
                last = nc.tensor.matmul(scores(s)[:, g, CTX:KEYS], null_bd[:, b % 2, h:h + 4, :].rearrange("p h n -> p (h n)"),
                                        core.ones[0:HEADS, 0:1], start=True, stop=True)
            last.then_inc(scored, 1)

        pe.sem_inc(mixed, UNITS)
        pe.sem_inc(scored, 4)
        pe.sem_inc(null_in, 16)
        pe.sem_inc(z_used, 1)
        pe.sem_inc(z_copied, 1)
        with pe.Fori(0, TILES) as t:
            n = t * UNITS
            for k in range(8):
                c, g = k // 4, k % 4
                if k == 3:
                    pe.wait_ge(z_copied, t + 1)
                for i in range(4):
                    last = nc.tensor.matmul(core.psum[:, k, i * P:(i + 1) * P], m_h[:, 4 * g + i, c * P:(c + 1) * P],
                                            xnT[:, ds(t, 1), :].rearrange("p a w -> p (a w)"), start=True, stop=True)
                last.then_inc(q_made, 1)
            pe.wait_ge(q_out, t * 8 + 8)
            score(t, 0)
            for u in range(UNITS):
                b, s = u // 2, u % 2
                pe.wait_ge(scaled, n + u + 1)
                for g in range(2):
                    for k in range(2):
                        nc.tensor.transpose(turned_bank(s)[:, k * 2 * P + g * P:k * 2 * P + (g + 1) * P],
                                            prob[:, s, g, k * P:(k + 1) * P], core.c("ident"))
                    last = nc.tensor.transpose(turned_last(s)[:, g, :], prob[:, s, g, 2 * P:KEYS], core.c("ident"))
                last.then_inc(turned, 1)
                if u < UNITS - 1:
                    score(t, u + 1)
                pe.wait_ge(probT_done, n + u + 1)
                pe.wait_ge(lastT_done, n + u + 1)
                for c in range(2):
                    dst = mix_bank(s)[:, c * 2 * P:(c + 1) * 2 * P]
                    for k in range(2):
                        nc.tensor.matmul(dst, ctx[:, b, k, c * P:(c + 1) * P], probT[:, s, k, :], start=(k == 0), stop=False)
                    last = nc.tensor.matmul(dst.rearrange("p (h n) -> p h n", n=SEQ), ctx_last[:, b, c * P:(c + 1) * P],
                                            lastT[0:1, 8 * s:8 * s + 8, b * SEQ:(b + 1) * SEQ], start=False, stop=True)
                last.then_inc(mixed, 1)
            pe.wait_ge(mix_out, n + UNITS)
            for c in range(2):
                for h in range(HEADS):
                    nc.tensor.matmul(OUT, mixed_ctx[:, c, h, :], u_h[:, c, h, :], start=(c + h == 0), stop=False)
            pe.wait_ge(null_in, t * 16 + 32)
            nc.tensor.matmul(OUT, nullT[:, :], v_null[:, :], start=False, stop=True).then_inc(out_done, 1)


def folded_attention(core, name):
    nc, dram = core.nc, core.dram
    S = 4
    CH = S * BT
    with ExitStack() as st:
        sb = lambda n, shape, dt=F32: st.enter_context(nc.sbuf_tensor(f"{name}_{n}", shape, dt))
        qkv_dram = nc.dram_tensor(f"{name}_qkv_scratch", (3, B, SEQ * D), F32).ap()
        out_dram = nc.dram_tensor(f"{name}_out_scratch", (B, SEQ * D), F32).ap()
        folded = lambda t: t.rearrange("b (r w) -> r b w", r=P)
        w = sb("w", [D, 3 * D])
        bias = sb("bias", [1, 3 * D])
        temp = sb("temp", [P, 1])
        head4 = sb("head4", [P, G])
        qkv = sb("qkv", [P, TILES, 3, D])
        rows = sb("rows", [P, 2, 3, CH, SEQ])
        k4 = sb("k4", [P, S, BT, G, SEQ])
        vbd = sb("vbd", [P, S, BT, G, SEQ])
        q4 = sb("q4", [P, S, BT, G, SEQ])
        qbd = sb("qbd", [P, S, BT * G, G, 8])
        prob = sb("prob", [P, S, HEADS, SEQ])
        top = sb("top", [P, S, HEADS])
        total = sb("total", [P, S, HEADS])
        res = sb("res", [P, B, SEQ])
        back = sb("back", [P, TILES, D])
        bank_a = lambda s: core.psum[:, 2 * s, :]
        bank_b = lambda s: core.psum[:, 2 * s + 1, :]
        front = Front(core, st, name, S, bank_a)
        (w_in, projected, qkv_done, stored, masked, scored, shifted, exped, normal, turned, qbd_done, mixed,
         res_done, res_stored, back_in, q4_done) = (core.sem(f"{name}_{n}") for n in (
             "w_in", "projected", "qkv_done", "stored", "masked", "scored", "shifted", "exped", "normal", "turned",
             "qbd_done", "mixed", "res_done", "res_stored", "back_in", "q4_done"))
        rows_in = [core.sem(f"{name}_rows_in{i}") for i in range(2)]

        with nc.Block() as block:
            @block.sync
            def _(sp):
                load(sp, [(w[:, :], dram[f"{name}_Wqkv"]), (bias[:, :], dram[f"{name}_bqkv"]),
                          (temp[:, :], dram[f"{name}_temp"])], w_in)
                with sp.Fori(0, TILES // S) as it:
                    sp.wait_ge(qkv_done, (it + 2) * S)
                    for f in range(3):
                        sp.dma_start(qkv_dram[f, ds(it * CH, CH), :].rearrange("(t b) (s d) -> (b s) t d", b=BT, d=D),
                                     qkv[:, ds(it * S, S), f, :]).then_inc(stored, 16)
                sp.wait_ge(stored, 16 * 3 * (TILES // S))

            @block.gpsimd
            def _(pool):
                with pool.Fori(0, TILES // S) as it:
                    front.pool_rstd(pool, it * S)

            @block.scalar
            def _(act):
                act.sem_inc(qkv_done, S)
                with act.Fori(0, TILES // S) as it:
                    n = it * S
                    front.act_copy(act, n)
                    for s in range(S):
                        act.wait_ge(projected, n + s + 1)
                        nc.scalar.copy(qkv[:, ds(n + s, 1), :, :].rearrange("p t f d -> p (t f d)"),
                                       bank_b(s)[:, 0:3 * D]).then_inc(qkv_done, 1)

            @block.vector
            def _(dve):
                dve.wait_ge(w_in, 48)
                nc.vector.tensor_scalar(head4[:, :], core.c("head4"), temp[:, :], None, ALU.mult)
                with dve.Fori(0, TILES // S) as it:
                    n = it * S
                    front.dve_moments(dve, n)
                    dve.wait_ge(qkv_done, n + S)
                    front.dve_normalise(dve, n)

            @block.tensor
            def _(pe):
                pe.wait_ge(w_in, 48)
                with pe.Fori(0, TILES // S) as it:
                    n = it * S
                    front.pe_transpose(pe, n)
                    for s in range(S):
                        pe.wait_ge(front.xnT_done, n + s + 1)
                        nc.tensor.matmul(bank_b(s)[:, 0:3 * D], front.xnT[:, s, :], w[:, :], start=True, stop=False)
                        nc.tensor.matmul(bank_b(s)[:, 0:3 * D], core.ones[0:1, :], bias[:, :], start=False,
                                         stop=True).then_inc(projected, 1)

        block = st.enter_context(nc.Block())

        @block.sync
        def _(sp):
            def load_rows(step, half):
                for f in range(3):
                    sp.dma_start(rows[:, half, f, :, :], folded(qkv_dram[f, ds(step * CH, CH), :])).then_inc(
                        rows_in[half], 16)

            def step_out(step):
                sp.wait_ge(res_done, (step + 2) * S)
                sp.dma_start(folded(out_dram[ds(step * CH, CH), :]), res[:, ds(step * CH, CH), :]).then_inc(
                    res_stored, 16)

            load_rows(0, 0)
            load_rows(1, 1)
            with sp.Fori(0, TILES // S // 2 - 1) as pair:
                for half in range(2):
                    step_out(pair * 2 + half)
                    load_rows(pair * 2 + half + 2, half)
            step_out(TILES // S - 2)
            step_out(TILES // S - 1)
            sp.wait_ge(res_stored, 16 * (TILES // S))
            sp.dma_start(back[:, :, :], out_dram.rearrange("(t b) (s d) -> (b s) t d", b=BT, d=D)).then_inc(back_in, 16)

        @block.gpsimd
        def _(pool):
            with pool.Fori(0, TILES // S // 2) as pair:
                for half in range(2):
                    n = (pair * 2 + half) * S
                    for s in range(S):
                        if s == 0:
                            pool.wait_ge(rows_in[half], (pair + 1) * 48)
                        pool.wait_ge(mixed, n + s + 1)
                        here = slice(s * BT, (s + 1) * BT)
                        a, m = spread(rows[:, half, 1, here, :], head4[:, :], SEQ)
                        nc.gpsimd.tensor_tensor(k4[:, s, :, :, :], a, m, ALU.mult)
                        a, m = spread(rows[:, half, 2, here, :], core.c("group"), SEQ)
                        nc.gpsimd.tensor_tensor(vbd[:, s, :, :, :], a, m, ALU.mult).then_inc(masked, 1)

        @block.scalar
        def _(act):
            act.sem_inc(res_done, S)
            with act.Fori(0, TILES // S // 2) as pair:
                for half in range(2):
                    n = (pair * 2 + half) * S
                    for s in range(S):
                        act.wait_ge(masked, n + s + 1)
                        q = rows[:, half, 0, s * BT:(s + 1) * BT, :].rearrange("p b (a w) -> p b a w", a=1)
                        nc.scalar.copy(q4[:, s, :, :, :], q.to_broadcast([P, BT, G, SEQ])).then_inc(q4_done, 1)
                    for s in range(S):
                        act.wait_ge(shifted, n + s + 1)
                        nc.scalar.activation(prob[:, s, :, :], prob[:, s, :, :], ACT.Exp).then_inc(exped, 1)
                    for s in range(S):
                        act.wait_ge(mixed, n + s + 1 + S)
                        nc.scalar.copy(res[:, ds((n + s) * BT, BT), :],
                                       bank_b(s)[:, 0:P].rearrange("p (b w) -> p b w", b=BT)).then_inc(res_done, 1)

        @block.vector
        def _(dve):
            mask = core.c("group").rearrange("p (a j w) -> p a j w", a=1, w=1).to_broadcast([P, BT * G, G, 8])
            with dve.Fori(0, TILES // S) as it:
                n = it * S
                for s in range(S):
                    dve.wait_ge(turned, n + s + 1)
                    nc.vector.tensor_tensor(qbd[:, s, :, :, :],
                                            bank_a(s).rearrange("p (a j w) -> p a j w", j=G, w=8), mask,
                                            ALU.mult).then_inc(qbd_done, 1)
                for s in range(S):
                    dve.wait_ge(scored, n + s + 1)
                    nc.vector.tensor_reduce(top[:, s, :], bank_b(s).rearrange("p (a w) -> p a w", w=SEQ), X, ALU.max)
                dve.drain()
                for s in range(S):
                    nc.vector.tensor_tensor(prob[:, s, :, :], bank_b(s).rearrange("p (a w) -> p a w", w=SEQ),
                                            per_row(top[:, s, :]), ALU.subtract).then_inc(shifted, 1)
                for s in range(S):
                    dve.wait_ge(exped, n + s + 1)
                    nc.vector.tensor_reduce(total[:, s, :], prob[:, s, :, :], X, ALU.add)
                dve.drain()
                for s in range(S):
                    nc.vector.reciprocal(total[:, s, :], total[:, s, :])
                dve.drain()
                for s in range(S):
                    nc.vector.tensor_tensor(prob[:, s, :, :], prob[:, s, :, :], per_row(total[:, s, :]),
                                            ALU.mult).then_inc(normal, 1)
            dve.wait_ge(back_in, 16)
            nc.vector.tensor_tensor(core.x[:, :, :], core.x[:, :, :], back[:, :, :], ALU.add)

        @block.tensor
        def _(pe):
            pe.sem_inc(mixed, S)
            with pe.Fori(0, TILES // S) as it:
                n = it * S
                for s in range(S):
                    pe.wait_ge(q4_done, n + s + 1)
                    for b in range(BT):
                        last = nc.tensor.transpose(bank_a(s)[:, b * P:(b + 1) * P],
                                                   q4[:, s, b, :, :].rearrange("p j w -> p (j w)"), core.c("ident"))
                    last.then_inc(turned, 1)
                for s in range(S):
                    pe.wait_ge(masked, n + s + 1)
                    pe.wait_ge(res_done, n + s + 1)
                    for b in range(BT):
                        last = nc.tensor.matmul(bank_b(s)[:, b * P:(b + 1) * P],
                                                k4[:, s, b, :, :].rearrange("p j w -> p (j w)"),
                                                vbd[:, s, b, :, :].rearrange("p j w -> p (j w)"), start=True, stop=True)
                    last.then_inc(scored, 1)
                for s in range(S):
                    pe.wait_ge(normal, n + s + 1)
                    pe.wait_ge(qbd_done, n + s + 1)
                    for b in range(BT):
                        for g in range(G):
                            last = nc.tensor.matmul(bank_b(s)[g * 32:(g + 1) * 32, b * 32:(b + 1) * 32],
                                                    qbd[:, s, b * G + g, :, :].rearrange("p j w -> p (j w)"),
                                                    prob[:, s, b * G + g, :], start=True, stop=True)
                    last.then_inc(mixed, 1)


def quantised_ffn(core, name):
    nc, dram = core.nc, core.dram
    S, H = 4, 512
    C = H // P
    ROUND = 1.5 * 2.0 ** 23
    with ExitStack() as st:
        sb = lambda n, shape, dt=F32: st.enter_context(nc.sbuf_tensor(f"{name}_{n}", shape, dt))
        w1 = sb("w1", [D, H])
        w2 = sb("w2", [P, C, D])
        w1q = sb("w1q", [D, H], BF16)
        w2q = sb("w2q", [P, C, D], BF16)
        b1 = sb("b1", [1, H])
        b2 = sb("b2", [1, D])
        xn = sb("xn_all", [P, TILES, D])
        h = sb("h", [P, TILES, H])
        peak_x = sb("peak_x", [P, TILES])
        peak_h = sb("peak_h", [P, TILES])
        peaks = sb("peaks", [P, 4])
        most = sb("most", [P, 4])
        inv = sb("inv", [P, 4])
        scale = sb("scale", [P, 2])
        q = sb("q", [P, S, H])
        qT = sb("qT", [P, S, C, P], BF16)
        bank_a = lambda s: core.psum[:, 2 * s, :]
        bank_b = lambda s: core.psum[:, 2 * s + 1, :]
        front = Front(core, st, name, S, bank_a, transposed=False)
        (w_in, peaks_x, most_x, x_rounded, turned, qT_done, wide, gelued, peaks_h, most_h, h_rounded, turned2,
         hT_done, out_done) = (core.sem(f"{name}_{n}") for n in (
             "w_in", "peaks_x", "most_x", "x_rounded", "turned", "qT_done", "wide", "gelued", "peaks_h", "most_h",
             "h_rounded", "turned2", "hT_done", "out_done"))
        block = st.enter_context(nc.Block())

        @block.sync
        def _(sp):
            load(sp, [(w1[:, :], dram[f"{name}_w1_T"]), (w2[:, :, :], dram[f"{name}_w2_T"]),
                      (b1[:, :], dram[f"{name}_b1"]), (b2[:, :], dram[f"{name}_b2"])], w_in)

        @block.gpsimd
        def _(pool):
            with pool.Fori(0, TILES // S) as it:
                front.pool_rstd(pool, it * S)
            pool.wait_ge(peaks_x, 1)
            nc.gpsimd.partition_all_reduce(most[:, 0:3], peaks[:, 0:3], P,
                                           bass.bass_isa.ReduceOp.max).then_inc(most_x, 1)
            pool.wait_ge(peaks_h, 1)
            nc.gpsimd.partition_all_reduce(most[:, 3:4], peaks[:, 3:4], P,
                                           bass.bass_isa.ReduceOp.max).then_inc(most_h, 1)

        @block.scalar
        def _(act):
            with act.Fori(0, TILES // S) as it:
                n = it * S
                for s in range(S):
                    act.wait_ge(turned, n + s + 1)
                    nc.scalar.copy(qT[:, s, 0, :], bank_a(s)[:, 0:P]).then_inc(qT_done, 1)
                for s in range(S):
                    act.wait_ge(wide, n + s + 1)
                    nc.scalar.activation(h[:, ds(n + s, 1), :], bank_b(s), ACT.Gelu,
                                         scale=scale[:, 0:1]).then_inc(gelued, 1)
            with act.Fori(0, TILES // S) as it:
                n = it * S
                for s in range(S):
                    act.wait_ge(turned2, n + s + 1)
                    nc.scalar.copy(qT[:, s, :, :], bank_a(s).rearrange("p (c w) -> p c w", c=C)).then_inc(hT_done, 1)

        @block.vector
        def _(dve):
            def steps_of(i, j):
                m = most[:, i:j]
                nc.vector.tensor_scalar(m, m, 1e-6, 1.0 / 127.0, ALU.max, ALU.mult)
                dve.drain()
                nc.vector.reciprocal(inv[:, i:j], m)
                dve.drain()

            def rounded(dst, src, col, tmp):
                nc.vector.tensor_scalar(tmp, src, inv[:, col:col + 1], ROUND, ALU.mult, ALU.add)
                dve.drain()
                return nc.vector.tensor_scalar(dst, tmp, ROUND, None, ALU.subtract)

            with dve.Fori(0, TILES // S) as it:
                n = it * S
                front.dve_moments(dve, n)
                for s in range(S):
                    dve.wait_ge(front.rstd_done, n + s + 1)
                    nc.vector.tensor_scalar(xn[:, ds(n + s, 1), :], core.x[:, ds(n + s, 1), :], front.mv[:, s, 0:1],
                                            front.rstd[:, s, :], ALU.subtract, ALU.mult)
            dve.drain()
            nc.vector.tensor_reduce(peaks[:, 0:1], xn[:, :, :], XY, ALU.max, apply_absolute_value=True)
            dve.wait_ge(w_in, 64)
            nc.vector.tensor_reduce(peaks[:, 1:2], w1[:, :], X, ALU.max, apply_absolute_value=True)
            nc.vector.tensor_reduce(peaks[:, 2:3], w2[:, :, :], XY, ALU.max,
                                    apply_absolute_value=True).then_inc(peaks_x, 1)
            dve.wait_ge(most_x, 1)
            steps_of(0, 3)
            nc.vector.tensor_tensor(scale[:, 0:1], most[:, 0:1], most[:, 1:2], ALU.mult)
            rounded(w1q[:, :], w1[:, :], 1, q[:, 0, :])
            rounded(w2q[:, :, :].rearrange("p c d -> p (c d)"), w2[:, :, :].rearrange("p c d -> p (c d)"), 2, q[:, 1, :])
            with dve.Fori(0, TILES // S) as it:
                n = it * S
                dve.drain()
                for s in range(S):
                    nc.vector.tensor_scalar(xn[:, ds(n + s, 1), :], xn[:, ds(n + s, 1), :], inv[:, 0:1], ROUND,
                                            ALU.mult, ALU.add)
                dve.drain()
                for s in range(S):
                    nc.vector.tensor_scalar(q[:, s, 0:D], xn[:, ds(n + s, 1), :], ROUND, None,
                                            ALU.subtract).then_inc(x_rounded, 1)
                for s in range(S):
                    dve.wait_ge(gelued, n + s + 1)
                    nc.vector.tensor_reduce(peak_h[:, ds(n + s, 1)], h[:, ds(n + s, 1), :], XY, ALU.max,
                                            apply_absolute_value=True)
            dve.drain()
            nc.vector.tensor_reduce(peaks[:, 3:4], peak_h[:, :], X, ALU.max).then_inc(peaks_h, 1)
            dve.wait_ge(most_h, 1)
            steps_of(3, 4)
            nc.vector.tensor_tensor(scale[:, 1:2], most[:, 2:3], most[:, 3:4], ALU.mult)
            with dve.Fori(0, TILES // S) as it:
                n = it * S
                dve.drain()
                for s in range(S):
                    nc.vector.tensor_scalar(h[:, ds(n + s, 1), :], h[:, ds(n + s, 1), :], inv[:, 3:4], ROUND,
                                            ALU.mult, ALU.add)
                dve.drain()
                for s in range(S):
                    nc.vector.tensor_scalar(q[:, s, :], h[:, ds(n + s, 1), :], ROUND, None,
                                            ALU.subtract).then_inc(h_rounded, 1)
                for s in range(S):
                    dve.wait_ge(out_done, n + s + 1)
                    nc.vector.scalar_tensor_tensor(core.x[:, ds(n + s, 1), :], bank_b(s)[:, 0:D], scale[:, 1:2],
                                                   core.x[:, ds(n + s, 1), :], ALU.mult, ALU.add)

        @block.tensor
        def _(pe):
            pe.wait_ge(w_in, 64)
            with pe.Fori(0, TILES // S) as it:
                n = it * S
                for s in range(S):
                    pe.wait_ge(x_rounded, n + s + 1)
                    nc.tensor.transpose(bank_a(s)[:, 0:P], q[:, s, 0:D], core.c("ident")).then_inc(turned, 1)
                for s in range(S):
                    pe.wait_ge(qT_done, n + s + 1)
                    nc.tensor.matmul(bank_b(s), qT[:, s, 0, :], w1q[:, :], start=True, stop=False)
                    nc.tensor.matmul(bank_b(s), core.ones[0:1, :], b1[:, :], start=False, stop=True).then_inc(wide, 1)
            with pe.Fori(0, TILES // S) as it:
                n = it * S
                for s in range(S):
                    pe.wait_ge(h_rounded, n + s + 1)
                    for c in range(C):
                        last = nc.tensor.transpose(bank_a(s)[:, c * P:(c + 1) * P], q[:, s, c * P:(c + 1) * P],
                                                   core.c("ident"))
                    last.then_inc(turned2, 1)
                for s in range(S):
                    pe.wait_ge(hT_done, n + s + 1)
                    for c in range(C):
                        nc.tensor.matmul(bank_b(s)[:, 0:D], qT[:, s, c, :], w2q[:, c, :], start=(c == 0), stop=False)
                    nc.tensor.matmul(bank_b(s)[:, 0:D], core.ones[0:1, :], b2[:, :], start=False,
                                     stop=True).then_inc(out_done, 1)


def min_gru(core, name):
    nc, dram = core.nc, core.dram
    S, U = 8, 2
    N = S // U * P
    with ExitStack() as st:
        sb = lambda n, shape, dt=F32: st.enter_context(nc.sbuf_tensor(f"{name}_{n}", shape, dt))
        w = sb("w", [D, 3])
        neg = sb("neg", [D, 3])
        soft = sb("soft", [P, U, 2, N])
        relu = sb("relu", [P, U, 2, N])
        diff = sb("diff", [P, U, N])
        f_gate = sb("f_gate", [P, U, N])
        i_gate = sb("i_gate", [P, U, N])
        hid = sb("hid", [P, U, N])
        grown = sb("grown", [P, U, N])
        state = sb("state", [P, U, N])
        bank = lambda s: core.psum[:, s // 4, s % 4 * P:s % 4 * P + P]
        front = Front(core, st, name, S, bank, pack=4)
        unit = lambda u: front.xnT[:, u * 4:u * 4 + 4, :].rearrange("p s w -> p (s w)")
        (w_in, signed, softs, diffs, gates, states, out_done) = (core.sem(f"{name}_{n}") for n in (
            "w_in", "signed", "softs", "diffs", "gates", "states", "out_done"))
        block = st.enter_context(nc.Block())

        @block.sync
        def _(sp):
            load(sp, [(w[:, :], dram[f"{name}_W"])], w_in)

        @block.gpsimd
        def _(pool):
            with pool.Fori(0, TILES // S) as it:
                front.pool_rstd(pool, it * S)

        @block.scalar
        def _(act):
            act.wait_ge(w_in, 16)
            with act.Fori(0, TILES // S) as it:
                front.act_copy(act, it * S)
                n = it * U
                act.drain()
                for u in range(U):
                    for k in range(2):
                        nc.scalar.activation(soft[:, u, k, :], unit(u), ACT.Abs, scale=w[:, k:k + 1])
                act.drain()
                for u in range(U):
                    nc.scalar.activation(soft[:, u, :, :], soft[:, u, :, :], ACT.Exp, scale=-1.0)
                act.drain()
                for u in range(U):
                    nc.scalar.activation(soft[:, u, :, :], soft[:, u, :, :], ACT.Ln, bias=1.0).then_inc(softs, 1)
                for u in range(U):
                    nc.scalar.activation(hid[:, u, :], unit(u), ACT.Sigmoid, scale=w[:, 2:3])
                    act.wait_ge(diffs, n + u + 1)
                    nc.scalar.activation(f_gate[:, u, :], diff[:, u, :], ACT.Sigmoid, scale=-1.0)
                    nc.scalar.activation(i_gate[:, u, :], diff[:, u, :], ACT.Sigmoid).then_inc(gates, 1)

        @block.vector
        def _(dve):
            dve.wait_ge(w_in, 16)
            nc.vector.tensor_scalar(neg[:, :], w[:, :], -1.0, None, ALU.mult)
            with dve.Fori(0, TILES // S) as it:
                front.dve_moments(dve, it * S)
                front.dve_normalise(dve, it * S)
                n = it * U
                for u in range(U):
                    dve.wait_ge(front.xnT_done, it * S + 4 * u + 4)
                    for k in range(2):
                        nc.vector.tensor_scalar(relu[:, u, k, :], unit(u), neg[:, k:k + 1], 0.0, ALU.mult, ALU.max)
                    nc.vector.tensor_scalar(grown[:, u, :], unit(u), w[:, 2:3], 0.5 + 1e-8, ALU.mult, ALU.add)
                dve.drain()
                for u in range(U):
                    dve.wait_ge(softs, n + u + 1)
                    nc.vector.tensor_tensor(soft[:, u, :, :], soft[:, u, :, :], relu[:, u, :, :], ALU.add)
                dve.drain()
                for u in range(U):
                    nc.vector.tensor_tensor(diff[:, u, :], soft[:, u, 0, :], soft[:, u, 1, :],
                                            ALU.subtract).then_inc(diffs, 1)
                for u in range(U):
                    dve.wait_ge(gates, n + u + 1)
                    nc.vector.tensor_tensor(grown[:, u, :], grown[:, u, :], hid[:, u, :], ALU.max)
                    nc.vector.memset(f_gate[:, u, :].rearrange("p (b t) -> p b t", t=SEQ)[:, :, 0:1], 0.0)
                dve.drain()
                for u in range(U):
                    nc.vector.tensor_tensor(grown[:, u, :], grown[:, u, :], i_gate[:, u, :], ALU.mult)
                dve.drain()
                for u in range(U):
                    nc.vector.tensor_tensor_scan(state[:, u, :], f_gate[:, u, :], grown[:, u, :], 0.0, ALU.mult,
                                                 ALU.add).then_inc(states, 1)
                for u in range(U):
                    dve.wait_ge(out_done, n + u + 1)
                    x = core.x[:, ds(it * S + 4 * u, 4), :]
                    nc.vector.tensor_tensor(x, x, core.psum[:, 4 + u, :].rearrange("p (t w) -> p t w", w=D), ALU.add)

        @block.tensor
        def _(pe):
            with pe.Fori(0, TILES // S) as it:
                front.pe_transpose(pe, it * S)
                for u in range(U):
                    pe.wait_ge(states, it * U + u + 1)
                    for t in range(4):
                        last = nc.tensor.transpose(core.psum[:, 4 + u, t * P:(t + 1) * P],
                                                   state[:, u, t * P:(t + 1) * P], core.c("ident"))
                    last.then_inc(out_done, 1)


def lora_experts(core, name):
    nc, dram = core.nc, core.dram
    S, E, R = 4, 8, 4
    with ExitStack() as st:
        sb = lambda n, shape, dt=F32: st.enter_context(nc.sbuf_tensor(f"{name}_{n}", shape, dt))
        w = sb("w", [D, D])
        w_gate = sb("w_gate", [D, E + E * R])
        right = sb("right", [E * R, D])
        b_lin = sb("b_lin", [1, D])
        gate = sb("gate", [P, S, E])
        best = sb("best", [P, S, E])
        index = sb("index", [P, S, E], U32)
        index_f = sb("index_f", [P, S, E])
        chosen = sb("chosen", [P, S, 2, E])
        total = sb("total", [P, S, 1])
        narrow = sb("narrow", [P, S, E, R])
        narrowT = sb("narrowT", [E * R, S, P])
        bank_a = lambda s: core.psum[:, 2 * s, :]
        bank_b = lambda s: core.psum[:, 2 * s + 1, :]
        front = Front(core, st, name, S, bank_a)
        (w_in, gated, shifted, exped, weighted, turned, narrowT_done, out_done) = (core.sem(f"{name}_{n}") for n in (
            "w_in", "gated", "shifted", "exped", "weighted", "turned", "narrowT_done", "out_done"))
        block = st.enter_context(nc.Block())

        @block.sync
        def _(sp):
            load(sp, [(w[:, :], dram[f"{name}_W_lin_T"]), (w_gate[:, :], dram[f"{name}_gate_left"]),
                      (right[:, :], dram[f"{name}_right"]), (b_lin[:, :], dram[f"{name}_b_lin"])], w_in)

        @block.gpsimd
        def _(pool):
            with pool.Fori(0, TILES // S) as it:
                front.pool_rstd(pool, it * S)

        @block.scalar
        def _(act):
            with act.Fori(0, TILES // S) as it:
                n = it * S
                front.act_copy(act, n)
                for s in range(S):
                    act.wait_ge(shifted, n + s + 1)
                    nc.scalar.activation(gate[:, s, :], gate[:, s, :], ACT.Exp,
                                         accum_out=total[:, s, :]).then_inc(exped, 1)
                for s in range(S):
                    act.wait_ge(turned, n + s + 1)
                    nc.scalar.copy(narrowT[:, s, :], bank_a(s)[0:E * R, 0:P]).then_inc(narrowT_done, 1)

        @block.vector
        def _(dve):
            with dve.Fori(0, TILES // S) as it:
                n = it * S
                front.dve_moments(dve, n)
                front.dve_normalise(dve, n)
                for s in range(S):
                    dve.wait_ge(gated, n + s + 1)
                    nc.vector.tensor_copy(gate[:, s, :], bank_a(s)[:, P:P + E])
                dve.drain()
                for s in range(S):
                    nc.vector.max(best[:, s, :], gate[:, s, :])
                dve.drain()
                for s in range(S):
                    nc.vector.max_index(index[:, s, :], best[:, s, :], gate[:, s, :])
                dve.drain()
                nc.vector.tensor_copy(index_f[:, :, :], index[:, :, :])
                for s in range(S):
                    nc.vector.tensor_scalar(gate[:, s, :], gate[:, s, :], best[:, s, 0:1], None,
                                            ALU.subtract).then_inc(shifted, 1)
                dve.drain()
                for s in range(S):
                    for k in range(2):
                        nc.vector.tensor_scalar(chosen[:, s, k, :], core.c("iota8"), index_f[:, s, k:k + 1], None,
                                                ALU.is_equal)
                dve.drain()
                nc.vector.tensor_tensor(chosen[:, :, 0, :], chosen[:, :, 0, :], chosen[:, :, 1, :], ALU.add)
                dve.drain()
                for s in range(S):
                    dve.wait_ge(exped, n + s + 1)
                    nc.vector.reciprocal(total[:, s, :], total[:, s, :])
                dve.drain()
                for s in range(S):
                    nc.vector.scalar_tensor_tensor(gate[:, s, :], gate[:, s, :], total[:, s, :], chosen[:, s, 0, :],
                                                   ALU.mult, ALU.mult)
                dve.drain()
                for s in range(S):
                    weight = gate[:, s, :].rearrange("p (e r) -> p e r", r=1).to_broadcast([P, E, R])
                    nc.vector.tensor_tensor(narrow[:, s, :, :],
                                            bank_a(s)[:, P + E:P + E + E * R].rearrange("p (e r) -> p e r", r=R),
                                            weight, ALU.mult).then_inc(weighted, 1)
                for s in range(S):
                    dve.wait_ge(out_done, n + s + 1)
                    add_to_x(core, n + s, bank_b(s)[:, 0:D])

        @block.tensor
        def _(pe):
            pe.wait_ge(w_in, 64)
            with pe.Fori(0, TILES // S) as it:
                n = it * S
                front.pe_transpose(pe, n)
                for s in range(S):
                    pe.wait_ge(front.xnT_done, n + s + 1)
                    nc.tensor.matmul(bank_a(s)[:, P:P + E + E * R], front.xnT[:, s, :], w_gate[:, :], start=True,
                                     stop=True).then_inc(gated, 1)
                for s in range(S):
                    pe.wait_ge(weighted, n + s + 1)
                    nc.tensor.transpose(bank_a(s)[0:E * R, 0:P],
                                        narrow[:, s, :, :].rearrange("p e r -> p (e r)"),
                                        core.c("ident")).then_inc(turned, 1)
                for s in range(S):
                    out = bank_b(s)[:, 0:D]
                    nc.tensor.matmul(out, front.xnT[:, s, :], w[:, :], start=True, stop=False)
                    nc.tensor.matmul(out, core.ones[0:1, :], b_lin[:, :], start=False, stop=False)
                    pe.wait_ge(narrowT_done, n + s + 1)
                    nc.tensor.matmul(out, narrowT[:, s, :], right[:, :], start=False, stop=True).then_inc(out_done, 1)


def finish(core):
    nc = core.nc
    stored = core.sem("stored")
    with nc.Block() as block:
        @block.sync
        def _(sp):
            sp.dma_start(core.dram["out"].rearrange("(t p) d -> p t d", p=P), core.x[:, :, :]).then_inc(stored, 16)
            sp.wait_ge(stored, 16)


def program(nc, dram):
    with ExitStack() as ctx:
        core = Core(nc, dram, ctx)
        start(core)
        for stage in (
            lambda: depool_cross(core, "L0_xattn"),
            lambda: rotary_attention(core, "L0_attn"),
            lambda: product_key_experts(core, "L0_ffn"),
            lambda: context_attention(core, "L1_xattn"),
            lambda: gated_scan(core, "L1_attn"),
            lambda: ternary_ffn(core, "L1_ffn"),
            core.clear_sems,
            lambda: wide_context_attention(core, "L2_xattn"),
            lambda: folded_attention(core, "L2_attn"),
            lambda: quantised_ffn(core, "L2_ffn"),
            lambda: depool_cross(core, "L3_xattn"),
            lambda: min_gru(core, "L3_attn"),
            lambda: lora_experts(core, "L3_ffn"),
        ):
            stage()
        finish(core)


def layouts(v):
    a = {"constants": constants(), "x": v["x"].reshape(B * SEQ, D), "ctx_2048": v["ctx_2048"],
         "mask_BxS2_if0": v["mask_BxS2_if0"]}
    for n in ("L0_xattn", "L3_xattn"):
        a[f"{n}_W_in_T"] = v[f"{n}_W_in"].T
        a[f"{n}_g_res"] = v[f"{n}_g_res"].reshape(D, 1)
        a[f"{n}_b_in"] = v[f"{n}_b_in"].reshape(1, D)
        a[f"{n}_g_init"] = v[f"{n}_g_init"].reshape(1, CD)
    pair = np.arange(D) ^ 1
    wk = np.repeat(v["L0_attn_Wk"].reshape(D, G, 1, 8), G, axis=2).reshape(D, D)
    wq = v["L0_attn_Wq"]
    a["L0_attn_Wqk"] = np.stack([wq, wq[:, pair], wk, wk[:, pair]], axis=1)
    a["L0_attn_Wv"] = v["L0_attn_Wv"]
    a["L0_attn_Wo"] = v["L0_attn_Wo"].reshape(G, G, 8, D).transpose(1, 0, 2, 3).reshape(D, D)
    a["L0_ffn_w_q"] = v["L0_ffn_w_q"]
    a["L0_ffn_w_q_T"] = v["L0_ffn_w_q"].T.reshape(16, P, D).transpose(1, 0, 2)
    a["L0_ffn_keys"] = v["L0_ffn_keys"].transpose(3, 2, 0, 1).reshape(P, 16, 32)
    a["L0_ffn_gamma"] = v["L0_ffn_bn_gamma"].reshape(16, P).T
    a["L0_ffn_beta"] = v["L0_ffn_bn_beta"].reshape(16, P).T
    a["L0_ffn_down_T"] = v["L0_ffn_down_embed"].T
    a["L0_ffn_up"] = v["L0_ffn_up_embed"].reshape(8, P, D).transpose(1, 0, 2)
    a["ctx_T"] = v["ctx_2048"].transpose(0, 2, 1)
    a["L1_xattn_w_qkv_T"] = v["L1_xattn_w_qkv"].T
    a["L1_xattn_w_proj_T"] = v["L1_xattn_w_proj"].T
    a["L1_xattn_b_proj"] = v["L1_xattn_b_proj"].reshape(1, D)
    halves = lambda t: t.reshape(2, P, -1).transpose(1, 0, 2)
    a["L1_attn_W_in"] = v["L1_attn_W_in"].reshape(D, 4, P)
    a["L1_attn_W_x"] = halves(v["L1_attn_W_x"])
    a["L1_attn_W_dt"] = v["L1_attn_W_dt"].reshape(16, 2, P)
    a["L1_attn_W_Bp"] = v["L1_attn_W_Bp"].reshape(16, 2, P)
    a["L1_attn_W_out"] = halves(v["L1_attn_W_out"])
    a["L1_attn_conv_w"] = halves(v["L1_attn_conv_w"].reshape(2 * P, 4))
    a["L1_attn_b_dt"] = v["L1_attn_b_dt"].reshape(2, P).T
    a["L1_attn_D_param"] = v["L1_attn_D_param"].reshape(2, P).T
    a["L1_ffn_W_fc_T"] = v["L1_ffn_W_fc"].T
    a["L1_ffn_W_proj_T"] = v["L1_ffn_W_proj"].T.reshape(4, P, D).transpose(1, 0, 2)
    a["L1_ffn_ln_w"] = v["L1_ffn_ln_w"].reshape(4, P).T
    a["L1_ffn_ln_b"] = v["L1_ffn_ln_b"].reshape(4, P).T
    F = 64
    heads = lambda w: w.reshape(-1, HEADS, F).transpose(2, 1, 0)
    a["L2_xattn_WqT"] = heads(v["L2_xattn_Wq"])
    a["L2_xattn_WkT"] = heads(v["L2_xattn_Wkv"][:, 0:HEADS * F])
    a["L2_xattn_WvT"] = heads(v["L2_xattn_Wkv"][:, HEADS * F:])
    a["L2_xattn_Wo"] = v["L2_xattn_Wout"].reshape(HEADS, F, D).transpose(1, 0, 2)
    a["L2_xattn_null_kv_T"] = v["L2_xattn_null_kv"].T
    a["L2_xattn_ln_scale"] = v["L2_xattn_ln_scale"].reshape(1, D)
    a["L2_xattn_ln_bias"] = v["L2_xattn_ln_bias"].reshape(1, D)
    a["L2_attn_Wqkv"] = np.concatenate([v[f"L2_attn_W{f}"] for f in "qkv"], axis=1)
    a["L2_attn_bqkv"] = np.concatenate([v[f"L2_attn_b{f}"] for f in "qkv"]).reshape(1, 3 * D)
    a["L2_attn_temp"] = np.repeat(v["L2_attn_temperature"].reshape(HEADS), 8).reshape(P, 1)
    a["L2_ffn_w1_T"] = v["L2_ffn_w1"].T
    a["L2_ffn_w2_T"] = v["L2_ffn_w2"].T.reshape(4, P, D).transpose(1, 0, 2)
    a["L2_ffn_b1"] = v["L2_ffn_b1"].reshape(1, -1)
    a["L2_ffn_b2"] = v["L2_ffn_b2"].reshape(1, -1)
    a["L3_attn_W"] = np.stack([v[f"L3_attn_W{f}"].reshape(D) for f in "fih"], axis=1)
    a["L3_ffn_W_lin_T"] = v["L3_ffn_W_lin"].T
    a["L3_ffn_gate_left"] = np.concatenate(
        [v["L3_ffn_gate_w"].T, v["L3_ffn_left"].transpose(1, 0, 2).reshape(D, -1)], axis=1)
    a["L3_ffn_right"] = v["L3_ffn_right"].reshape(-1, D)
    a["L3_ffn_b_lin"] = v["L3_ffn_b_lin"].reshape(1, D)
    return {k: np.ascontiguousarray(t) for k, t in a.items()}


def kernel(**inputs):
    import concourse.bacc as bacc
    from concourse.bass_utils import run_bass_kernel_spmd

    arrays = layouts({k: np.asarray(v) for k, v in inputs.items()})
    nc = bacc.Bacc("TRN2", target_bir_lowering=False, num_devices=1)
    dram = {k: nc.dram_tensor(f"{k}_dram", a.shape, mybir.dt.from_np(a.dtype), kind="ExternalInput").ap()
            for k, a in arrays.items()}
    dram["out"] = nc.dram_tensor("out_dram", (B * SEQ, D), F32, kind="ExternalOutput").ap()
    program(nc, dram)
    got = run_bass_kernel_spmd(nc, [{f"{k}_dram": a for k, a in arrays.items()}], core_ids=[0])
    return got.results[0]["out_dram"].reshape(B, SEQ, D)
```

```python
from contextlib import ExitStack

import concourse.bass as bass
import numpy as np
from concourse import mybir

F32 = mybir.dt.float32
BF16 = mybir.dt.bfloat16
I32 = mybir.dt.int32
U32 = mybir.dt.uint32
ALU = mybir.AluOpType
ACT = mybir.ActivationFunctionType
X = mybir.AxisListType.X
XY = mybir.AxisListType.XY
ds = bass.ds

B, SEQ, D = 128, 32, 128
CTX, CD = 257, 256
P = 128
BT = P // SEQ
TILES = B * SEQ // P
HEADS = 16
G = 4
LN_EPS = 1e-5

CONST_WIDTHS = dict(ident=P, group=G, head4=G, head=HEADS, sel=SEQ, band=SEQ, rope=4 * SEQ, decay=P, iota8=8)
CONST_AT = {}
for _name, _w in CONST_WIDTHS.items():
    CONST_AT[_name] = sum(CONST_WIDTHS[k] for k in list(CONST_WIDTHS)[:len(CONST_AT)])
N_CONST = sum(CONST_WIDTHS.values())


def constants():
    p = np.arange(P)
    c = {}
    c["ident"] = np.eye(P)
    c["group"] = (p[:, None] // 32 == np.arange(G))
    c["head4"] = (p[:, None] // 8 % 4 == np.arange(G))
    c["head"] = (p[:, None] // 8 == np.arange(HEADS))
    c["sel"] = (p[:, None] % SEQ == np.arange(SEQ))
    c["band"] = np.where(abs(p[:, None] % SEQ - np.arange(SEQ)) <= 16, 0.0, -1e30)
    hd = 8
    inv = (np.float32(1.0) / np.float32(10000.0) ** (np.arange(0, hd, 2, dtype=np.float32) / np.float32(hd)))
    ang = np.arange(SEQ, dtype=np.float32)[None, :] * inv[(p % hd) // 2][:, None]
    cos, sin = np.cos(ang), np.sin(ang) * np.where(p % 2 == 0, -1.0, 1.0)[:, None]
    scale = 1.0 / np.sqrt(hd)
    c["rope"] = np.concatenate([cos * scale, sin * scale, cos, sin], axis=1)
    logp = np.float32(-0.001)
    dt = -np.log(-np.expm1(logp))
    k, j = p[:, None], p[None, :]
    lag = np.where((k >= j) & (k // SEQ == j // SEQ), k - j, 0)
    c["decay"] = np.where((k >= j) & (k // SEQ == j // SEQ), np.exp(np.float64(logp)) * np.exp(-np.float64(dt) * lag), 0.0)
    c["iota8"] = np.broadcast_to(np.arange(8), (P, 8))
    return np.concatenate([c[n].astype(np.float32) for n in CONST_WIDTHS], axis=1)


class Core:

    def __init__(self, nc, dram, ctx):
        self.nc, self.dram, self.sems = nc, dram, []
        self.x = ctx.enter_context(nc.sbuf_tensor("x_sb", [P, TILES, D], F32))
        self.ctx_n = ctx.enter_context(nc.sbuf_tensor("ctx_n", [P, TILES, D], F32))
        self.depool = ctx.enter_context(nc.sbuf_tensor("depool", [P, TILES, P], F32))
        self.const = ctx.enter_context(nc.sbuf_tensor("const", [P, N_CONST], F32))
        self.ones = ctx.enter_context(nc.sbuf_tensor("ones", [P, P], F32))
        self.eps = ctx.enter_context(nc.sbuf_tensor("eps", [P, 1], F32))
        self.half = ctx.enter_context(nc.sbuf_tensor("minus_half", [P, 1], F32))
        self.psum = ctx.enter_context(nc.psum_tensor("psum", [P, 8, 512], F32))

    def c(self, name):
        return self.const[:, CONST_AT[name]:CONST_AT[name] + CONST_WIDTHS[name]]

    def sem(self, name):
        handle = self.nc.alloc_semaphore(name=name)
        self.sems.append(handle)
        return handle

    def clear_sems(self):
        self.nc.clear_and_free_semaphores(self.sems)
        self.nc.all_engine_barrier()
        self.sems = []


class Front:

    def __init__(self, core, stage, name, S, bank, transposed=True, rms=False, pack=1):
        nc = core.nc
        self.core, self.nc, self.S, self.bank, self.rms, self.pack = core, nc, S, bank, rms, pack
        sb = lambda n, w: stage.enter_context(nc.sbuf_tensor(f"{name}_front_{n}_sb", [P, S, w], F32))
        self.stats, self.mv, self.var, self.rstd = sb("stats", 6), sb("mv", 2), sb("var", 2), sb("rstd", 1)
        self.xn = sb("xn", D)
        if transposed:
            self.xnT = sb("xnT", P)
        self.moments, self.rstd_done, self.normed, self.turned, self.xnT_done = (
            core.sem(f"{name}_front_{n}") for n in ("moments", "rstd_done", "normed", "turned", "xnT_done"))

    def streams(self, only):
        return range(self.S) if only is None else range(only, only + 1)

    def dve_moments(self, dve, n, only=None):
        dve.drain()
        for s in self.streams(only):
            self.nc.vector.bn_stats(self.stats[:, s, :], self.core.x[:, ds(n + s, 1), :])
        dve.drain()
        for s in self.streams(only):
            self.nc.vector.bn_aggr(self.mv[:, s, :], self.stats[:, s, :]).then_inc(self.moments, 1)

    def pool_rstd(self, pool, n, only=None):
        streams = self.streams(only)
        lo, hi, count = streams[0], streams[-1] + 1, len(streams)
        var = self.mv[:, lo:hi, 1:2]
        column = lambda k: self.var[:, lo:hi, k:k + 1]
        spread_s = lambda t: t[:, :].rearrange("p (s a) -> p s a", a=1).to_broadcast([P, count, 1])
        eps, half = spread_s(self.core.eps), spread_s(self.core.half)
        pool.wait_ge(self.moments, n + hi)
        self.nc.gpsimd.tensor_tensor(column(0), var, eps, ALU.add)
        if self.rms:
            pool.drain()
            self.nc.gpsimd.tensor_tensor(column(1), column(0), eps, ALU.mult)
            pool.drain()
            self.nc.gpsimd.tensor_tensor(column(0), column(1), var, ALU.add)
        pool.drain()
        self.nc.gpsimd.tensor_tensor(self.rstd[:, lo:hi, :], column(0), half, ALU.pow).then_inc(self.rstd_done, count)

    def dve_normalise(self, dve, n, only=None):
        for s in self.streams(only):
            dve.wait_ge(self.rstd_done, n + s + 1)
            self.nc.vector.tensor_scalar(self.xn[:, s, :], self.core.x[:, ds(n + s, 1), :], self.mv[:, s, 0:1],
                                         self.rstd[:, s, :], ALU.subtract, ALU.mult).then_inc(self.normed, 1)

    def pe_transpose(self, pe, n, only=None):
        for s in self.streams(only):
            pe.wait_ge(self.normed, n + s + 1)
            self.nc.tensor.transpose(self.bank(s)[:, 0:P], self.xn[:, s, :],
                                     self.core.c("ident")).then_inc(self.turned, 1)

    def act_copy(self, act, n, only=None):
        for s in self.streams(only)[::self.pack]:
            act.wait_ge(self.turned, n + s + self.pack)
            src = self.core.psum[:, s // self.pack, 0:self.pack * P] if self.pack > 1 else self.bank(s)[:, 0:P]
            self.nc.scalar.copy(self.xnT[:, s:s + self.pack, :],
                                src.rearrange("p (s w) -> p s w", w=P)).then_inc(self.xnT_done, self.pack)


def load(eng, items, sem):
    for dst, src in items:
        eng.dma_start(dst, src).then_inc(sem, 16)
    return 16 * len(items)


def add_to_x(core, t, update):
    return core.nc.vector.tensor_tensor(core.x[:, ds(t, 1), :], core.x[:, ds(t, 1), :], update, ALU.add)


def over_steps(eng, steps, step):
    with eng.Fori(0, steps - 1) as it:
        step(it, True)
    step(steps - 1, False)


def start(core):
    nc, dram = core.nc, core.dram
    LOADS = 4
    with ExitStack() as st:
        sb = lambda n, shape, dt=F32: st.enter_context(nc.sbuf_tensor(f"start_{n}", shape, dt))
        lens_i = sb("lens_i", [B, CTX], I32)
        lens = sb("lens", [B, CTX])
        ends = sb("ends", [B, CTX])
        wrap = sb("wrap", [B, CTX])
        hit = sb("hit", [B, SEQ, CTX])
        steps = sb("steps", [B, SEQ])
        bound = sb("bound", [B, SEQ])
        plug = sb("plug", [B, SEQ])
        plug_all = sb("plug_all", [P, TILES * P])
        pick = sb("pick", [P, TILES, BT, SEQ])
        rowpos = sb("rowpos", [P, 1])
        raw = sb("raw", [P, TILES, CD])
        sq = sb("sq", [P, 2, TILES // LOADS, CD])
        ms = sb("ms", [P, 3, TILES])
        halves = sb("halves", [P, TILES])
        const_in, x_in, lens_in, plug_out, plug_in = (
            core.sem(n) for n in ("const_in", "x_in", "lens_in", "plug_out", "plug_in"))
        plug_done, pos_done, pick_done, scanned, mat_done = (
            core.sem(n) for n in ("plug_done", "pos_done", "pick_done", "scanned", "mat_done"))
        ctx_in = [core.sem(f"ctx_in{q}") for q in range(LOADS)]
        squared, summed_part, summed, rs_done = (core.sem(n) for n in (
            "ctx_squared", "ctx_summed_part", "ctx_summed", "ctx_rs"))
        scratch = nc.dram_tensor("plug_scratch", (B, SEQ), F32).ap()
        block = st.enter_context(nc.Block())

        @block.sync
        def _(sp):
            sp.dma_start(lens_i[:, :], dram["mask_BxS2_if0"]).then_inc(lens_in, 16)
            sp.dma_start(core.const[:, :], dram["constants"]).then_inc(const_in, 16)
            sp.dma_start(core.x[:, :, :], dram["x"].rearrange("(t p) d -> p t d", p=P)).then_inc(x_in, 16)
            sp.wait_ge(plug_done, 1)
            sp.dma_start(scratch, plug[:, :]).then_inc(plug_out, 16)
            sp.wait_ge(plug_out, 16)
            flat = scratch.rearrange("b s -> (b s)").rearrange("(a n) -> a n", a=1)
            sp.dma_start(plug_all[:, :], flat.to_broadcast([P, B * SEQ])).then_inc(plug_in, 16)

        @block.gpsimd
        def _(pool):
            pool.wait_ge(const_in, 16)
            nc.gpsimd.memset(core.ones[:, :], 1.0)
            nc.gpsimd.memset(core.half[:, :], -0.5)
            nc.gpsimd.memset(core.eps[:, :], LN_EPS)
            nc.gpsimd.memset(halves[:, :], -0.5)
            pool.drain()
            nc.gpsimd.iota(rowpos[:, :], [[0, 1]], base=0, channel_multiplier=1,
                           allow_small_or_imprecise_dtypes=True).then_inc(pos_done, 1)
            pool.wait_ge(summed, 1)
            nc.gpsimd.tensor_tensor(ms[:, 2, :], ms[:, 1, :], halves[:, :], ALU.pow).then_inc(rs_done, 1)

        @block.scalar
        def _(act):
            part = TILES // LOADS
            for q in range(LOADS):
                for b in range(BT):
                    first = q * part * BT + b
                    act.dma_start(raw[b * SEQ:(b + 1) * SEQ, q * part:(q + 1) * part, :],
                                  dram["ctx_2048"][first:(q + 1) * part * BT:BT, 0:SEQ, :].rearrange(
                                      "t k c -> k t c")).then_inc(ctx_in[q], 16)
            for q in range(LOADS):
                act.wait_ge(ctx_in[q], 16 * BT)
                if q >= 2:
                    act.wait_ge(summed_part, q - 1)
                nc.scalar.activation(sq[:, q % 2, :, :], raw[:, q * part:(q + 1) * part, :],
                                     ACT.Square).then_inc(squared, 1)

        @block.vector
        def _(dve):
            def then_wait(ins):
                dve.drain()

            dve.wait_ge(lens_in, 16)
            then_wait(nc.vector.tensor_copy(lens[:, :], lens_i[:, :]))
            then_wait(nc.vector.memset(wrap[:, :], 1.0))
            then_wait(nc.vector.tensor_tensor_scan(ends[:, :], wrap[:, :], lens[:, :], -1.0, ALU.mult, ALU.add))
            then_wait(nc.vector.tensor_scalar(wrap[:, :], ends[:, :], 0.0, float(SEQ), ALU.is_lt, ALU.mult))
            then_wait(nc.vector.tensor_tensor(ends[:, :], ends[:, :], wrap[:, :], ALU.add))
            for t in range(SEQ):
                ins = nc.vector.tensor_scalar(hit[:, t, :], ends[:, :], float(t), None, ALU.is_equal)
            then_wait(ins)
            then_wait(nc.vector.tensor_reduce(bound[:, :], hit[:, :, :], X, ALU.max))
            then_wait(nc.vector.memset(steps[:, :], 1.0))
            then_wait(nc.vector.tensor_tensor_scan(plug[:, :], steps[:, :], bound[:, :], -1.0, ALU.mult, ALU.add))
            nc.vector.tensor_scalar(plug[:, :], plug[:, :], 0.0, float(CTX - 1), ALU.max,
                                    ALU.min).then_inc(plug_done, 1)
            dve.wait_ge(pos_done, 1)
            for g in range(1, G):
                then_wait(nc.vector.scalar_tensor_tensor(rowpos[:, :], core.c("group")[:, g:g + 1], -32.0 * g,
                                                         rowpos[:, :], ALU.mult, ALU.add))
            dve.wait_ge(plug_in, 16)
            then_wait(nc.vector.tensor_scalar(plug_all[:, :], plug_all[:, :], rowpos[:, :], None, ALU.is_equal))
            nc.vector.tensor_tensor(
                pick[:, :, :, :], plug_all[:, :].rearrange("p (t b s) -> p t b s", t=TILES, b=BT),
                core.c("group").rearrange("p (a b c) -> p a b c", a=1, c=1).to_broadcast([P, TILES, BT, SEQ]),
                ALU.mult).then_inc(pick_done, 1)
            part = TILES // LOADS
            for q in range(LOADS):
                dve.wait_ge(squared, q + 1)
                nc.vector.tensor_reduce(ms[:, 0, q * part:(q + 1) * part], sq[:, q % 2, :, :], X,
                                        ALU.add).then_inc(summed_part, 1)
            dve.drain()
            nc.vector.tensor_scalar(ms[:, 1, :], ms[:, 0, :], 1.0 / CD, LN_EPS, ALU.mult, ALU.add).then_inc(summed, 1)
            for q in range(TILES * P // 512):
                dve.wait_ge(scanned, q + 1)
                nc.vector.tensor_copy(core.depool[:, q * 4:q * 4 + 4, :],
                                      core.psum[:, q, :].rearrange("p (t s) -> p t s", s=P)).then_inc(mat_done, 1)
            dve.wait_ge(rs_done, 1)
            nc.vector.tensor_tensor(core.ctx_n[:, :, :], raw[:, :, 0:D],
                                    ms[:, 2, :].rearrange("p (t c) -> p t c", c=1).to_broadcast([P, TILES, D]), ALU.mult)
            dve.wait_ge(x_in, 16)

        @block.tensor
        def _(pe):
            pe.wait_ge(pick_done, 1)
            pe.wait_ge(const_in, 16)
            for q in range(TILES * P // 512):
                nc.tensor.matmul(core.psum[:, q, :], core.c("decay"),
                                 pick[:, :, :, :].rearrange("p t b s -> p (t b s)")[:, q * 512:q * 512 + 512],
                                 start=True, stop=True).then_inc(scanned, 1)


def depool_cross(core, name):
    nc, dram = core.nc, core.dram
    S, PACK = 8, 4
    with ExitStack() as st:
        sb = lambda n, shape, dt=F32: st.enter_context(nc.sbuf_tensor(f"{name}_{n}", shape, dt))
        w = sb("w", [D, D])
        g_res = sb("g_res", [D, 1])
        b_in = sb("b_in", [1, D])
        g_init = sb("g_init", [P, D])
        mat = sb("mat", [P, S, P])
        patch = sb("patch", [P, S, D])
        front = Front(core, st, name, S, lambda s: core.psum[:, s // PACK, s % PACK * P:s % PACK * P + P], rms=True,
                      pack=PACK)
        out = lambda u: core.psum[:, 2 + u, :].rearrange("p (s d) -> p s d", d=D)
        w_in, w_done, copied, patch_done, out_done, added = (core.sem(f"{name}_{n}") for n in (
            "w_in", "w_done", "copied", "patch_done", "out_done", "added"))
        block = st.enter_context(nc.Block())
        U = S // PACK

        @block.sync
        def _(sp):
            load(sp, [(w[:, :], dram[f"{name}_W_in_T"]), (g_res[:, :], dram[f"{name}_g_res"]),
                      (b_in[:, :], dram[f"{name}_b_in"]),
                      (g_init[:, :], dram[f"{name}_g_init"][:, 0:D].to_broadcast([P, D]))], w_in)

        @block.gpsimd
        def _(pool):
            pool.wait_ge(w_in, 64)
            g4 = g_init[:, :].rearrange("p (s d) -> p s d", s=1).to_broadcast([P, PACK, D])
            def step(it, more):
                for u in range(U):
                    pool.wait_ge(out_done, it * U + u + 1)
                    nc.gpsimd.tensor_tensor(patch[:, 4 * u:4 * u + 4, :], core.ctx_n[:, ds(it * S + 4 * u, PACK), :], g4,
                                            ALU.mult).then_inc(patch_done, 1)
                if more:
                    front.pool_rstd(pool, (it + 1) * S)

            front.pool_rstd(pool, 0)
            over_steps(pool, TILES // S, step)

        @block.scalar
        def _(act):
            with act.Fori(0, TILES // S) as it:
                for u in range(U):
                    act.wait_ge(out_done, it * U + u + 1)
                    nc.scalar.copy(mat[:, 4 * u:4 * u + 4, :], core.depool[:, ds(it * S + 4 * u, PACK), :]).then_inc(copied, 1)
                front.act_copy(act, it * S)

        @block.vector
        def _(dve):
            dve.wait_ge(w_in, 64)
            nc.vector.tensor_scalar(w[:, :], w[:, :], g_res[:, :], None, ALU.mult).then_inc(w_done, 1)
            def step(it, more):
                if more:
                    front.dve_moments(dve, (it + 1) * S)
                    dve.wait_ge(front.turned, (it + 1) * S)
                    front.dve_normalise(dve, (it + 1) * S)
                for u in range(U):
                    dve.wait_ge(out_done, (it + 1) * U + u + 1)
                    x = core.x[:, ds(it * S + 4 * u, PACK), :]
                    nc.vector.tensor_tensor(x, x, out(u), ALU.add).then_inc(added, 1)

            front.dve_moments(dve, 0)
            front.dve_normalise(dve, 0)
            over_steps(dve, TILES // S, step)

        @block.tensor
        def _(pe):
            pe.sem_inc(out_done, U)
            pe.sem_inc(added, U)
            pe.wait_ge(w_done, 1)
            with pe.Fori(0, TILES // S) as it:
                front.pe_transpose(pe, it * S)
                for u in range(U):
                    pe.wait_ge(added, it * U + u + 1)
                    pe.wait_ge(copied, it * U + u + 1)
                    pe.wait_ge(patch_done, it * U + u + 1)
                    pe.wait_ge(front.xnT_done, it * S + 4 * u + 4)
                    for s in range(4 * u, 4 * u + 4):
                        nc.tensor.matmul(out(u)[:, s % 4, :], mat[:, s, :], patch[:, s, :], start=True, stop=False)
                        nc.tensor.matmul(out(u)[:, s % 4, :], core.ones[0:1, :], b_in[:, :], start=False, stop=False)
                        last = nc.tensor.matmul(out(u)[:, s % 4, :], front.xnT[:, s, :], w[:, :], start=False, stop=True)
                    last.then_inc(out_done, 1)


def spread(t, block, width):
    return (t.rearrange("p b (a w) -> p b a w", a=1).to_broadcast([P, BT, G, width]),
            block.rearrange("p (b j w) -> p b j w", b=1, w=1).to_broadcast([P, BT, G, width]))


def per_row(t):
    return t.rearrange("p (r w) -> p r w", w=1).to_broadcast([P, t.shape[1], SEQ])


def rotary_attention(core, name):
    nc, dram = core.nc, core.dram
    S = 4
    with ExitStack() as st:
        sb = lambda n, shape, dt=F32: st.enter_context(nc.sbuf_tensor(f"{name}_{n}", shape, dt))
        w_qk = sb("w_qk", [D, 4, D])
        w_v = sb("w_v", [D, G * 8])
        w_o = sb("w_o", [G * 8, G, D])
        prod = sb("prod", [P, S, 4, P])
        qk = sb("qk", [P, S, 2, P])
        q4 = sb("q4", [P, S, BT, G, SEQ])
        kbd = sb("kbd", [P, S, BT, G, SEQ])
        v = sb("v", [P, S, G * 8])
        vbd = sb("vbd", [P, S, BT, G * 8])
        prob = sb("prob", [P, S, HEADS, SEQ])
        top = sb("top", [P, S, HEADS])
        total = sb("total", [P, S, HEADS])
        probT = sb("probT", [P, S, BT, P])
        mixT = sb("mixT", [G * 8, S, G, P])
        bank_a = lambda s: core.psum[:, 2 * s, :]
        bank_b = lambda s: core.psum[:, 2 * s + 1, :]
        front = Front(core, st, name, S, bank_a)
        (w_in, zeroed, projected, v_done, vbd_in, roped, masked, scored, shifted, exped, summed, normal, turned, probT_done,
         mixed, mixT_done, out_done, added) = (core.sem(f"{name}_{n}") for n in (
             "w_in", "zeroed", "projected", "v_done", "vbd_in", "roped", "masked", "scored", "shifted", "exped", "summed",
             "normal", "turned", "probT_done", "mixed", "mixT_done", "out_done", "added"))
        block = st.enter_context(nc.Block())

        @block.sync
        def _(sp):
            load(sp, [(w_qk[:, :, :], dram[f"{name}_Wqk"]), (w_v[:, :], dram[f"{name}_Wv"]),
                      (w_o[:, :, :], dram[f"{name}_Wo"])], w_in)
            sp.wait_ge(zeroed, 1)
            with sp.Fori(0, TILES // S) as it:
                sp.wait_ge(v_done, (it + 1) * S)
                sp.wait_ge(mixed, (it + 1) * S)
                for b in range(BT):
                    for g in range(G):
                        sp.dma_start(vbd[g * 32:(g + 1) * 32, :, b, 8 * g:8 * g + 8],
                                     v[b * 32:(b + 1) * 32, :, 8 * g:8 * g + 8]).then_inc(vbd_in, 16)

        @block.gpsimd
        def _(pool):
            nc.gpsimd.memset(vbd[:, :, :, :], 0.0).then_inc(zeroed, 1)
            def step(it, more):
                n = it * S
                for s in range(S):
                    pool.wait_ge(roped, n + s + 1)
                    a, m = spread(qk[:, s, 0, :].rearrange("p (b w) -> p b w", b=BT), core.c("head4"), SEQ)
                    nc.gpsimd.tensor_tensor(q4[:, s, :, :, :], a, m, ALU.mult)
                    a, m = spread(qk[:, s, 1, :].rearrange("p (b w) -> p b w", b=BT), core.c("group"), SEQ)
                    nc.gpsimd.tensor_tensor(kbd[:, s, :, :, :], a, m, ALU.mult).then_inc(masked, 1)
                for s in range(S):
                    pool.wait_ge(summed, n + s + 1)
                    nc.gpsimd.tensor_tensor(prob[:, s, :, :], prob[:, s, :, :], per_row(total[:, s, :]),
                                            ALU.mult).then_inc(normal, 1)
                if more:
                    front.pool_rstd(pool, n + S)

            front.pool_rstd(pool, 0)
            over_steps(pool, TILES // S, step)

        @block.scalar
        def _(act):
            with act.Fori(0, TILES // S) as it:
                n = it * S
                front.act_copy(act, n)
                act.wait_ge(vbd_in, (it + 1) * 256)
                for s in range(S):
                    act.wait_ge(projected, n + s + 1)
                    nc.scalar.copy(v[:, s, :], bank_a(s)[:, 0:G * 8]).then_inc(v_done, 1)
                for s in range(S):
                    act.wait_ge(shifted, n + s + 1)
                    nc.scalar.activation(prob[:, s, :, :], prob[:, s, :, :], ACT.Exp).then_inc(exped, 1)
                for s in range(S):
                    act.wait_ge(turned, n + s + 1)
                    nc.scalar.copy(probT[:, s, :, :], bank_a(s).rearrange("p (b w) -> p b w", b=BT)).then_inc(probT_done, 1)
                for s in range(S):
                    act.wait_ge(mixed, n + s + 1 + S)
                    nc.scalar.copy(mixT[:, s, :, :].rearrange("p h (b q) -> p b h q", b=BT),
                                   bank_b(s)[0:G * 8, :].rearrange("p (b h q) -> p b h q", b=BT, h=G)).then_inc(mixT_done, 1)

        @block.vector
        def _(dve):
            def step(it, more):
                n = it * S
                rope = core.c("rope").rearrange("p (f a w) -> p f a w", f=4, a=1).to_broadcast([P, 4, BT, SEQ])
                for s in range(S):
                    dve.wait_ge(projected, n + s + 1)
                    nc.vector.tensor_tensor(prod[:, s, :, :].rearrange("p f (b w) -> p f b w", b=BT),
                                            bank_b(s).rearrange("p (f b w) -> p f b w", f=4, b=BT), rope, ALU.mult)
                dve.drain()
                for s in range(S):
                    v = prod[:, s, :, :].rearrange("p (a f) w -> p a f w", a=2)
                    nc.vector.tensor_tensor(qk[:, s, :, :], v[:, :, 0, :], v[:, :, 1, :], ALU.add).then_inc(roped, 1)
                band = core.c("band").rearrange("p (a w) -> p a w", a=1).to_broadcast([P, HEADS, SEQ])
                for streams in ((0, 1), (2, 3)):
                    for s in streams:
                        dve.wait_ge(scored, n + s + 1)
                        nc.vector.tensor_tensor(prob[:, s, :, :], bank_b(s).rearrange("p (a w) -> p a w", w=SEQ), band,
                                                ALU.add)
                    dve.drain()
                    for s in streams:
                        nc.vector.tensor_reduce(top[:, s, :], prob[:, s, :, :], X, ALU.max)
                    dve.drain()
                    for s in streams:
                        nc.vector.tensor_tensor(prob[:, s, :, :], prob[:, s, :, :], per_row(top[:, s, :]),
                                                ALU.subtract).then_inc(shifted, 1)
                for streams in ((0, 1), (2, 3)):
                    for s in streams:
                        dve.wait_ge(exped, n + s + 1)
                        nc.vector.tensor_reduce(total[:, s, :], prob[:, s, :, :], X, ALU.add)
                    dve.drain()
                    for s in streams:
                        nc.vector.reciprocal(total[:, s, :], total[:, s, :]).then_inc(summed, 1)
                if more:
                    front.dve_moments(dve, n + S)
                    front.dve_normalise(dve, n + S)
                for s in range(S):
                    dve.wait_ge(out_done, n + s + 1)
                    add_to_x(core, n + s, bank_a(s)[:, 0:D]).then_inc(added, 1)

            front.dve_moments(dve, 0)
            front.dve_normalise(dve, 0)
            over_steps(dve, TILES // S, step)

        @block.tensor
        def _(pe):
            pe.wait_ge(w_in, 48)
            pe.sem_inc(mixed, S)
            pe.sem_inc(added, S)
            pe.sem_inc(vbd_in, 256)
            with pe.Fori(0, TILES // S) as it:
                n = it * S
                pe.wait_ge(added, n + S)
                front.pe_transpose(pe, n)
                for s in range(S):
                    pe.wait_ge(front.xnT_done, n + s + 1)
                    for f in range(4):
                        nc.tensor.matmul(bank_b(s)[:, f * P:(f + 1) * P], w_qk[:, f, :], front.xnT[:, s, :],
                                         start=True, stop=True)
                    nc.tensor.matmul(bank_a(s)[:, 0:G * 8], front.xnT[:, s, :], w_v[:, :], start=True,
                                     stop=True).then_inc(projected, 1)
                for s in range(S):
                    pe.wait_ge(masked, n + s + 1)
                    for b in range(BT):
                        last = nc.tensor.matmul(bank_b(s)[:, b * P:(b + 1) * P],
                                                q4[:, s, b, :, :].rearrange("p j w -> p (j w)"),
                                                kbd[:, s, b, :, :].rearrange("p j w -> p (j w)"), start=True, stop=True)
                    last.then_inc(scored, 1)
                for s in range(S):
                    pe.wait_ge(normal, n + s + 1)
                    for b in range(BT):
                        last = nc.tensor.transpose(bank_a(s)[:, b * P:(b + 1) * P],
                                                   prob[:, s, b * G:(b + 1) * G, :].rearrange("p g k -> p (g k)"),
                                                   core.c("ident"))
                    last.then_inc(turned, 1)
                pe.wait_ge(vbd_in, (it + 2) * 256)
                for s in range(S):
                    pe.wait_ge(probT_done, n + s + 1)
                    for b in range(BT):
                        last = nc.tensor.matmul(bank_b(s)[0:G * 8, b * P:(b + 1) * P], vbd[:, s, b, :], probT[:, s, b, :],
                                                start=True, stop=True)
                    last.then_inc(mixed, 1)
                for s in range(S):
                    pe.wait_ge(mixT_done, n + s + 1)
                    for h in range(G):
                        last = nc.tensor.matmul(bank_a(s)[:, 0:D], mixT[:, s, h, :], w_o[:, h, :], start=(h == 0),
                                                stop=(h == G - 1))
                    last.then_inc(out_done, 1)


def product_key_experts(core, name):
    nc, dram = core.nc, core.dram
    H, K, TOP, KG = 8, 32, 8, 16
    E = K * K
    with ExitStack() as outer:
        keep = lambda n, shape, dt=F32: outer.enter_context(nc.sbuf_tensor(f"{name}_{n}", shape, dt))
        w_sim = keep("w_sim", [D, KG * K])
        b_sim = keep("b_sim", [P, KG * K])
        down = keep("down", [D, E])
        up = keep("up", [P, E // P, D])
        experts_in = core.sem(f"{name}_experts_in")
        query_keys(core, name, w_sim, b_sim, down, up, experts_in)

        S, RING = 2, 4
        sb = keep
        sims = sb("sims", [P, S, KG, K])
        top = sb("top", [P, S, KG, TOP])
        pairs = sb("pairs", [P, H, TOP * TOP])
        best = sb("best", [P, S, H, TOP])
        shift = sb("shift", [P, H, TOP])
        total = sb("total", [P, H])
        bias = sb("bias", [P, S, H])
        sums = sb("sums", [P, RING, K, K])
        prob = sb("prob", [P, RING, E])
        weight = sb("weight", [P, E])
        value = sb("value", [P, S, E])
        mixT = sb("mixT", [P, E // P, P])
        pair = lambda k: core.psum[:, k:k + 2, :].rearrange("p a w -> p (a w)")
        SIMS = core.psum[:, 6, :]
        OUT = core.psum[:, 7, P:P + D]
        front = Front(core, outer, f"{name}2", S, lambda s: core.psum[:, 7, 0:P])
        (simmed, sims_ready, valued, gelued, cut, exped, reduced, logged, biased, summed, probs, used, kept, mixed, turned,
         mixT_done, out_done) = (core.sem(f"{name}_{n}") for n in (
             "simmed", "sims_ready", "valued", "gelued", "cut", "exped", "reduced", "logged", "biased", "summed", "probs", "used",
             "kept", "mixed", "turned", "mixT_done", "out_done"))
        block = outer.enter_context(nc.Block())

        def over_tiles(eng, phase):
            phase(0, 0, False, True)
            with eng.Fori(0, TILES // 2 - 1) as it:
                phase(1 + 2 * it, 1, True, True)
                phase(2 + 2 * it, 0, True, True)
            phase(TILES - 1, 1, True, False)

        @block.gpsimd
        def _(pool):
            def phase(t, s, before, after):
                for h in range(H):
                    if h == 0:
                        pool.wait_ge(sims_ready, t + 1)
                    pool.wait_ge(kept, t * H + h + 1)
                    sx = sims[:, s, h, :].rearrange("p (i j) -> p i j", j=1).to_broadcast([P, K, K])
                    sy = sims[:, s, H + h, :].rearrange("p (i j) -> p i j", i=1).to_broadcast([P, K, K])
                    nc.gpsimd.tensor_tensor(sums[:, h % RING, :, :], sx, sy, ALU.add).then_inc(summed, 1)
                    if after and h == 0:
                        front.pool_rstd(pool, t + s, only=1 - s)

            front.pool_rstd(pool, 0, only=0)
            over_tiles(pool, phase)

        @block.scalar
        def _(act):
            def shift_exp(t):
                act.wait_ge(cut, t + 1)
                nc.scalar.activation(shift[:, :, :], shift[:, :, :], ACT.Exp).then_inc(exped, 1)

            def total_ln(t):
                act.wait_ge(reduced, t + 1)
                nc.scalar.activation(total[:, :], total[:, :], ACT.Ln).then_inc(logged, 1)

            def gelu(t, s):
                act.wait_ge(valued, t + 1)
                nc.scalar.activation(value[:, s, :], pair(2 * s), ACT.Gelu_apprx_tanh).then_inc(gelued, 1)

            def mixT_copy(t):
                act.wait_ge(turned, t + 1)
                nc.scalar.copy(mixT[:, :, :], pair(4).rearrange("p (c w) -> p c w", w=P)).then_inc(mixT_done, 1)

            def phase(t, s, before, after):
                for h in range(H):
                    if h == 0:
                        act.wait_ge(biased, t + 1)
                    act.wait_ge(used, t * H + h + 1)
                    act.wait_ge(summed, t * H + h + 1)
                    nc.scalar.activation(prob[:, h % RING, :], sums[:, h % RING, :, :].rearrange("p i j -> p (i j)"),
                                         ACT.Exp, bias=bias[:, s, h:h + 1]).then_inc(probs, 1)
                    if after and h == 2:
                        front.act_copy(act, t + s, only=1 - s)
                    if before and h == 3:
                        mixT_copy(t - 1)
                if after:
                    shift_exp(t + 1)
                    total_ln(t + 1)
                    gelu(t + 1, 1 - s)

            front.act_copy(act, 0, only=0)
            shift_exp(0)
            total_ln(0)
            gelu(0, 0)
            over_tiles(act, phase)
            mixT_copy(TILES - 1)

        @block.vector
        def _(dve):
            def add_bias(t, s):
                dve.wait_ge(simmed, t + 1)
                nc.vector.tensor_tensor(sims[:, s, :, :].rearrange("p g k -> p (g k)"), SIMS, b_sim[:, :],
                                        ALU.add).then_inc(sims_ready, 1)
                dve.drain()

            def tops(s, groups):
                for g in groups:
                    nc.vector.max(top[:, s, g, :], sims[:, s, g, :])

            def pair_sums(s):
                dve.drain()
                for h in range(H):
                    sx = top[:, s, h, :].rearrange("p (i j) -> p i j", j=1).to_broadcast([P, TOP, TOP])
                    sy = top[:, s, H + h, :].rearrange("p (i j) -> p i j", i=1).to_broadcast([P, TOP, TOP])
                    nc.vector.tensor_tensor(pairs[:, h, :].rearrange("p (i j) -> p i j", j=TOP), sx, sy, ALU.add)
                dve.drain()

            def bests(s):
                for h in range(H):
                    nc.vector.max(best[:, s, h, :], pairs[:, h, :])
                dve.drain()
                nc.vector.tensor_tensor(shift[:, :, :], best[:, s, :, :],
                                        best[:, s, :, 0:1].to_broadcast([P, H, TOP]), ALU.subtract).then_inc(cut, 1)

            def reduce_exps(t):
                dve.wait_ge(exped, t + 1)
                nc.vector.tensor_reduce(total[:, :], shift[:, :, :], X, ALU.add).then_inc(reduced, 1)

            def biases(t, s):
                dve.wait_ge(logged, t + 1)
                nc.vector.scalar_tensor_tensor(bias[:, s, :], total[:, :], -1.0,
                                               best[:, s, :, 0:1].rearrange("p h a -> p (h a)"), ALU.mult,
                                               ALU.subtract).then_inc(biased, 1)

            def weigh(t, s):
                dve.wait_ge(gelued, t + 1)
                dve.wait_ge(used, (t + 1) * H + RING)
                nc.vector.tensor_tensor(weight[:, :], pair(2 * s), value[:, s, :], ALU.mult).then_inc(mixed, 1)

            def phase(t, s, before, after):
                o = 1 - s
                if after:
                    front.dve_moments(dve, t + s, only=o)
                for h in range(H):
                    dve.wait_ge(probs, t * H + h + 1)
                    nc.vector.scalar_tensor_tensor(
                        prob[:, h % RING, :], sums[:, h % RING, :, :].rearrange("p i j -> p (i j)"),
                        best[:, s, h, TOP - 1:TOP], prob[:, h % RING, :], ALU.is_ge, ALU.mult).then_inc(kept, 1)
                    if before and h == 0:
                        weigh(t - 1, o)
                    if after and h == 1:
                        front.dve_normalise(dve, t + s, only=o)
                    if after and h == 3:
                        add_bias(t + 1, o)
                        tops(o, range(0, KG // 2))
                    if after and h == 4:
                        tops(o, range(KG // 2, KG))
                        pair_sums(o)
                    if after and h == 5:
                        bests(o)
                    if after and h == 6:
                        reduce_exps(t + 1)
                    if before and h == 6:
                        dve.wait_ge(out_done, t)
                        add_to_x(core, t - 1, OUT)
                if after:
                    biases(t + 1, o)

            front.dve_moments(dve, 0, only=0)
            front.dve_normalise(dve, 0, only=0)
            add_bias(0, 0)
            tops(0, range(KG))
            pair_sums(0)
            bests(0)
            reduce_exps(0)
            biases(0, 0)
            over_tiles(dve, phase)
            weigh(TILES - 1, 1)
            dve.wait_ge(out_done, TILES)
            add_to_x(core, TILES - 1, OUT)

        @block.tensor
        def _(pe):
            def sim(t, s):
                pe.wait_ge(front.xnT_done, t + 1)
                nc.tensor.matmul(SIMS, front.xnT[:, s, :], w_sim[:, :], start=True, stop=True).then_inc(simmed, 1)

            def values(t, s):
                for k in range(2):
                    last = nc.tensor.matmul(core.psum[:, 2 * s + k, :], front.xnT[:, s, :], down[:, k * 512:(k + 1) * 512],
                                            start=True, stop=True)
                last.then_inc(valued, 1)

            def turn_weights(t):
                pe.wait_ge(mixed, t + 1)
                for c in range(E // P):
                    last = nc.tensor.transpose(pair(4)[:, c * P:(c + 1) * P], weight[:, c * P:(c + 1) * P], core.c("ident"))
                last.then_inc(turned, 1)

            def output(t):
                pe.wait_ge(mixT_done, t + 1)
                for c in range(E // P):
                    last = nc.tensor.matmul(OUT, mixT[:, c, :], up[:, c, :], start=(c == 0), stop=(c == E // P - 1))
                last.then_inc(out_done, 1)

            def phase(t, s, before, after):
                o = 1 - s
                for h in range(H):
                    if h == 0:
                        pe.wait_ge(gelued, t + 1)
                    pe.wait_ge(kept, t * H + h + 1 + RING)
                    for k in range(2):
                        last = nc.tensor.matmul(core.psum[:, 2 * s + k, :], core.c("ident"),
                                                prob[:, h % RING, k * 512:(k + 1) * 512], start=(h == 0), stop=(h == H - 1))
                    last.then_inc(used, 1)
                    if after and h == 1:
                        front.pe_transpose(pe, t + s, only=o)
                    if before and h == 1:
                        turn_weights(t - 1)
                    if after and h == 2:
                        sim(t + 1, o)
                    if before and h == 3:
                        output(t - 1)
                    if after and h == 4:
                        values(t + 1, o)

            pe.wait_ge(experts_in, 32)
            pe.sem_inc(used, RING)
            pe.sem_inc(kept, RING)
            front.pe_transpose(pe, 0, only=0)
            sim(0, 0)
            values(0, 0)
            over_tiles(pe, phase)
            turn_weights(TILES - 1)
            output(TILES - 1)


def query_keys(core, name, w_sim, b_sim, down, up, experts_in):
    nc, dram = core.nc, core.dram
    S, KG, K = 4, 16, 32
    TOKENS = B * SEQ
    with ExitStack() as st:
        sb = lambda n, shape, dt=F32: st.enter_context(nc.sbuf_tensor(f"{name}_keys_{n}", shape, dt))
        w_q = sb("w_q", [D, KG * P])
        w_qT = sb("w_qT", [P, KG, D])
        keys = sb("keys", [P, KG, K])
        keys_s = sb("keys_s", [P, KG, K])
        gamma = sb("gamma", [P, KG])
        beta = sb("beta", [P, KG])
        zeros = sb("zeros", [P, P])
        gram = sb("gram", [D, D])
        mean = sb("mean", [D, 1])
        mean_row = sb("mean_row", [1, D])
        spread_w = sb("spread_w", [D, KG * P])
        var = sb("var", [P, KG])
        rstd = sb("rstd", [P, KG])
        shift = sb("shift", [P, KG])
        halves = sb("halves", [P, KG])
        front = Front(core, st, f"{name}1", S, None, transposed=False)
        names = ("wq_in", "zeroed", "added", "gram_done", "mean_done", "row_made", "row_done", "outer_made", "cov_done",
                 "cov_w", "cov_w_done", "stats_made", "var_done", "rstd_q", "keys_done", "sim_made")
        (wq_in, zeroed, added, gram_done, mean_done, row_made, row_done, outer_made, cov_done, cov_w, cov_w_done,
         stats_made, var_done, rstd_q, keys_done, sim_made) = (core.sem(f"{name}_{n}") for n in names)
        GRAM, MEAN = core.psum[:, 6, 0:D], core.psum[:, 7, 0:1]
        block = st.enter_context(nc.Block())

        @block.sync
        def _(sp):
            load(sp, [(w_q[:, :], dram[f"{name}_w_q"]), (w_qT[:, :, :], dram[f"{name}_w_q_T"]),
                      (keys[:, :, :], dram[f"{name}_keys"]), (gamma[:, :], dram[f"{name}_gamma"]),
                      (beta[:, :], dram[f"{name}_beta"])], wq_in)
            load(sp, [(down[:, :], dram[f"{name}_down_T"]), (up[:, :, :], dram[f"{name}_up"])], experts_in)

        @block.gpsimd
        def _(pool):
            nc.gpsimd.memset(zeros[:, :], 0.0).then_inc(zeroed, 1)
            nc.gpsimd.memset(halves[:, :], -0.5)
            with pool.Fori(0, TILES // S) as it:
                front.pool_rstd(pool, it * S)
            pool.wait_ge(var_done, 1)
            nc.gpsimd.tensor_tensor(rstd[:, :], var[:, :], halves[:, :], ALU.pow).then_inc(rstd_q, 1)

        @block.vector
        def _(dve):
            dve.sem_inc(added, S)
            with dve.Fori(0, TILES // S) as it:
                n = it * S
                front.dve_moments(dve, n)
                dve.wait_ge(added, n + S)
                front.dve_normalise(dve, n)
            dve.wait_ge(gram_done, 1)
            nc.vector.tensor_scalar(gram[:, :], GRAM, 1.0 / TOKENS, None, ALU.mult)
            nc.vector.tensor_scalar(mean[:, :], MEAN, 1.0 / TOKENS, None, ALU.mult).then_inc(mean_done, 1)
            dve.wait_ge(row_made, 1)
            nc.vector.tensor_copy(mean_row[:, :], core.psum[0:1, 0, 0:D]).then_inc(row_done, 1)
            dve.wait_ge(outer_made, 1)
            nc.vector.tensor_tensor(gram[:, :], gram[:, :], core.psum[:, 1, 0:D], ALU.subtract).then_inc(cov_done, 1)
            dve.wait_ge(cov_w, 1)
            for k in range(4):
                ins = nc.vector.tensor_tensor(spread_w[:, k * 512:(k + 1) * 512], w_q[:, k * 512:(k + 1) * 512],
                                              core.psum[:, k, :], ALU.mult)
            ins.then_inc(cov_w_done, 1)
            dve.wait_ge(stats_made, 1)
            nc.vector.tensor_scalar(var[:, :], core.psum[:, 4, 0:KG], LN_EPS, None, ALU.add).then_inc(var_done, 1)
            dve.wait_ge(rstd_q, 1)
            nc.vector.tensor_tensor(gamma[:, :], gamma[:, :], rstd[:, :], ALU.mult)
            dve.drain()
            nc.vector.tensor_tensor(shift[:, :], core.psum[:, 4, KG:2 * KG], gamma[:, :], ALU.mult)
            nc.vector.tensor_tensor(keys_s[:, :, :], keys[:, :, :],
                                    gamma[:, :].rearrange("p (g k) -> p g k", k=1).to_broadcast([P, KG, K]), ALU.mult)
            dve.drain()
            nc.vector.tensor_tensor(shift[:, :], beta[:, :], shift[:, :], ALU.subtract).then_inc(keys_done, 1)
            dve.wait_ge(sim_made, 1)
            nc.vector.tensor_copy(w_sim[:, :], core.psum[:, 2, :])
            nc.vector.tensor_copy(b_sim[:, :], core.psum[:, 3, :])

        @block.tensor
        def _(pe):
            pe.wait_ge(zeroed, 1)
            nc.tensor.matmul(GRAM, zeros[:, :], zeros[:, :], start=True, stop=False)
            nc.tensor.matmul(MEAN, zeros[:, :], zeros[:, 0:1], start=True, stop=False)
            with pe.Fori(0, TILES // S) as it:
                for s in range(S):
                    pe.wait_ge(front.normed, it * S + s + 1)
                    nc.tensor.matmul(GRAM, front.xn[:, s, :], front.xn[:, s, :], start=False, stop=False)
                    nc.tensor.matmul(MEAN, front.xn[:, s, :], core.ones[:, 0:1], start=False, stop=False).then_inc(added, 1)
            nc.tensor.matmul(GRAM, zeros[:, :], zeros[:, :], start=False, stop=True)
            nc.tensor.matmul(MEAN, zeros[:, :], zeros[:, 0:1], start=False, stop=True).then_inc(gram_done, 1)
            pe.wait_ge(mean_done, 1)
            nc.tensor.transpose(core.psum[0:1, 0, 0:D], mean[:, :], core.c("ident")).then_inc(row_made, 1)
            pe.wait_ge(row_done, 1)
            nc.tensor.matmul(core.psum[:, 1, 0:D], mean_row[:, :], mean_row[:, :], start=True, stop=True).then_inc(outer_made, 1)
            pe.wait_ge(cov_done, 1)
            pe.wait_ge(wq_in, 80)
            for k in range(4):
                last = nc.tensor.matmul(core.psum[:, k, :], gram[:, :], w_q[:, k * 512:(k + 1) * 512], start=True, stop=True)
            last.then_inc(cov_w, 1)
            pe.wait_ge(cov_w_done, 1)
            for g in range(KG):
                nc.tensor.matmul(core.psum[:, 4, g:g + 1], spread_w[:, g * P:(g + 1) * P], core.ones[:, 0:1],
                                 start=True, stop=True)
            for g in range(KG):
                last = nc.tensor.matmul(core.psum[:, 4, KG + g:KG + g + 1], w_q[:, g * P:(g + 1) * P], mean[:, :],
                                        start=True, stop=True)
            last.then_inc(stats_made, 1)
            pe.wait_ge(keys_done, 1)
            for g in range(KG):
                nc.tensor.matmul(core.psum[:, 2, g * K:(g + 1) * K], w_qT[:, g, :], keys_s[:, g, :], start=True, stop=True)
            for g in range(KG):
                last = nc.tensor.matmul(core.psum[:, 3, g * K:(g + 1) * K], shift[:, g:g + 1].to_broadcast([P, P]),
                                        keys[:, g, :], start=True, stop=True)
            last.then_inc(sim_made, 1)


def context_attention(core, name):
    nc, dram = core.nc, core.dram
    KEYS = CTX + SEQ
    scale = 8 ** -0.5
    with ExitStack() as outer:
        keep = lambda n, shape, dt=F32: outer.enter_context(nc.sbuf_tensor(f"{name}_{n}", shape, dt))
        qT = keep("qT", [P, TILES, P])
        kT = keep("kT", [P, TILES, P])
        v = keep("v", [P, TILES, D])
        w_proj = keep("w_proj", [D, D])
        b_proj = keep("b_proj", [1, D])
        w_in = core.sem(f"{name}_w_in")
        own_qkv(core, name, qT, kT, v, scale, w_in, w_proj, b_proj)

        k_all = keep("k_all", [P, BT, KEYS])
        v_all = keep("v_all", [P, BT, 2, D])
        v_end = keep("v_end", [P, BT, 2, 2, 32])
        q_bd = keep("q_bd", [P, BT, HEADS, SEQ])
        prob = keep("prob", [P, 2, 2, KEYS])
        nmax = keep("nmax", [P, 2, 2])
        total = keep("total", [P, 2, 2])
        end = keep("end", [P, 2, 2, 64])
        probT = keep("probT", [P, 2, 2, 2, P])
        endT = keep("endT", [P, 2, P])
        picked = keep("picked", [P, G, SEQ])
        attnT = keep("attnT", [P, P])
        scores = lambda s: core.psum[:, 4 * s:4 * s + 2, 0:KEYS]
        turned_end = lambda s: core.psum[:, 4 * s + 3, 0:P]
        turned_bank = lambda s: core.psum[:, 4 * s + 2, :].rearrange("p (k g w) -> p k g w", k=2, g=2)
        mix = lambda s: core.psum[64 * s:64 * s + 64, 4 * s + 3, P:2 * P]
        OUT = core.psum[:, 7, 2 * P:3 * P]
        ctx_in = [core.sem(f"{name}_ctx_in{b}") for b in range(BT)]
        (zeroed, prepared, scored, maxed, exped, scaled, turned, probT_done, endT_done, mixed, joined,
         out_done, tile_done) = (core.sem(f"{name}_{n}") for n in (
             "zeroed", "prepared", "scored", "maxed", "exped", "scaled", "turned", "probT_done", "endT_done",
             "mixed", "joined", "out_done", "tile_done"))
        block = outer.enter_context(nc.Block())
        UNITS = 2 * BT

        def over_tiles(eng, tile):
            with eng.Fori(0, TILES - 1) as t:
                tile(t, False)
            tile(TILES - 1, True)

        def ahead(t, u, last, by):
            return (t, u + by) if u + by < UNITS else None if last else (t + 1, u + by - UNITS)

        @block.sync
        def _(sp):
            sp.wait_ge(zeroed, 1)
            with sp.Fori(0, TILES) as t:
                for b in range(BT):
                    sp.wait_ge(mixed, t * UNITS + 2 * b + 2)
                    seq = t * BT + b
                    row = dram["ctx_2048"][ds(seq, 1), :, :].rearrange("a m c -> (a m) c")
                    for dst, src in ((k_all[:, b, 0:CTX], dram["ctx_T"][ds(seq, 1), 0:D, :].rearrange("a c m -> (a c) m")),
                                     (v_all[:, b, 0:2, :], row[0:2 * P, D:2 * D].rearrange("(k m) c -> m k c", m=P))):
                        sp.dma_start(dst, src).then_inc(ctx_in[b], 16)
                    for g in range(2):
                        by_half = lambda rows: rows.rearrange("p (s g j) -> p s g j", s=2, g=2)[:, :, g, :]
                        sp.dma_start(v_end[64 * g:64 * g + 1, b, :, g, :],
                                     by_half(row[2 * P:CTX, D:2 * D])).then_inc(ctx_in[b], 16)
                        sp.dma_start(v_end[64 * g + 1:64 * g + 1 + SEQ, b, :, g, :],
                                     by_half(v[b * SEQ:(b + 1) * SEQ, ds(t, 1), :].rearrange(
                                         "p a w -> p (a w)"))).then_inc(ctx_in[b], 16)

        @block.gpsimd
        def _(pool):
            nc.gpsimd.memset(end[:, :, :, :], 0.0)
            nc.gpsimd.memset(v_end[:, :, :, :, :], 0.0).then_inc(zeroed, 1)
            with pool.Fori(0, TILES) as t:
                for b in range(BT):
                    pool.wait_ge(mixed, t * UNITS + 2 * b + 2)
                    cols = slice(b * SEQ, (b + 1) * SEQ)
                    a = qT[:, ds(t, 1), cols].to_broadcast([P, HEADS, SEQ])
                    m = core.c("head").rearrange("p (j w) -> p j w", w=1).to_broadcast([P, HEADS, SEQ])
                    nc.gpsimd.tensor_tensor(q_bd[:, b, :, :], a, m, ALU.mult)
                    nc.gpsimd.tensor_copy(k_all[:, b, CTX:KEYS], kT[:, ds(t, 1), cols]).then_inc(prepared, 1)

        @block.scalar
        def _(act):
            def exps(t, u):
                s = u % 2
                act.wait_ge(maxed, t * UNITS + u + 1)
                for g in range(2):
                    ins = nc.scalar.activation(prob[:, s, g, :], scores(s)[:, g, :], ACT.Exp,
                                               bias=nmax[:, s, g:g + 1], accum_out=total[:, s, g:g + 1])
                ins.then_inc(exped, 1)

            def tile(t, last):
                for u in range(UNITS):
                    act.wait_ge(turned, t * UNITS + u + 1)
                    nc.scalar.copy(probT[:, u % 2, :, :, :], turned_bank(u % 2)).then_inc(probT_done, 1)
                    if ahead(t, u, last, 2):
                        exps(*ahead(t, u, last, 2))

            exps(0, 0)
            exps(0, 1)
            over_tiles(act, tile)

        @block.vector
        def _(dve):
            def maxes(t, u):
                dve.wait_ge(scored, t * UNITS + u + 1)
                nc.vector.tensor_reduce(nmax[:, u % 2, :], scores(u % 2), X, ALU.max, negate=True).then_inc(maxed, 1)

            def scales(t, u):
                s = u % 2
                dve.wait_ge(exped, t * UNITS + u + 1)
                nc.vector.reciprocal(total[:, s, :], total[:, s, :])
                dve.drain()
                for g in range(2):
                    nc.vector.tensor_scalar(prob[:, s, g, 0:2 * P], prob[:, s, g, 0:2 * P], total[:, s, g:g + 1],
                                            None, ALU.mult)
                nc.vector.tensor_tensor(end[:, s, :, 0:KEYS - 2 * P], prob[:, s, :, 2 * P:KEYS],
                                        total[:, s, :].rearrange("p (g k) -> p g k", k=1).to_broadcast([P, 2, KEYS - 2 * P]),
                                        ALU.mult).then_inc(scaled, 1)

            def join(t, u):
                b, s = u // 2, u % 2
                rows = slice(64 * s, 64 * s + 64)
                dve.wait_ge(mixed, (t + 1) * UNITS + u + 1)
                nc.vector.tensor_tensor(picked[rows, :, :], mix(s).rearrange("p (h n) -> p h n", h=G),
                                        core.c("head4")[rows, :].rearrange("p (h n) -> p h n", n=1).to_broadcast(
                                            [64, G, SEQ]), ALU.mult)
                dve.drain()
                nc.vector.tensor_reduce(attnT[rows, b * SEQ:(b + 1) * SEQ],
                                        picked[rows, :, :].rearrange("p h n -> p n h"), X, ALU.add).then_inc(joined, 1)

            def tile(t, last):
                for u in range(UNITS):
                    s = u % 2
                    dve.wait_ge(turned, t * UNITS + u + 1)
                    nc.vector.tensor_copy(endT[:, s, :], turned_end(s)).then_inc(endT_done, 1)
                    if ahead(t, u, last, 1):
                        scales(*ahead(t, u, last, 1))
                    if ahead(t, u, last, 2):
                        maxes(*ahead(t, u, last, 2))
                    join(t, u)
                dve.wait_ge(out_done, t + 1)
                add_to_x(core, t, OUT).then_inc(tile_done, 1)

            maxes(0, 0)
            maxes(0, 1)
            scales(0, 0)
            over_tiles(dve, tile)

        @block.tensor
        def _(pe):
            def score(t, u):
                b, s = u // 2, u % 2
                if s == 0:
                    pe.wait_ge(ctx_in[b], (t + 1) * 16 * 6)
                    pe.wait_ge(prepared, t * BT + b + 1)
                for g in range(2):
                    h = 8 * s + 4 * g
                    ins = nc.tensor.matmul(scores(s)[:, g, :], q_bd[:, b, h:h + 4, :].rearrange("p j w -> p (j w)"),
                                           k_all[:, b, :], start=True, stop=True)
                ins.then_inc(scored, 1)

            def tile(t, last):
                n = t * UNITS
                for u in range(UNITS):
                    b, s = u // 2, u % 2
                    pe.wait_ge(scaled, n + u + 1)
                    for g in range(2):
                        for k in range(2):
                            nc.tensor.transpose(turned_bank(s)[:, k, g, :], prob[:, s, g, k * P:(k + 1) * P], core.c("ident"))
                    if u == 1:
                        pe.wait_ge(tile_done, t + 1)
                    if u >= 2:
                        pe.wait_ge(joined, n + u - 1)
                    nc.tensor.transpose(turned_end(s), end[:, s, :, :].rearrange("p g k -> p (g k)"),
                                        core.c("ident")).then_inc(turned, 1)
                    if ahead(t, u, last, 2):
                        score(*ahead(t, u, last, 2))
                    pe.wait_ge(probT_done, n + u + 1)
                    pe.wait_ge(endT_done, n + u + 1)
                    for g in range(2):
                        rows = mix(s)[32 * g:32 * g + 32, :]
                        for k in range(2):
                            nc.tensor.matmul(rows, v_all[:, b, k, 32 * (2 * s + g):32 * (2 * s + g) + 32],
                                             probT[:, s, k, g, :], start=(k == 0), stop=False)
                    nc.tensor.matmul(mix(s), v_end[:, b, s, :, :].rearrange("p g j -> p (g j)"), endT[:, s, :],
                                     start=False, stop=True).then_inc(mixed, 1)
                pe.wait_ge(joined, n + UNITS)
                nc.tensor.matmul(OUT, attnT[:, :], w_proj[:, :], start=True, stop=False)
                nc.tensor.matmul(OUT, core.ones[0:1, :], b_proj[:, :], start=False, stop=True).then_inc(out_done, 1)

            pe.sem_inc(mixed, UNITS)
            pe.sem_inc(tile_done, 1)
            pe.wait_ge(w_in, 48)
            score(0, 0)
            score(0, 1)
            over_tiles(pe, tile)


def own_qkv(core, name, qT, kT, v, scale, w_in, w_proj, b_proj):
    nc, dram = core.nc, core.dram
    S, U = 8, 2
    with ExitStack() as st:
        w = st.enter_context(nc.sbuf_tensor(f"{name}_w", [D, 3 * D], F32))
        front = Front(core, st, name, S, lambda s: core.psum[:, s // 4, s % 4 * P:s % 4 * P + P], pack=4)
        made, q_done, kv_done = (core.sem(f"{name}_own_{n}") for n in ("made", "q_done", "kv_done"))
        block = st.enter_context(nc.Block())

        @block.sync
        def _(sp):
            load(sp, [(w[:, :], dram[f"{name}_w_qkv_T"]), (w_proj[:, :], dram[f"{name}_w_proj_T"]),
                      (b_proj[:, :], dram[f"{name}_b_proj"])], w_in)

        @block.gpsimd
        def _(pool):
            with pool.Fori(0, TILES // S) as it:
                front.pool_rstd(pool, it * S)

        tiles = lambda t: t.rearrange("p (t w) -> p t w", w=P)

        @block.scalar
        def _(act):
            with act.Fori(0, TILES // S) as it:
                front.act_copy(act, it * S)
                for u in range(U):
                    act.wait_ge(made, it * U + u + 1)
                    nc.scalar.activation(qT[:, ds(it * S + 4 * u, 4), :], tiles(core.psum[:, 2 + u, :]), ACT.Copy,
                                         scale=scale).then_inc(q_done, 1)

        @block.vector
        def _(dve):
            with dve.Fori(0, TILES // S) as it:
                front.dve_moments(dve, it * S)
                front.dve_normalise(dve, it * S)
                for u in range(U):
                    dve.wait_ge(made, it * U + u + 1)
                    nc.vector.tensor_copy(kT[:, ds(it * S + 4 * u, 4), :], tiles(core.psum[:, 4 + u, :]))
                    nc.vector.tensor_copy(v[:, ds(it * S + 4 * u, 4), :], tiles(core.psum[:, 6 + u, :])).then_inc(kv_done, 1)

        @block.tensor
        def _(pe):
            pe.wait_ge(w_in, 48)
            pe.sem_inc(q_done, U)
            with pe.Fori(0, TILES // S) as it:
                front.pe_transpose(pe, it * S)
                for u in range(U):
                    xnT = front.xnT[:, 4 * u:4 * u + 4, :].rearrange("p s w -> p (s w)")
                    pe.wait_ge(front.xnT_done, it * S + 4 * u + 4)
                    pe.wait_ge(q_done, it * U + u + 1)
                    nc.tensor.matmul(core.psum[:, 2 + u, :], w[:, 0:D], xnT, start=True, stop=True)
                    nc.tensor.matmul(core.psum[:, 4 + u, :], w[:, D:2 * D], xnT, start=True, stop=True)
                    for s in range(4):
                        last = nc.tensor.matmul(core.psum[:, 6 + u, s * P:(s + 1) * P], front.xnT[:, 4 * u + s, :],
                                                w[:, 2 * D:3 * D], start=True, stop=True)
                    last.then_inc(made, 1)


def gated_scan(core, name):
    nc, dram = core.nc, core.dram
    V, W, C, N = 2, 4, 2, 512
    S = V * W
    R = 16
    with ExitStack() as st:
        sb = lambda n, shape, dt=F32: st.enter_context(nc.sbuf_tensor(f"{name}_{n}", shape, dt))
        w_in = sb("w_in", [D, 2 * C, P])
        w_x = sb("w_x", [P, C, 2 * R])
        w_dt = sb("w_dt", [2 * R, C, P])
        w_bp = sb("w_bp", [2 * R, C, P])
        w_out = sb("w_out", [P, C, D])
        taps = sb("taps", [P, C, 4])
        b_dt = sb("b_dt", [P, C])
        skip = sb("skip", [P, C])
        conv = sb("conv", [P, V, C, N])
        u = sb("u", [P, V, C, N])
        z = sb("z", [P, V, C, N])
        low = sb("low", [2 * R, V, N])
        soft = sb("soft", [P, V, C, N])
        dt = sb("dt", [P, V, C, N])
        ub = sb("ub", [P, V, C, N])
        y = sb("y", [P, V, C, N])
        bank = lambda v, k: core.psum[:, 4 * v + k, :]
        in_bank = (1, 2, 3, 0)
        b_bank = (3, 0)
        front = Front(core, st, name, S, lambda s: bank(s // W, 0)[:, s % W * P:(s % W + 1) * P], transposed=False)
        xnT = sb("xnT", [D, V, N])
        (wts_in, zeroed, in_done, conv_first, conv_done, u_done, low_made, low_done, dt_made, b_made, soft_done, y_done,
         out_done) = (core.sem(f"{name}_{n}") for n in (
             "wts_in", "zeroed", "in_done", "conv_first", "conv_done", "u_done", "low_made", "low_done", "dt_made",
             "b_made", "soft_done", "y_done", "out_done"))
        z_made, z_out, dt_read, added = (core.sem(f"{name}_{n}") for n in ("z_made", "z_out", "dt_read", "added"))
        block = st.enter_context(nc.Block())
        seqs = lambda t: t.rearrange("p (b t) -> p b t", t=SEQ)
        STEPS = TILES // S

        @block.sync
        def _(sp):
            sp.wait_ge(zeroed, 1)
            load(sp, [(w_in[:, :, :], dram[f"{name}_W_in"]), (w_x[:, :, :], dram[f"{name}_W_x"]),
                      (w_dt[0:R, :, :], dram[f"{name}_W_dt"]), (w_bp[R:2 * R, :, :], dram[f"{name}_W_Bp"]),
                      (w_out[:, :, :], dram[f"{name}_W_out"]), (taps[:, :, :], dram[f"{name}_conv_w"]),
                      (b_dt[:, :], dram[f"{name}_b_dt"]), (skip[:, :], dram[f"{name}_D_param"])], wts_in)

        @block.gpsimd
        def _(pool):
            nc.gpsimd.memset(w_dt[:, :, :], 0.0)
            nc.gpsimd.memset(w_bp[:, :, :], 0.0).then_inc(zeroed, 1)
            with pool.Fori(0, STEPS) as it:
                front.pool_rstd(pool, it * S)

        @block.scalar
        def _(act):
            act.wait_ge(wts_in, 128)
            with act.Fori(0, STEPS) as it:
                for v in range(V):
                    act.wait_ge(front.turned, it * S + (v + 1) * W)
                    nc.scalar.copy(xnT[:, v, :], bank(v, 0)).then_inc(front.xnT_done, 1)
                n = it * V * C
                for v in range(V):
                    for c in range(C):
                        act.wait_ge(in_done, n + v * C + c + 1)
                        nc.scalar.activation(conv[:, v, c, :], bank(v, 1 + c), ACT.Copy,
                                             scale=taps[:, c, 3:4]).then_inc(conv_first, 1)
                for v in range(V):
                    act.wait_ge(z_made, it * V + v + 1)
                    for c in range(C):
                        ins = nc.scalar.activation(z[:, v, c, :], bank(v, in_bank[C + c]), ACT.Silu)
                    ins.then_inc(z_out, 1)
                for v in range(V):
                    for c in range(C):
                        act.wait_ge(conv_done, n + v * C + c + 1)
                        nc.scalar.activation(u[:, v, c, :], conv[:, v, c, :], ACT.Silu).then_inc(u_done, 1)
                for v in range(V):
                    act.wait_ge(low_made, it * V + v + 1)
                    nc.scalar.copy(low[:, v, :], bank(v, 0)[0:2 * R, :]).then_inc(low_done, 1)
                for v in range(V):
                    for c in range(C):
                        act.wait_ge(dt_read, n + v * C + c + 1)
                        nc.scalar.activation(soft[:, v, c, :], bank(v, 1 + c), ACT.Abs, bias=b_dt[:, c:c + 1])
                act.drain()
                for v in range(V):
                    nc.scalar.activation(soft[:, v, :, :], soft[:, v, :, :], ACT.Exp, scale=-1.0)
                act.drain()
                for v in range(V):
                    nc.scalar.activation(soft[:, v, :, :], soft[:, v, :, :], ACT.Ln, bias=1.0).then_inc(soft_done, 1)

        @block.vector
        def _(dve):
            dve.wait_ge(wts_in, 128)
            def step(it, more):
                n = it * V * C
                for v in range(V):
                    for tap in range(3):
                        lag = 3 - tap
                        for c in range(C):
                            if tap == 0:
                                dve.wait_ge(conv_first, n + v * C + c + 1)
                            nc.vector.scalar_tensor_tensor(
                                seqs(conv[:, v, c, :])[:, :, lag:], seqs(bank(v, 1 + c))[:, :, 0:SEQ - lag],
                                taps[:, c, tap:tap + 1], seqs(conv[:, v, c, :])[:, :, lag:], ALU.mult, ALU.add)
                        dve.drain()
                    dve.sem_inc(conv_done, C)
                for v in range(V):
                    for c in range(C):
                        dve.wait_ge(dt_made, n + v * C + c + 1)
                        nc.vector.tensor_scalar(dt[:, v, c, :], bank(v, 1 + c), b_dt[:, c:c + 1], 0.0,
                                                ALU.add, ALU.max).then_inc(dt_read, 1)
                    for c in range(C):
                        dve.wait_ge(b_made, n + v * C + c + 1)
                        nc.vector.tensor_tensor(ub[:, v, c, :], u[:, v, c, :], bank(v, b_bank[c]), ALU.mult)
                    dve.drain()
                if more:
                    front.dve_moments(dve, (it + 1) * S)
                    front.dve_normalise(dve, (it + 1) * S)
                for v in range(V):
                    dve.wait_ge(soft_done, it * V + v + 1)
                    nc.vector.tensor_tensor(dt[:, v, :, :], dt[:, v, :, :], soft[:, v, :, :], ALU.add)
                    dve.drain()
                    nc.vector.tensor_scalar(dt[:, v, :, :], dt[:, v, :, :], 1e-4, 1.0, ALU.max, ALU.min)
                    dve.drain()
                    nc.vector.tensor_scalar(dt[:, v, :, :], dt[:, v, :, :], -1.0, 1.0, ALU.mult, ALU.add)
                    dve.drain()
                    nc.vector.memset(dt[:, v, :, :].rearrange("p c (b t) -> p (c b) t", t=SEQ)[:, :, 0:1], 0.0)
                    dve.drain()
                    for c in range(C):
                        nc.vector.tensor_tensor_scan(y[:, v, c, :], dt[:, v, c, :], ub[:, v, c, :], 0.0, ALU.mult, ALU.add)
                    dve.drain()
                    for c in range(C):
                        nc.vector.scalar_tensor_tensor(y[:, v, c, :], u[:, v, c, :], skip[:, c:c + 1], y[:, v, c, :],
                                                       ALU.mult, ALU.add)
                    dve.drain()
                    nc.vector.tensor_tensor(y[:, v, :, :], y[:, v, :, :], z[:, v, :, :], ALU.mult).then_inc(y_done, 1)
                for v in range(V):
                    dve.wait_ge(out_done, it * V + v + 1)
                    x = core.x[:, ds(it * S + v * W, W), :]
                    nc.vector.tensor_tensor(x, x, bank(v, 3).rearrange("p (t w) -> p t w", w=D),
                                            ALU.add).then_inc(added, 1)

            front.dve_moments(dve, 0)
            front.dve_normalise(dve, 0)
            over_steps(dve, STEPS, step)

        @block.tensor
        def _(pe):
            pe.wait_ge(wts_in, 128)
            pe.sem_inc(added, V)
            with pe.Fori(0, STEPS) as it:
                n = it * V * C
                front.pe_transpose(pe, it * S)
                for v in range(V):
                    pe.wait_ge(added, it * V + v + 1)
                    pe.wait_ge(front.xnT_done, it * V + v + 1)
                    for m in range(2 * C):
                        ins = nc.tensor.matmul(bank(v, in_bank[m]), w_in[:, m, :], xnT[:, v, :], start=True, stop=True)
                        if m < C:
                            ins.then_inc(in_done, 1)
                    ins.then_inc(z_made, 1)
                for v in range(V):
                    pe.wait_ge(z_out, it * V + v + 1)
                    pe.wait_ge(u_done, n + v * C + C)
                    for c in range(C):
                        last = nc.tensor.matmul(bank(v, 0)[0:2 * R, :], w_x[:, c, :], u[:, v, c, :], start=(c == 0),
                                                stop=(c == C - 1))
                    last.then_inc(low_made, 1)
                for v in range(V):
                    pe.wait_ge(low_done, it * V + v + 1)
                    for c in range(C):
                        nc.tensor.matmul(bank(v, 1 + c), w_dt[:, c, :], low[:, v, :], start=True,
                                         stop=True).then_inc(dt_made, 1)
                    for c in range(C):
                        nc.tensor.matmul(bank(v, b_bank[c]), w_bp[:, c, :], low[:, v, :], start=True,
                                         stop=True).then_inc(b_made, 1)
                for v in range(V):
                    pe.wait_ge(y_done, it * V + v + 1)
                    for t in range(W):
                        for c in range(C):
                            last = nc.tensor.matmul(bank(v, 3)[:, t * P:(t + 1) * P], y[:, v, c, t * P:(t + 1) * P],
                                                    w_out[:, c, :], start=(c == 0), stop=(c == C - 1))
                    last.then_inc(out_done, 1)


def ternary_ffn(core, name):
    nc, dram = core.nc, core.dram
    S, H = 4, 512
    C = H // P
    with ExitStack() as st:
        sb = lambda n, shape, dt=F32: st.enter_context(nc.sbuf_tensor(f"{name}_{n}", shape, dt))
        w_fc = sb("w_fc", [D, H])
        w_proj = sb("w_proj", [P, C, D])
        ln_w = sb("ln_w", [P, C])
        ln_b = sb("ln_b", [P, C])
        row = sb("row", [1, D])
        mass = sb("mass", [P, 2])
        limit = sb("limit", [P, 2, 2])
        low = sb("low", [P, H])
        h = sb("h", [P, S, H])
        hT = sb("hT", [P, S, C, P])
        h_stats, h_mv = sb("h_stats", [P, S, 6]), sb("h_mv", [P, S, 2])
        h_var, h_rstd = sb("h_var", [P, S, 1]), sb("h_rstd", [P, S, 1])
        bank_a = lambda s: core.psum[:, 2 * s, :]
        bank_b = lambda s: core.psum[:, 2 * s + 1, :]
        front = Front(core, st, name, S, bank_a)
        (w_in, masses, summed, w_done, row_made, row_done, wide, gelued, h_moments, h_rstd_done, h_normed, turned,
         hT_done, out_done, added) = (core.sem(f"{name}_{n}") for n in (
             "w_in", "masses", "summed", "w_done", "row_made", "row_done", "wide", "gelued", "h_moments",
             "h_rstd_done", "h_normed", "turned", "hT_done", "out_done", "added"))
        block = st.enter_context(nc.Block())

        @block.sync
        def _(sp):
            load(sp, [(w_fc[:, :], dram[f"{name}_W_fc_T"]), (w_proj[:, :, :], dram[f"{name}_W_proj_T"]),
                      (ln_w[:, :], dram[f"{name}_ln_w"]), (ln_b[:, :], dram[f"{name}_ln_b"])], w_in)

        @block.gpsimd
        def _(pool):
            def step(it, more):
                n = it * S
                for s in range(S):
                    pool.wait_ge(h_moments, n + s + 1)
                    nc.gpsimd.tensor_tensor(h_var[:, s, :], h_mv[:, s, 1:2], core.eps[:, :], ALU.add)
                pool.drain()
                for s in range(S):
                    nc.gpsimd.tensor_tensor(h_rstd[:, s, :], h_var[:, s, :], core.half[:, :],
                                            ALU.pow).then_inc(h_rstd_done, 1)
                if more:
                    front.pool_rstd(pool, n + S)

            front.pool_rstd(pool, 0)
            over_steps(pool, TILES // S, step)

        @block.scalar
        def _(act):
            act.wait_ge(row_made, 1)
            nc.scalar.copy(row[:, :], core.psum[0:1, 6, 0:D]).then_inc(row_done, 1)
            with act.Fori(0, TILES // S) as it:
                n = it * S
                front.act_copy(act, n)
                for s in range(S):
                    act.wait_ge(wide, n + s + 1)
                    nc.scalar.activation(h[:, s, :], bank_b(s), ACT.Gelu).then_inc(gelued, 1)
                for s in range(S):
                    act.wait_ge(turned, n + s + 1)
                    nc.scalar.copy(hT[:, s, :, :], bank_a(s).rearrange("p (c w) -> p c w", c=C)).then_inc(hT_done, 1)

        @block.vector
        def _(dve):
            dve.wait_ge(w_in, 64)
            nc.vector.tensor_reduce(mass[:, 0:1], w_fc[:, :], X, ALU.add, apply_absolute_value=True)
            nc.vector.tensor_reduce(mass[:, 1:2], w_proj[:, :, :], XY, ALU.add,
                                    apply_absolute_value=True).then_inc(masses, 1)
            dve.wait_ge(summed, 1)
            nc.vector.tensor_scalar(limit[:, 0, :], core.psum[:, 7, 0:2], 1.0 / (H * D), 1e-6, ALU.mult, ALU.add)
            dve.drain()
            nc.vector.tensor_scalar(limit[:, 1, :], limit[:, 0, :], -0.5, None, ALU.mult)
            dve.drain()
            nc.vector.tensor_scalar(limit[:, 0, :], limit[:, 0, :], 0.5, None, ALU.mult)
            for i, w in enumerate((w_fc[:, :], w_proj[:, :, :].rearrange("p c d -> p (c d)"))):
                dve.drain()
                nc.vector.tensor_scalar(low[:, :], w, limit[:, 1, i:i + 1], None, ALU.is_lt)
                dve.drain()
                nc.vector.scalar_tensor_tensor(w, w, limit[:, 0, i:i + 1], low[:, :], ALU.is_gt,
                                               ALU.subtract).then_inc(w_done, 1)
            dve.wait_ge(row_made, 1)
            for c in range(C):
                nc.vector.tensor_scalar(w_proj[:, c, :], w_proj[:, c, :], ln_w[:, c:c + 1], None,
                                        ALU.mult).then_inc(w_done, 1)
            def step(it, more):
                n = it * S
                for s in range(S):
                    dve.wait_ge(gelued, n + s + 1)
                    nc.vector.bn_stats(h_stats[:, s, :], h[:, s, :])
                dve.drain()
                for s in range(S):
                    nc.vector.bn_aggr(h_mv[:, s, :], h_stats[:, s, :]).then_inc(h_moments, 1)
                for s in range(S):
                    dve.wait_ge(h_rstd_done, n + s + 1)
                    nc.vector.tensor_scalar(h[:, s, :], h[:, s, :], h_mv[:, s, 0:1], h_rstd[:, s, :], ALU.subtract,
                                            ALU.mult).then_inc(h_normed, 1)
                if more:
                    front.dve_moments(dve, n + S)
                    front.dve_normalise(dve, n + S)
                for s in range(S):
                    dve.wait_ge(out_done, n + s + 1)
                    add_to_x(core, n + s, bank_b(s)[:, 0:D]).then_inc(added, 1)

            front.dve_moments(dve, 0)
            front.dve_normalise(dve, 0)
            over_steps(dve, TILES // S, step)

        @block.tensor
        def _(pe):
            pe.wait_ge(masses, 1)
            nc.tensor.matmul(core.psum[:, 7, 0:2], core.ones[:, :], mass[:, :], start=True, stop=True).then_inc(summed, 1)
            pe.wait_ge(w_done, 2)
            for c in range(C):
                last = nc.tensor.matmul(core.psum[0:1, 6, 0:D], ln_b[:, c:c + 1], w_proj[:, c, :], start=(c == 0),
                                        stop=(c == C - 1))
            last.then_inc(row_made, 1)
            pe.wait_ge(w_done, 2 + C)
            pe.sem_inc(added, S)
            pe.wait_ge(row_done, 1)
            with pe.Fori(0, TILES // S) as it:
                n = it * S
                front.pe_transpose(pe, n)
                for s in range(S):
                    pe.wait_ge(added, n + s + 1)
                    pe.wait_ge(front.xnT_done, n + s + 1)
                    nc.tensor.matmul(bank_b(s), front.xnT[:, s, :], w_fc[:, :], start=True, stop=True).then_inc(wide, 1)
                for s in range(S):
                    pe.wait_ge(h_normed, n + s + 1)
                    for c in range(C):
                        last = nc.tensor.transpose(bank_a(s)[:, c * P:(c + 1) * P], h[:, s, c * P:(c + 1) * P],
                                                   core.c("ident"))
                    last.then_inc(turned, 1)
                for s in range(S):
                    pe.wait_ge(hT_done, n + s + 1)
                    for c in range(C):
                        nc.tensor.matmul(bank_b(s)[:, 0:D], hT[:, s, c, :], w_proj[:, c, :], start=(c == 0), stop=False)
                    nc.tensor.matmul(bank_b(s)[:, 0:D], core.ones[0:1, :], row[:, :], start=False,
                                     stop=True).then_inc(out_done, 1)


def wide_context_attention(core, name):
    with ExitStack() as outer:
        keep = lambda n, shape, dt=F32: outer.enter_context(core.nc.sbuf_tensor(f"{name}_{n}", shape, dt))
        m_h = keep("m_h", [D, HEADS, CD])
        u_h = keep("u_h", [P, 2, HEADS, D])
        w_null = keep("w_null", [D, HEADS])
        v_null = keep("v_null", [HEADS, D])
        xnT = keep("xnT", [D, TILES, P])
        last_rows = core.nc.dram_tensor(f"{name}_last_rows", (B, 2, 2, G, D), F32).ap()
        fold_weights(core, name, m_h, u_h, w_null, v_null, last_rows)
        transposed_tokens(core, name, xnT)
        wide_attention(core, name, outer, m_h, u_h, w_null, v_null, last_rows, xnT)


def fold_weights(core, name, m_h, u_h, w_null, v_null, last_rows):
    nc, dram = core.nc, core.dram
    F = 64
    with ExitStack() as st:
        sb = lambda n, shape, dt=F32: st.enter_context(nc.sbuf_tensor(f"{name}_{n}", shape, dt))
        wq, wk, wv, wo = sb("wq", [F, HEADS, D]), sb("wk", [F, HEADS, CD]), sb("wv", [F, HEADS, CD]), sb("wo", [F, HEADS, D])
        null = sb("null", [F, 2])
        diag = sb("diag", [F, HEADS * HEADS])
        ctx_last = sb("ctx_last", [P, 2, B])
        rows = sb("rows", [B, HEADS, D])
        rows_made, rows_done, rows_out = (core.sem(f"{name}_{n}") for n in ("rows_made", "rows_done", "rows_out"))
        qk_in, vo_in, diag_done, m_made, m_out, u_made, u_out, null_made = (core.sem(f"{name}_{n}") for n in (
            "qk_in", "vo_in", "diag_done", "m_made", "m_out", "u_made", "u_out", "null_made"))
        block = st.enter_context(nc.Block())

        @block.sync
        def _(sp):
            load(sp, [(wq[:, :, :], dram[f"{name}_WqT"]), (wk[:, :, :], dram[f"{name}_WkT"]),
                      (null[:, :], dram[f"{name}_null_kv_T"]), (ctx_last[:, :, :], dram[f"{name}_ctx_last_T"])], qk_in)
            sp.wait_ge(rows_done, 4)
            for s in range(2):
                for g in range(2):
                    h = 8 * s + 4 * g
                    sp.dma_start(last_rows[:, g, s, :, :], rows[:, h:h + 4, :]).then_inc(rows_out, 16)
            sp.wait_ge(rows_out, 64)

        @block.scalar
        def _(act):
            load(act, [(wv[:, :, :], dram[f"{name}_WvT"]), (wo[:, :, :], dram[f"{name}_Wo"])], vo_in)
            for k in range(8):
                act.wait_ge(m_made, k + 1)
                nc.scalar.activation(m_h[:, 2 * k:2 * k + 2, :], core.psum[:, k, :].rearrange("p (h c) -> p h c", h=2),
                                     ACT.Copy, scale=F ** -0.5).then_inc(m_out, 1)
            act.wait_ge(null_made, 1)
            nc.scalar.activation(w_null[:, :], core.psum[:, 0, 0:HEADS], ACT.Copy, scale=F ** -0.5)
            nc.scalar.copy(v_null[:, :], core.psum[0:HEADS, 0, P:2 * P])

        @block.vector
        def _(dve):
            nc.vector.memset(diag[:, :], 0.0)
            dve.drain()
            dve.wait_ge(qk_in, 64)
            for s in range(2):
                for g in range(2):
                    first = (8 * s + 4 * g) * HEADS + 8 * g + 4 * s
                    nc.vector.tensor_copy(diag[:, first:first + 3 * (HEADS + 1) + 1:HEADS + 1],
                                          null[:, 1:2].to_broadcast([F, G])).then_inc(diag_done, 1)
            for k in range(8):
                dve.wait_ge(u_made, k + 1)
                nc.vector.tensor_copy(u_h[:, k // 4, k % 4 * 4:k % 4 * 4 + 4, :],
                                      core.psum[:, k, :].rearrange("p (h e) -> p h e", h=4)).then_inc(u_out, 1)
            for k in range(4):
                dve.wait_ge(rows_made, k + 1)
                nc.vector.tensor_copy(rows[:, 4 * k:4 * k + 4, :],
                                      core.psum[:, 4 + k, :].rearrange("p (h e) -> p h e", h=4)).then_inc(rows_done, 1)

        @block.tensor
        def _(pe):
            pe.wait_ge(qk_in, 64)
            for k in range(8):
                for i in range(2):
                    last = nc.tensor.matmul(core.psum[:, k, i * CD:(i + 1) * CD], wq[:, 2 * k + i, :], wk[:, 2 * k + i, :],
                                            start=True, stop=True)
                last.then_inc(m_made, 1)
            pe.wait_ge(vo_in, 32)
            for k in range(8):
                c, h = k // 4, k % 4 * 4
                pe.wait_ge(m_out, k + 1)
                for i in range(4):
                    last = nc.tensor.matmul(core.psum[:, k, i * D:(i + 1) * D], wv[:, h + i, c * P:(c + 1) * P],
                                            wo[:, h + i, :], start=True, stop=True)
                last.then_inc(u_made, 1)
            pe.wait_ge(u_out, 1)
            for h in range(HEADS):
                nc.tensor.matmul(core.psum[:, 0, h:h + 1], wq[:, h, :], null[:, 0:1], start=True, stop=True)
            pe.wait_ge(diag_done, 4)
            for h in range(HEADS):
                last = nc.tensor.matmul(core.psum[0:HEADS, 0, P:2 * P], diag[:, h * HEADS:(h + 1) * HEADS], wo[:, h, :],
                                        start=(h == 0), stop=(h == HEADS - 1))
            last.then_inc(null_made, 1)
            pe.wait_ge(u_out, 8)
            for k in range(4):
                for c in range(2):
                    last = nc.tensor.matmul(core.psum[:, 4 + k, :], ctx_last[:, c, :],
                                            u_h[:, c, 4 * k:4 * k + 4, :].rearrange("p h e -> p (h e)"),
                                            start=(c == 0), stop=(c == 1))
                last.then_inc(rows_made, 1)


def transposed_tokens(core, name, xnT):
    nc = core.nc
    S, U = 8, 2
    with ExitStack() as st:
        front = Front(core, st, name, S, lambda s: core.psum[:, s // 4, s % 4 * P:s % 4 * P + P], transposed=False, pack=4)
        block = st.enter_context(nc.Block())

        @block.gpsimd
        def _(pool):
            with pool.Fori(0, TILES // S) as it:
                front.pool_rstd(pool, it * S)

        @block.scalar
        def _(act):
            with act.Fori(0, TILES // S) as it:
                for u in range(U):
                    act.wait_ge(front.turned, it * S + 4 * u + 4)
                    nc.scalar.copy(xnT[:, ds(it * S + 4 * u, 4), :],
                                   core.psum[:, u, :].rearrange("p (s w) -> p s w", w=P)).then_inc(front.xnT_done, 4)

        @block.vector
        def _(dve):
            with dve.Fori(0, TILES // S) as it:
                front.dve_moments(dve, it * S)
                dve.wait_ge(front.xnT_done, it * S + S)
                front.dve_normalise(dve, it * S)

        @block.tensor
        def _(pe):
            pe.sem_inc(front.xnT_done, S)
            with pe.Fori(0, TILES // S) as it:
                pe.wait_ge(front.xnT_done, it * S + S)
                front.pe_transpose(pe, it * S)


def wide_attention(core, name, st, m_h, u_h, w_null, v_null, last_rows, xnT):
    nc, dram = core.nc, core.dram
    KEYS = CTX + 1
    LN2_EPS = 1e-6
    UNITS = 2 * BT
    TAIL = (BT + 1) * HEADS
    sb = lambda n, shape, dt=F32: st.enter_context(nc.sbuf_tensor(f"{name}_{n}", shape, dt))
    ctxT = sb("ctxT", [P, BT, 2, CTX])
    ctx = sb("ctx", [P, BT, 2, CD])
    q_ctx = sb("q_ctx", [P, 2, 2, BT, HEADS, SEQ])
    null = sb("null_scores", [HEADS, 2, P])
    null_bd = sb("null_bd", [HEADS, 2, HEADS, SEQ])
    prob = sb("prob", [P, 2, 2, KEYS])
    tail = sb("tail", [P, 2, 4])
    nmax = sb("nmax", [P, 2, 2])
    total = sb("total", [P, 2, 2])
    probT = sb("probT", [P, 2, 2, 2 * P])
    lastT = sb("lastT", [4, 2 * G, BT, SEQ])
    tailT = sb("tailT", [TAIL, P])
    tail_w = sb("tail_w", [TAIL, D])
    mixed_ctx = sb("mixed_ctx", [P, 2, HEADS, P])
    z = sb("z", [P, D])
    z_stats, z_mv, z_var = sb("z_stats", [P, 6]), sb("z_mv", [P, 2]), sb("z_var", [P, 2])
    z_eps = sb("z_eps", [P, 1])
    ln_scale, ln_bias = sb("ln_scale", [P, D]), sb("ln_bias", [P, D])
    scores = lambda s: core.psum[:, 2 * s:2 * s + 2, 0:KEYS]
    TURNED, MIX, Q = core.psum[:, 4, :], core.psum[:, 5, :], core.psum[:, 6, :]
    OUT = core.psum[:, 7, 0:D]
    TURNED_TAIL = core.psum[0:4, 7, P:2 * P]
    NULL = core.psum[0:HEADS, 7, 2 * P:3 * P]
    ctx_in = [core.sem(f"{name}_ctx_in{b}") for b in range(BT)]
    (ln_in, zeroed, q_made, q_out, null_made, null_out, null_ready, scored, maxed, exped, scaled, turned, probT_done,
     lastT_done, mixed, mix_out, tail_in, out_done, z_copied, z_done, z_used) = (core.sem(f"{name}_{n}") for n in (
         "ln_in", "zeroed", "q_made", "q_out", "null_q_made", "null_q_out", "null_ready", "scored", "maxed", "exped",
         "scaled", "turned", "probT_done", "lastT_done", "mixed", "mix_out", "tail_in", "out_done", "z_copied",
         "z_done", "z_used"))
    block = st.enter_context(nc.Block())
    Q_STEPS = {0: (0, 1), 1: (2, 3), 2: (4,), 3: (5,), 4: (6,), 5: (7,)}
    NULL_STEP = 3
    TAIL_DMAS = BT + 2

    def over_tiles(eng, tile):
        tile(0, 0, False, True)
        with eng.Fori(0, TILES // 2 - 1) as it:
            tile(1 + 2 * it, 1, True, True)
            tile(2 + 2 * it, 0, True, True)
        tile(TILES - 1, 1, True, False)

    def ahead(t, u, after, by):
        return (t, u + by) if u + by < UNITS else (t + 1, u + by - UNITS) if after else None

    def q_bank(p, k):
        c, j = k // 4, k % 4
        return q_ctx[:, p, c, :, 4 * j:4 * j + 4, :], Q.rearrange("p (h b n) -> p b h n", h=4, b=BT)

    @block.sync
    def _(sp):
        load(sp, [(ln_scale[:, :], dram[f"{name}_ln_scale"].to_broadcast([P, D])),
                  (ln_bias[:, :], dram[f"{name}_ln_bias"].to_broadcast([P, D])),
                  (tail_w[BT * HEADS:TAIL, :], v_null[:, :])], ln_in)

        def load_ctx(t, b):
            sp.wait_ge(mixed, t * UNITS + 2 * b + 2)
            seq = t * BT + b
            row = dram["ctx_2048"][ds(seq, 1), :, :].rearrange("a m c -> (a m) c")
            for dst, src in ((ctxT[:, b, :, :], dram["ctx_T"][ds(seq, 1), :, :].rearrange("a (k c) m -> c (a k) m", c=P)),
                             (ctx[:, b, :, :], row[0:2 * P, :].rearrange("(k m) c -> m k c", m=P))):
                sp.dma_start(dst, src).then_inc(ctx_in[b], 16)

        def send_tail(t):
            sp.wait_ge(out_done, t + 1)
            sp.dma_start(tail_w[0:BT * HEADS, :],
                         last_rows[ds(t * BT, BT), :, :, :, :].rearrange("b g s h e -> (b g s h) e")).then_inc(tail_in, 16)
            sp.wait_ge(lastT_done, (t + 1) * UNITS)
            for b in range(BT):
                sp.dma_start(tailT[b * HEADS:(b + 1) * HEADS, b * SEQ:(b + 1) * SEQ],
                             lastT[0:4:2, :, b, :]).then_inc(tail_in, 16)
            sp.dma_start(tailT[BT * HEADS:TAIL, :],
                         lastT[1:4:2, :, :, :]).then_inc(tail_in, 16)

        for b in range(BT):
            load_ctx(0, b)
        sp.wait_ge(zeroed, 1)
        with sp.Fori(0, TILES - 1) as t:
            for b in range(BT - 1):
                load_ctx(t + 1, b)
            send_tail(t)
            load_ctx(t + 1, BT - 1)
        send_tail(TILES - 1)

    @block.gpsimd
    def _(pool):
        def spread_null(t, p, b):
            pool.wait_ge(null_out, t + 1)
            pool.wait_ge(scored, t * UNITS + 2 * b + 2)
            a = null[:, p:p + 1, b * SEQ:(b + 1) * SEQ].to_broadcast([HEADS, HEADS, SEQ])
            m = core.c("ident")[0:HEADS, 0:HEADS].rearrange("p (h n) -> p h n", n=1).to_broadcast([HEADS, HEADS, SEQ])
            nc.gpsimd.tensor_tensor(null_bd[:, b % 2, :, :], a, m, ALU.mult).then_inc(null_ready, 1)

        def add_normalised(t):
            pool.wait_ge(z_done, t + 1)
            nc.gpsimd.tensor_tensor(z_var[:, 0:1], z_mv[:, 1:2], z_eps[:, :], ALU.add)
            pool.drain()
            nc.gpsimd.tensor_tensor(z_var[:, 1:2], z_var[:, 0:1], core.half[:, :], ALU.pow)
            pool.drain()
            nc.gpsimd.tensor_scalar(z[:, :], z[:, :], z_mv[:, 0:1], z_var[:, 1:2], ALU.subtract, ALU.mult)
            pool.drain()
            nc.gpsimd.tensor_tensor(z[:, :], z[:, :], ln_scale[:, :], ALU.mult)
            pool.drain()
            nc.gpsimd.tensor_tensor(z[:, :], z[:, :], ln_bias[:, :], ALU.add)
            pool.drain()
            nc.gpsimd.tensor_tensor(core.x[:, ds(t, 1), :], core.x[:, ds(t, 1), :], z[:, :], ALU.add).then_inc(z_used, 1)

        def tile(t, p, before, after):
            for b in range(BT):
                spread_null(t, p, b)
                if before and b == 2:
                    add_normalised(t - 1)

        nc.gpsimd.memset(z_eps[:, :], LN2_EPS)
        nc.gpsimd.memset(tailT[:, :], 0.0).then_inc(zeroed, 1)
        pool.drain()
        pool.wait_ge(ln_in, 48)
        over_tiles(pool, tile)
        add_normalised(TILES - 1)

    @block.scalar
    def _(act):
        def exps(t, u):
            s = u % 2
            act.wait_ge(maxed, t * UNITS + u + 1)
            for g in range(2):
                ins = nc.scalar.activation(prob[:, s, g, :], scores(s)[:, g, :], ACT.Exp,
                                           bias=nmax[:, s, g:g + 1], accum_out=total[:, s, g:g + 1])
            ins.then_inc(exped, 1)

        def null_scores(t, p):
            act.wait_ge(null_made, t + 1)
            nc.scalar.copy(null[:, p, :], NULL).then_inc(null_out, 1)

        def tile(t, p, before, after):
            n = t * UNITS
            for u in range(UNITS):
                b, s = u // 2, u % 2
                act.wait_ge(turned, n + u + 1)
                if before and u == 0:
                    act.wait_ge(tail_in, t * 16 * TAIL_DMAS)
                nc.scalar.copy(lastT[:, s * G:(s + 1) * G, b, :],
                               TURNED_TAIL.rearrange("p (h n) -> p h n", h=G)).then_inc(lastT_done, 1)
                if ahead(t, u, after, 2):
                    exps(*ahead(t, u, after, 2))
                if after and u == NULL_STEP:
                    null_scores(t + 1, 1 - p)
                act.wait_ge(mixed, n + u + 1 + UNITS)
                nc.scalar.copy(mixed_ctx[:, :, 8 * s:8 * s + 8, b * SEQ:(b + 1) * SEQ],
                               MIX.rearrange("p (c h n) -> p c h n", c=2, h=8)).then_inc(mix_out, 1)

        null_scores(0, 0)
        exps(0, 0)
        exps(0, 1)
        over_tiles(act, tile)

    @block.vector
    def _(dve):
        def q_copy(t, p, k):
            dve.wait_ge(q_made, t * 8 + k + 1)
            nc.vector.tensor_copy(*q_bank(p, k)).then_inc(q_out, 1)

        def maxes(t, u):
            dve.wait_ge(scored, t * UNITS + u + 4 + 1)
            nc.vector.tensor_reduce(nmax[:, u % 2, :], scores(u % 2), X, ALU.max, negate=True).then_inc(maxed, 1)

        def scales(t, u):
            s = u % 2
            dve.wait_ge(exped, t * UNITS + u + 1)
            nc.vector.reciprocal(total[:, s, :], total[:, s, :])
            dve.drain()
            for g in range(2):
                nc.vector.tensor_scalar(prob[:, s, g, 0:2 * P], prob[:, s, g, 0:2 * P], total[:, s, g:g + 1], None, ALU.mult)
            nc.vector.tensor_tensor(tail[:, s, :].rearrange("p (g k) -> p g k", g=2), prob[:, s, :, 2 * P:KEYS],
                                    total[:, s, :].rearrange("p (g k) -> p g k", k=1).to_broadcast([P, 2, 2]),
                                    ALU.mult).then_inc(scaled, 1)

        def tile(t, p, before, after):
            n = t * UNITS
            for u in range(UNITS):
                s = u % 2
                dve.wait_ge(turned, n + u + 1)
                nc.vector.tensor_copy(probT[:, s, :, :], TURNED.rearrange("p (k w) -> p k w", k=2)).then_inc(probT_done, 1)
                if ahead(t, u, after, 1):
                    scales(*ahead(t, u, after, 1))
                if ahead(t, u, after, 2):
                    maxes(*ahead(t, u, after, 2))
                if before and u == 0:
                    dve.wait_ge(z_used, t)
                    dve.wait_ge(out_done, t + 1)
                    nc.vector.tensor_copy(z[:, :], OUT).then_inc(z_copied, 1)
                    dve.drain()
                    nc.vector.bn_stats(z_stats[:, :], z[:, :])
                    dve.drain()
                    nc.vector.bn_aggr(z_mv[:, :], z_stats[:, :]).then_inc(z_done, 1)
                if after:
                    for k in Q_STEPS.get(u, ()):
                        q_copy(t + 1, 1 - p, k)

        for k in range(8):
            q_copy(0, 0, k)
        maxes(0, 0)
        maxes(0, 1)
        scales(0, 0)
        over_tiles(dve, tile)
        dve.wait_ge(z_used, TILES)
        dve.wait_ge(out_done, TILES + 1)
        nc.vector.tensor_copy(z[:, :], OUT)
        dve.drain()
        nc.vector.bn_stats(z_stats[:, :], z[:, :])
        dve.drain()
        nc.vector.bn_aggr(z_mv[:, :], z_stats[:, :]).then_inc(z_done, 1)

    @block.tensor
    def _(pe):
        tokens = lambda t: xnT[:, ds(t, 1), :].rearrange("p a w -> p (a w)")

        def q_part(t, k):
            c, j = k // 4, k % 4
            pe.wait_ge(q_out, t * 8 + k + 1)
            for i in range(4):
                last = nc.tensor.matmul(Q[:, i * P:(i + 1) * P], m_h[:, 4 * j + i, c * P:(c + 1) * P], tokens(t),
                                        start=True, stop=True)
            last.then_inc(q_made, 1)

        def null_part(t):
            nc.tensor.matmul(NULL, w_null[:, :], tokens(t), start=True, stop=True).then_inc(null_made, 1)

        def score(t, u, p):
            b, s = u // 2, u % 2
            if s == 0:
                pe.wait_ge(ctx_in[b], (t + 1) * 16 * 2)
                pe.wait_ge(null_ready, t * BT + b + 1)
            if u == 0:
                pe.wait_ge(q_out, t * 8 + 9)
            for g in range(2):
                h = 8 * s + 4 * g
                for c in range(2):
                    nc.tensor.matmul(scores(s)[:, g, 0:CTX], q_ctx[:, p, c, b, h:h + 4, :].rearrange("p h n -> p (h n)"),
                                     ctxT[:, b, c, :], start=(c == 0), stop=(c == 1))
                last = nc.tensor.matmul(scores(s)[:, g, CTX:KEYS], null_bd[:, b % 2, h:h + 4, :].rearrange("p h n -> p (h n)"),
                                        core.ones[0:HEADS, 0:1], start=True, stop=True)
            last.then_inc(scored, 1)

        def output(t):
            pe.wait_ge(mix_out, (t + 1) * UNITS)
            for c in range(2):
                for h in range(HEADS):
                    nc.tensor.matmul(OUT, mixed_ctx[:, c, h, :], u_h[:, c, h, :], start=(c + h == 0), stop=False)
            pe.wait_ge(tail_in, (t + 1) * 16 * TAIL_DMAS)
            nc.tensor.matmul(OUT, tailT[:, :], tail_w[:, :], start=False, stop=True).then_inc(out_done, 1)

        def tile(t, p, before, after):
            n = t * UNITS
            for u in range(UNITS):
                b, s = u // 2, u % 2
                pe.wait_ge(scaled, n + u + 1)
                for g in range(2):
                    for k in range(2):
                        nc.tensor.transpose(TURNED[:, k * 2 * P + g * P:k * 2 * P + (g + 1) * P],
                                            prob[:, s, g, k * P:(k + 1) * P], core.c("ident"))
                if before and u == 1:
                    pe.wait_ge(z_copied, t)
                if after and u == NULL_STEP + 1:
                    pe.wait_ge(null_out, t + 2)
                nc.tensor.transpose(TURNED_TAIL, tail[:, s, :], core.c("ident")).then_inc(turned, 1)
                if ahead(t, u, after, 2):
                    score(*ahead(t, u, after, 2), p if u + 2 < UNITS else 1 - p)
                pe.wait_ge(lastT_done, n + u + 1)
                if before and u == 0:
                    output(t - 1)
                if after:
                    for k in Q_STEPS.get(u, ()):
                        q_part(t + 1, k)
                    if u == NULL_STEP:
                        null_part(t + 1)
                pe.wait_ge(probT_done, n + u + 1)
                if u or before:
                    pe.wait_ge(mix_out, n + u)
                for c in range(2):
                    dst = MIX[:, c * 2 * P:(c + 1) * 2 * P]
                    for k in range(2):
                        last = nc.tensor.matmul(dst, ctx[:, b, k, c * P:(c + 1) * P], probT[:, s, k, :],
                                                start=(k == 0), stop=(k == 1))
                last.then_inc(mixed, 1)

        pe.sem_inc(mixed, UNITS)
        pe.sem_inc(scored, 4)
        pe.sem_inc(q_out, 1)
        pe.sem_inc(out_done, 1)
        pe.sem_inc(z_used, 1)
        null_part(0)
        for k in range(8):
            q_part(0, k)
        score(0, 0, 0)
        score(0, 1, 0)
        over_tiles(pe, tile)
        output(TILES - 1)


def folded_attention(core, name):
    nc, dram = core.nc, core.dram
    S = 4
    CH = S * BT
    with ExitStack() as st:
        sb = lambda n, shape, dt=F32: st.enter_context(nc.sbuf_tensor(f"{name}_{n}", shape, dt))
        qkv_dram = nc.dram_tensor(f"{name}_qkv_scratch", (3, B, SEQ * D), F32).ap()
        out_dram = nc.dram_tensor(f"{name}_out_scratch", (B, SEQ * D), F32).ap()
        folded = lambda t: t.rearrange("b (r w) -> r b w", r=P)
        w = sb("w", [D, 3 * D])
        bias = sb("bias", [1, 3 * D])
        temp = sb("temp", [P, 1])
        head4 = sb("head4", [P, G])
        qkv = sb("qkv", [P, TILES, 3, D])
        rows = sb("rows", [P, 2, 3, CH, SEQ])
        k4 = sb("k4", [P, S, BT, G, SEQ])
        vbd = sb("vbd", [P, S, BT, G, SEQ])
        q4 = sb("q4", [P, S, BT, G, SEQ])
        qbd = sb("qbd", [P, S, BT * G, G, 8])
        prob = sb("prob", [P, S, HEADS, SEQ])
        top = sb("top", [P, S, HEADS])
        total = sb("total", [P, S, HEADS])
        res = sb("res", [P, B, SEQ])
        back = sb("back", [P, TILES, D])
        bank_a = lambda s: core.psum[:, 2 * s, :]
        bank_b = lambda s: core.psum[:, 2 * s + 1, :]
        front = Front(core, st, name, S, bank_a)
        (w_in, projected, qkv_done, stored, masked, scored, shifted, exped, normal, turned, qbd_done, mixed,
         res_done, res_stored, back_in, q4_done) = (core.sem(f"{name}_{n}") for n in (
             "w_in", "projected", "qkv_done", "stored", "masked", "scored", "shifted", "exped", "normal", "turned",
             "qbd_done", "mixed", "res_done", "res_stored", "back_in", "q4_done"))
        rows_in = [core.sem(f"{name}_rows_in{i}") for i in range(2)]

        with nc.Block() as block:
            @block.sync
            def _(sp):
                load(sp, [(w[:, :], dram[f"{name}_Wqkv"]), (bias[:, :], dram[f"{name}_bqkv"]),
                          (temp[:, :], dram[f"{name}_temp"])], w_in)
                with sp.Fori(0, TILES // S) as it:
                    sp.wait_ge(qkv_done, (it + 2) * S)
                    for f in range(3):
                        sp.dma_start(qkv_dram[f, ds(it * CH, CH), :].rearrange("(t b) (s d) -> (b s) t d", b=BT, d=D),
                                     qkv[:, ds(it * S, S), f, :]).then_inc(stored, 16)
                sp.wait_ge(stored, 16 * 3 * (TILES // S))

            @block.gpsimd
            def _(pool):
                with pool.Fori(0, TILES // S) as it:
                    front.pool_rstd(pool, it * S)

            @block.scalar
            def _(act):
                act.sem_inc(qkv_done, S)
                with act.Fori(0, TILES // S) as it:
                    n = it * S
                    front.act_copy(act, n)
                    for s in range(S):
                        act.wait_ge(projected, n + s + 1)
                        nc.scalar.copy(qkv[:, ds(n + s, 1), :, :].rearrange("p t f d -> p (t f d)"),
                                       bank_b(s)[:, 0:3 * D]).then_inc(qkv_done, 1)

            @block.vector
            def _(dve):
                dve.wait_ge(w_in, 48)
                nc.vector.tensor_scalar(head4[:, :], core.c("head4"), temp[:, :], None, ALU.mult)
                with dve.Fori(0, TILES // S) as it:
                    n = it * S
                    front.dve_moments(dve, n)
                    dve.wait_ge(qkv_done, n + S)
                    front.dve_normalise(dve, n)

            @block.tensor
            def _(pe):
                pe.wait_ge(w_in, 48)
                with pe.Fori(0, TILES // S) as it:
                    n = it * S
                    front.pe_transpose(pe, n)
                    for s in range(S):
                        pe.wait_ge(front.xnT_done, n + s + 1)
                        nc.tensor.matmul(bank_b(s)[:, 0:3 * D], front.xnT[:, s, :], w[:, :], start=True, stop=False)
                        nc.tensor.matmul(bank_b(s)[:, 0:3 * D], core.ones[0:1, :], bias[:, :], start=False,
                                         stop=True).then_inc(projected, 1)

        block = st.enter_context(nc.Block())

        @block.sync
        def _(sp):
            def load_rows(step, half):
                for f in range(3):
                    sp.dma_start(rows[:, half, f, :, :], folded(qkv_dram[f, ds(step * CH, CH), :])).then_inc(
                        rows_in[half], 16)

            def step_out(step):
                sp.wait_ge(res_done, (step + 2) * S)
                sp.dma_start(folded(out_dram[ds(step * CH, CH), :]), res[:, ds(step * CH, CH), :]).then_inc(
                    res_stored, 16)

            load_rows(0, 0)
            load_rows(1, 1)
            with sp.Fori(0, TILES // S // 2 - 1) as pair:
                for half in range(2):
                    step_out(pair * 2 + half)
                    load_rows(pair * 2 + half + 2, half)
            step_out(TILES // S - 2)
            step_out(TILES // S - 1)
            sp.wait_ge(res_stored, 16 * (TILES // S))
            sp.dma_start(back[:, :, :], out_dram.rearrange("(t b) (s d) -> (b s) t d", b=BT, d=D)).then_inc(back_in, 16)

        @block.gpsimd
        def _(pool):
            with pool.Fori(0, TILES // S // 2) as pair:
                for half in range(2):
                    n = (pair * 2 + half) * S
                    for s in range(S):
                        if s == 0:
                            pool.wait_ge(rows_in[half], (pair + 1) * 48)
                        pool.wait_ge(scored, n + s + 1)
                        here = slice(s * BT, (s + 1) * BT)
                        a, m = spread(rows[:, half, 1, here, :], head4[:, :], SEQ)
                        nc.gpsimd.tensor_tensor(k4[:, s, :, :, :], a, m, ALU.mult)
                        a, m = spread(rows[:, half, 2, here, :], core.c("group"), SEQ)
                        nc.gpsimd.tensor_tensor(vbd[:, s, :, :, :], a, m, ALU.mult).then_inc(masked, 1)

        @block.scalar
        def _(act):
            act.sem_inc(res_done, S)
            with act.Fori(0, TILES // S // 2) as pair:
                for half in range(2):
                    n = (pair * 2 + half) * S
                    for s in range(S):
                        act.wait_ge(masked, n + s + 1)
                        q = rows[:, half, 0, s * BT:(s + 1) * BT, :].rearrange("p b (a w) -> p b a w", a=1)
                        nc.scalar.copy(q4[:, s, :, :, :], q.to_broadcast([P, BT, G, SEQ])).then_inc(q4_done, 1)
                    for s in range(S):
                        act.wait_ge(shifted, n + s + 1)
                        nc.scalar.activation(prob[:, s, :, :], prob[:, s, :, :], ACT.Exp).then_inc(exped, 1)
                    for s in range(S):
                        act.wait_ge(mixed, n + s + 1)
                        nc.scalar.copy(res[:, ds((n + s) * BT, BT), :],
                                       bank_b(s)[:, 0:P].rearrange("p (b w) -> p b w", b=BT)).then_inc(res_done, 1)

        @block.vector
        def _(dve):
            mask = core.c("group").rearrange("p (a j w) -> p a j w", a=1, w=1).to_broadcast([P, BT * G, G, 8])
            with dve.Fori(0, TILES // S) as it:
                n = it * S
                for s in range(S):
                    dve.wait_ge(turned, n + s + 1)
                    nc.vector.tensor_tensor(qbd[:, s, :, :, :],
                                            bank_a(s).rearrange("p (a j w) -> p a j w", j=G, w=8), mask,
                                            ALU.mult).then_inc(qbd_done, 1)
                for streams in ((0, 1), (2, 3)):
                    for s in streams:
                        dve.wait_ge(scored, n + s + 1 + S)
                        nc.vector.tensor_reduce(top[:, s, :], bank_b(s).rearrange("p (a w) -> p a w", w=SEQ), X, ALU.max)
                    dve.drain()
                    for s in streams:
                        nc.vector.tensor_tensor(prob[:, s, :, :], bank_b(s).rearrange("p (a w) -> p a w", w=SEQ),
                                                per_row(top[:, s, :]), ALU.subtract).then_inc(shifted, 1)
                for streams in ((0, 1), (2, 3)):
                    for s in streams:
                        dve.wait_ge(exped, n + s + 1)
                        nc.vector.tensor_reduce(total[:, s, :], prob[:, s, :, :], X, ALU.add)
                    dve.drain()
                    for s in streams:
                        nc.vector.reciprocal(total[:, s, :], total[:, s, :])
                    dve.drain()
                    for s in streams:
                        nc.vector.tensor_tensor(prob[:, s, :, :], prob[:, s, :, :], per_row(total[:, s, :]),
                                                ALU.mult).then_inc(normal, 1)
            dve.wait_ge(back_in, 16)
            nc.vector.tensor_tensor(core.x[:, :, :], core.x[:, :, :], back[:, :, :], ALU.add)

        @block.tensor
        def _(pe):
            pe.sem_inc(scored, S)
            with pe.Fori(0, TILES // S) as it:
                n = it * S
                for s in range(S):
                    pe.wait_ge(q4_done, n + s + 1)
                    for b in range(BT):
                        last = nc.tensor.transpose(bank_a(s)[:, b * P:(b + 1) * P],
                                                   q4[:, s, b, :, :].rearrange("p j w -> p (j w)"), core.c("ident"))
                    last.then_inc(turned, 1)
                for s in range(S):
                    pe.wait_ge(masked, n + s + 1)
                    pe.wait_ge(res_done, n + s + 1)
                    for b in range(BT):
                        last = nc.tensor.matmul(bank_b(s)[:, b * P:(b + 1) * P],
                                                k4[:, s, b, :, :].rearrange("p j w -> p (j w)"),
                                                vbd[:, s, b, :, :].rearrange("p j w -> p (j w)"), start=True, stop=True)
                    last.then_inc(scored, 1)
                for s in range(S):
                    pe.wait_ge(normal, n + s + 1)
                    pe.wait_ge(qbd_done, n + s + 1)
                    for b in range(BT):
                        for g in range(G):
                            last = nc.tensor.matmul(bank_b(s)[g * 32:(g + 1) * 32, b * 32:(b + 1) * 32],
                                                    qbd[:, s, b * G + g, :, :].rearrange("p j w -> p (j w)"),
                                                    prob[:, s, b * G + g, :], start=True, stop=True)
                    last.then_inc(mixed, 1)


def quantised_ffn(core, name):
    nc, dram = core.nc, core.dram
    S, H = 4, 512
    C = H // P
    ROUND = 1.5 * 2.0 ** 23
    with ExitStack() as st:
        sb = lambda n, shape, dt=F32: st.enter_context(nc.sbuf_tensor(f"{name}_{n}", shape, dt))
        w1 = sb("w1", [D, H])
        w2 = sb("w2", [P, C, D])
        w1q = sb("w1q", [D, H], BF16)
        w2q = sb("w2q", [P, C, D], BF16)
        b1 = sb("b1", [1, H])
        b2 = sb("b2", [1, D])
        xn = sb("xn_all", [P, TILES, D])
        h = sb("h", [P, TILES, H])
        peak_x = sb("peak_x", [P, TILES])
        peak_h = sb("peak_h", [P, TILES])
        peaks = sb("peaks", [P, 4])
        most = sb("most", [P, 4])
        inv = sb("inv", [P, 4])
        scale = sb("scale", [P, 2])
        q = sb("q", [P, S, H])
        qT = sb("qT", [P, S, C, P], BF16)
        bank_a = lambda s: core.psum[:, 2 * s, :]
        bank_b = lambda s: core.psum[:, 2 * s + 1, :]
        front = Front(core, st, name, S, bank_a, transposed=False)
        (w_in, peaks_x, most_x, x_rounded, turned, qT_done, wide, gelued, peaks_h, most_h, h_rounded, turned2,
         hT_done, out_done) = (core.sem(f"{name}_{n}") for n in (
             "w_in", "peaks_x", "most_x", "x_rounded", "turned", "qT_done", "wide", "gelued", "peaks_h", "most_h",
             "h_rounded", "turned2", "hT_done", "out_done"))
        block = st.enter_context(nc.Block())

        @block.sync
        def _(sp):
            load(sp, [(w1[:, :], dram[f"{name}_w1_T"]), (w2[:, :, :], dram[f"{name}_w2_T"]),
                      (b1[:, :], dram[f"{name}_b1"]), (b2[:, :], dram[f"{name}_b2"])], w_in)

        @block.gpsimd
        def _(pool):
            with pool.Fori(0, TILES // S) as it:
                front.pool_rstd(pool, it * S)
            pool.wait_ge(peaks_x, 1)
            nc.gpsimd.partition_all_reduce(most[:, 0:3], peaks[:, 0:3], P,
                                           bass.bass_isa.ReduceOp.max).then_inc(most_x, 1)
            pool.wait_ge(peaks_h, 1)
            nc.gpsimd.partition_all_reduce(most[:, 3:4], peaks[:, 3:4], P,
                                           bass.bass_isa.ReduceOp.max).then_inc(most_h, 1)

        @block.scalar
        def _(act):
            with act.Fori(0, TILES // S) as it:
                n = it * S
                for s in range(S):
                    act.wait_ge(turned, n + s + 1)
                    nc.scalar.copy(qT[:, s, 0, :], bank_a(s)[:, 0:P]).then_inc(qT_done, 1)
                for s in range(S):
                    act.wait_ge(wide, n + s + 1)
                    nc.scalar.activation(h[:, ds(n + s, 1), :], bank_b(s), ACT.Gelu,
                                         scale=scale[:, 0:1]).then_inc(gelued, 1)
            with act.Fori(0, TILES // S) as it:
                n = it * S
                for s in range(S):
                    act.wait_ge(turned2, n + s + 1)
                    nc.scalar.copy(qT[:, s, :, :], bank_a(s).rearrange("p (c w) -> p c w", c=C)).then_inc(hT_done, 1)

        @block.vector
        def _(dve):
            def steps_of(i, j):
                m = most[:, i:j]
                nc.vector.tensor_scalar(m, m, 1e-6, 1.0 / 127.0, ALU.max, ALU.mult)
                dve.drain()
                nc.vector.reciprocal(inv[:, i:j], m)
                dve.drain()

            def rounded(dst, src, col, tmp):
                nc.vector.tensor_scalar(tmp, src, inv[:, col:col + 1], ROUND, ALU.mult, ALU.add)
                dve.drain()
                return nc.vector.tensor_scalar(dst, tmp, ROUND, None, ALU.subtract)

            with dve.Fori(0, TILES // S) as it:
                n = it * S
                front.dve_moments(dve, n)
                for s in range(S):
                    dve.wait_ge(front.rstd_done, n + s + 1)
                    nc.vector.tensor_scalar(xn[:, ds(n + s, 1), :], core.x[:, ds(n + s, 1), :], front.mv[:, s, 0:1],
                                            front.rstd[:, s, :], ALU.subtract, ALU.mult)
            dve.drain()
            nc.vector.tensor_reduce(peaks[:, 0:1], xn[:, :, :], XY, ALU.max, apply_absolute_value=True)
            dve.wait_ge(w_in, 64)
            nc.vector.tensor_reduce(peaks[:, 1:2], w1[:, :], X, ALU.max, apply_absolute_value=True)
            nc.vector.tensor_reduce(peaks[:, 2:3], w2[:, :, :], XY, ALU.max,
                                    apply_absolute_value=True).then_inc(peaks_x, 1)
            dve.wait_ge(most_x, 1)
            steps_of(0, 3)
            nc.vector.tensor_tensor(scale[:, 0:1], most[:, 0:1], most[:, 1:2], ALU.mult)
            rounded(w1q[:, :], w1[:, :], 1, q[:, 0, :])
            rounded(w2q[:, :, :].rearrange("p c d -> p (c d)"), w2[:, :, :].rearrange("p c d -> p (c d)"), 2, q[:, 1, :])
            with dve.Fori(0, TILES // S) as it:
                n = it * S
                dve.drain()
                for s in range(S):
                    nc.vector.tensor_scalar(xn[:, ds(n + s, 1), :], xn[:, ds(n + s, 1), :], inv[:, 0:1], ROUND,
                                            ALU.mult, ALU.add)
                dve.drain()
                for s in range(S):
                    nc.vector.tensor_scalar(q[:, s, 0:D], xn[:, ds(n + s, 1), :], ROUND, None,
                                            ALU.subtract).then_inc(x_rounded, 1)
                for s in range(S):
                    dve.wait_ge(gelued, n + s + 1)
                    nc.vector.tensor_reduce(peak_h[:, ds(n + s, 1)], h[:, ds(n + s, 1), :], XY, ALU.max,
                                            apply_absolute_value=True)
            dve.drain()
            nc.vector.tensor_reduce(peaks[:, 3:4], peak_h[:, :], X, ALU.max).then_inc(peaks_h, 1)
            dve.wait_ge(most_h, 1)
            steps_of(3, 4)
            nc.vector.tensor_tensor(scale[:, 1:2], most[:, 2:3], most[:, 3:4], ALU.mult)
            with dve.Fori(0, TILES // S) as it:
                n = it * S
                dve.drain()
                for s in range(S):
                    nc.vector.tensor_scalar(h[:, ds(n + s, 1), :], h[:, ds(n + s, 1), :], inv[:, 3:4], ROUND,
                                            ALU.mult, ALU.add)
                dve.drain()
                for s in range(S):
                    nc.vector.tensor_scalar(q[:, s, :], h[:, ds(n + s, 1), :], ROUND, None,
                                            ALU.subtract).then_inc(h_rounded, 1)
                for s in range(S):
                    dve.wait_ge(out_done, n + s + 1)
                    nc.vector.scalar_tensor_tensor(core.x[:, ds(n + s, 1), :], bank_b(s)[:, 0:D], scale[:, 1:2],
                                                   core.x[:, ds(n + s, 1), :], ALU.mult, ALU.add)

        @block.tensor
        def _(pe):
            pe.wait_ge(w_in, 64)
            with pe.Fori(0, TILES // S) as it:
                n = it * S
                for s in range(S):
                    pe.wait_ge(x_rounded, n + s + 1)
                    nc.tensor.transpose(bank_a(s)[:, 0:P], q[:, s, 0:D], core.c("ident")).then_inc(turned, 1)
                for s in range(S):
                    pe.wait_ge(qT_done, n + s + 1)
                    nc.tensor.matmul(bank_b(s), qT[:, s, 0, :], w1q[:, :], start=True, stop=False)
                    nc.tensor.matmul(bank_b(s), core.ones[0:1, :], b1[:, :], start=False, stop=True).then_inc(wide, 1)
            with pe.Fori(0, TILES // S) as it:
                n = it * S
                for s in range(S):
                    pe.wait_ge(h_rounded, n + s + 1)
                    for c in range(C):
                        last = nc.tensor.transpose(bank_a(s)[:, c * P:(c + 1) * P], q[:, s, c * P:(c + 1) * P],
                                                   core.c("ident"))
                    last.then_inc(turned2, 1)
                for s in range(S):
                    pe.wait_ge(hT_done, n + s + 1)
                    for c in range(C):
                        nc.tensor.matmul(bank_b(s)[:, 0:D], qT[:, s, c, :], w2q[:, c, :], start=(c == 0), stop=False)
                    nc.tensor.matmul(bank_b(s)[:, 0:D], core.ones[0:1, :], b2[:, :], start=False,
                                     stop=True).then_inc(out_done, 1)


def min_gru(core, name):
    nc, dram = core.nc, core.dram
    S, U = 8, 2
    N = S // U * P
    with ExitStack() as st:
        sb = lambda n, shape, dt=F32: st.enter_context(nc.sbuf_tensor(f"{name}_{n}", shape, dt))
        w = sb("w", [D, 3])
        neg = sb("neg", [D, 3])
        soft = sb("soft", [P, U, 2, N])
        relu = sb("relu", [P, U, 2, N])
        diff = sb("diff", [P, U, N])
        f_gate = sb("f_gate", [P, U, N])
        i_gate = sb("i_gate", [P, U, N])
        hid = sb("hid", [P, U, N])
        grown = sb("grown", [P, U, N])
        state = sb("state", [P, U, N])
        bank = lambda s: core.psum[:, s // 4, s % 4 * P:s % 4 * P + P]
        front = Front(core, st, name, S, bank, pack=4)
        unit = lambda u: front.xnT[:, u * 4:u * 4 + 4, :].rearrange("p s w -> p (s w)")
        (w_in, signed, softs, diffs, gates, states, out_done) = (core.sem(f"{name}_{n}") for n in (
            "w_in", "signed", "softs", "diffs", "gates", "states", "out_done"))
        block = st.enter_context(nc.Block())

        @block.sync
        def _(sp):
            load(sp, [(w[:, :], dram[f"{name}_W"])], w_in)

        @block.gpsimd
        def _(pool):
            with pool.Fori(0, TILES // S) as it:
                front.pool_rstd(pool, it * S)

        @block.scalar
        def _(act):
            act.wait_ge(w_in, 16)
            with act.Fori(0, TILES // S) as it:
                front.act_copy(act, it * S)
                n = it * U
                act.drain()
                for u in range(U):
                    for k in range(2):
                        nc.scalar.activation(soft[:, u, k, :], unit(u), ACT.Abs, scale=w[:, k:k + 1])
                act.drain()
                for u in range(U):
                    nc.scalar.activation(soft[:, u, :, :], soft[:, u, :, :], ACT.Exp, scale=-1.0)
                act.drain()
                for u in range(U):
                    nc.scalar.activation(soft[:, u, :, :], soft[:, u, :, :], ACT.Ln, bias=1.0).then_inc(softs, 1)
                for u in range(U):
                    nc.scalar.activation(hid[:, u, :], unit(u), ACT.Sigmoid, scale=w[:, 2:3])
                    act.wait_ge(diffs, n + u + 1)
                    nc.scalar.activation(f_gate[:, u, :], diff[:, u, :], ACT.Sigmoid, scale=-1.0)
                    nc.scalar.activation(i_gate[:, u, :], diff[:, u, :], ACT.Sigmoid).then_inc(gates, 1)

        @block.vector
        def _(dve):
            dve.wait_ge(w_in, 16)
            nc.vector.tensor_scalar(neg[:, :], w[:, :], -1.0, None, ALU.mult)
            def step(it, more):
                n = it * U
                for u in range(U):
                    dve.wait_ge(front.xnT_done, it * S + 4 * u + 4)
                    for k in range(2):
                        nc.vector.tensor_scalar(relu[:, u, k, :], unit(u), neg[:, k:k + 1], 0.0, ALU.mult, ALU.max)
                    nc.vector.tensor_scalar(grown[:, u, :], unit(u), w[:, 2:3], 0.5 + 1e-8, ALU.mult, ALU.add)
                dve.drain()
                for u in range(U):
                    dve.wait_ge(softs, n + u + 1)
                    nc.vector.tensor_tensor(soft[:, u, :, :], soft[:, u, :, :], relu[:, u, :, :], ALU.add)
                dve.drain()
                for u in range(U):
                    nc.vector.tensor_tensor(diff[:, u, :], soft[:, u, 0, :], soft[:, u, 1, :],
                                            ALU.subtract).then_inc(diffs, 1)
                if more:
                    front.dve_moments(dve, (it + 1) * S)
                    front.dve_normalise(dve, (it + 1) * S)
                for u in range(U):
                    dve.wait_ge(gates, n + u + 1)
                    nc.vector.tensor_tensor(grown[:, u, :], grown[:, u, :], hid[:, u, :], ALU.max)
                    nc.vector.memset(f_gate[:, u, :].rearrange("p (b t) -> p b t", t=SEQ)[:, :, 0:1], 0.0)
                dve.drain()
                for u in range(U):
                    nc.vector.tensor_tensor(grown[:, u, :], grown[:, u, :], i_gate[:, u, :], ALU.mult)
                dve.drain()
                for u in range(U):
                    nc.vector.tensor_tensor_scan(state[:, u, :], f_gate[:, u, :], grown[:, u, :], 0.0, ALU.mult,
                                                 ALU.add).then_inc(states, 1)
                for u in range(U):
                    dve.wait_ge(out_done, n + u + 1)
                    x = core.x[:, ds(it * S + 4 * u, 4), :]
                    nc.vector.tensor_tensor(x, x, core.psum[:, 4 + u, :].rearrange("p (t w) -> p t w", w=D), ALU.add)

            front.dve_moments(dve, 0)
            front.dve_normalise(dve, 0)
            over_steps(dve, TILES // S, step)

        @block.tensor
        def _(pe):
            with pe.Fori(0, TILES // S) as it:
                front.pe_transpose(pe, it * S)
                for u in range(U):
                    pe.wait_ge(states, it * U + u + 1)
                    for t in range(4):
                        last = nc.tensor.transpose(core.psum[:, 4 + u, t * P:(t + 1) * P],
                                                   state[:, u, t * P:(t + 1) * P], core.c("ident"))
                    last.then_inc(out_done, 1)


def lora_experts(core, name):
    nc, dram = core.nc, core.dram
    S, E, R = 4, 8, 4
    with ExitStack() as st:
        sb = lambda n, shape, dt=F32: st.enter_context(nc.sbuf_tensor(f"{name}_{n}", shape, dt))
        w = sb("w", [D, D])
        w_gate = sb("w_gate", [D, E + E * R])
        right = sb("right", [E * R, D])
        b_lin = sb("b_lin", [1, D])
        gate = sb("gate", [P, S, E])
        best = sb("best", [P, S, E])
        index = sb("index", [P, S, E], U32)
        index_f = sb("index_f", [P, S, E])
        chosen = sb("chosen", [P, S, 2, E])
        total = sb("total", [P, S, 1])
        narrow = sb("narrow", [P, S, E, R])
        narrowT = sb("narrowT", [E * R, S, P])
        bank_a = lambda s: core.psum[:, 2 * s, :]
        bank_b = lambda s: core.psum[:, 2 * s + 1, :]
        front = Front(core, st, name, S, bank_a)
        (w_in, gated, shifted, exped, weighted, turned, narrowT_done, out_done) = (core.sem(f"{name}_{n}") for n in (
            "w_in", "gated", "shifted", "exped", "weighted", "turned", "narrowT_done", "out_done"))
        block = st.enter_context(nc.Block())

        @block.sync
        def _(sp):
            load(sp, [(w[:, :], dram[f"{name}_W_lin_T"]), (w_gate[:, :], dram[f"{name}_gate_left"]),
                      (right[:, :], dram[f"{name}_right"]), (b_lin[:, :], dram[f"{name}_b_lin"])], w_in)

        @block.gpsimd
        def _(pool):
            with pool.Fori(0, TILES // S) as it:
                front.pool_rstd(pool, it * S)

        @block.scalar
        def _(act):
            with act.Fori(0, TILES // S) as it:
                n = it * S
                front.act_copy(act, n)
                for s in range(S):
                    act.wait_ge(shifted, n + s + 1)
                    nc.scalar.activation(gate[:, s, :], gate[:, s, :], ACT.Exp,
                                         accum_out=total[:, s, :]).then_inc(exped, 1)
                for s in range(S):
                    act.wait_ge(turned, n + s + 1)
                    nc.scalar.copy(narrowT[:, s, :], bank_a(s)[0:E * R, 0:P]).then_inc(narrowT_done, 1)

        @block.vector
        def _(dve):
            def step(it, more):
                n = it * S
                for s in range(S):
                    dve.wait_ge(gated, n + s + 1)
                    nc.vector.tensor_copy(gate[:, s, :], bank_a(s)[:, P:P + E])
                dve.drain()
                for s in range(S):
                    nc.vector.max(best[:, s, :], gate[:, s, :])
                dve.drain()
                for s in range(S):
                    nc.vector.max_index(index[:, s, :], best[:, s, :], gate[:, s, :])
                dve.drain()
                nc.vector.tensor_copy(index_f[:, :, :], index[:, :, :])
                for s in range(S):
                    nc.vector.tensor_scalar(gate[:, s, :], gate[:, s, :], best[:, s, 0:1], None,
                                            ALU.subtract).then_inc(shifted, 1)
                dve.drain()
                for s in range(S):
                    for k in range(2):
                        nc.vector.tensor_scalar(chosen[:, s, k, :], core.c("iota8"), index_f[:, s, k:k + 1], None,
                                                ALU.is_equal)
                dve.drain()
                nc.vector.tensor_tensor(chosen[:, :, 0, :], chosen[:, :, 0, :], chosen[:, :, 1, :], ALU.add)
                dve.drain()
                for s in range(S):
                    dve.wait_ge(exped, n + s + 1)
                    nc.vector.reciprocal(total[:, s, :], total[:, s, :])
                dve.drain()
                for s in range(S):
                    nc.vector.scalar_tensor_tensor(gate[:, s, :], gate[:, s, :], total[:, s, :], chosen[:, s, 0, :],
                                                   ALU.mult, ALU.mult)
                dve.drain()
                for s in range(S):
                    weight = gate[:, s, :].rearrange("p (e r) -> p e r", r=1).to_broadcast([P, E, R])
                    nc.vector.tensor_tensor(narrow[:, s, :, :],
                                            bank_a(s)[:, P + E:P + E + E * R].rearrange("p (e r) -> p e r", r=R),
                                            weight, ALU.mult).then_inc(weighted, 1)
                if more:
                    front.dve_moments(dve, n + S)
                    front.dve_normalise(dve, n + S)
                for s in range(S):
                    dve.wait_ge(out_done, n + s + 1)
                    add_to_x(core, n + s, bank_b(s)[:, 0:D])

            front.dve_moments(dve, 0)
            front.dve_normalise(dve, 0)
            over_steps(dve, TILES // S, step)

        @block.tensor
        def _(pe):
            pe.wait_ge(w_in, 64)
            with pe.Fori(0, TILES // S) as it:
                n = it * S
                front.pe_transpose(pe, n)
                for s in range(S):
                    pe.wait_ge(front.xnT_done, n + s + 1)
                    nc.tensor.matmul(bank_a(s)[:, P:P + E + E * R], front.xnT[:, s, :], w_gate[:, :], start=True,
                                     stop=True).then_inc(gated, 1)
                for s in range(S):
                    pe.wait_ge(weighted, n + s + 1)
                    nc.tensor.transpose(bank_a(s)[0:E * R, 0:P],
                                        narrow[:, s, :, :].rearrange("p e r -> p (e r)"),
                                        core.c("ident")).then_inc(turned, 1)
                for s in range(S):
                    out = bank_b(s)[:, 0:D]
                    nc.tensor.matmul(out, front.xnT[:, s, :], w[:, :], start=True, stop=False)
                    nc.tensor.matmul(out, core.ones[0:1, :], b_lin[:, :], start=False, stop=False)
                    pe.wait_ge(narrowT_done, n + s + 1)
                    nc.tensor.matmul(out, narrowT[:, s, :], right[:, :], start=False, stop=True).then_inc(out_done, 1)


def finish(core):
    nc = core.nc
    stored = core.sem("stored")
    with nc.Block() as block:
        @block.sync
        def _(sp):
            sp.dma_start(core.dram["out"].rearrange("(t p) d -> p t d", p=P), core.x[:, :, :]).then_inc(stored, 16)
            sp.wait_ge(stored, 16)


def program(nc, dram):
    with ExitStack() as ctx:
        core = Core(nc, dram, ctx)
        start(core)
        for stage in (
            lambda: depool_cross(core, "L0_xattn"),
            lambda: rotary_attention(core, "L0_attn"),
            lambda: product_key_experts(core, "L0_ffn"),
            core.clear_sems,
            lambda: context_attention(core, "L1_xattn"),
            lambda: gated_scan(core, "L1_attn"),
            lambda: ternary_ffn(core, "L1_ffn"),
            core.clear_sems,
            lambda: wide_context_attention(core, "L2_xattn"),
            lambda: folded_attention(core, "L2_attn"),
            lambda: quantised_ffn(core, "L2_ffn"),
            core.clear_sems,
            lambda: depool_cross(core, "L3_xattn"),
            lambda: min_gru(core, "L3_attn"),
            lambda: lora_experts(core, "L3_ffn"),
        ):
            stage()
        finish(core)


def layouts(v):
    a = {"constants": constants(), "x": v["x"].reshape(B * SEQ, D), "ctx_2048": v["ctx_2048"],
         "mask_BxS2_if0": v["mask_BxS2_if0"]}
    for n in ("L0_xattn", "L3_xattn"):
        a[f"{n}_W_in_T"] = v[f"{n}_W_in"].T
        a[f"{n}_g_res"] = v[f"{n}_g_res"].reshape(D, 1)
        a[f"{n}_b_in"] = v[f"{n}_b_in"].reshape(1, D)
        a[f"{n}_g_init"] = v[f"{n}_g_init"].reshape(1, CD)
    pair = np.arange(D) ^ 1
    wk = np.repeat(v["L0_attn_Wk"].reshape(D, G, 1, 8), G, axis=2).reshape(D, D)
    wq = v["L0_attn_Wq"]
    a["L0_attn_Wqk"] = np.stack([wq, wq[:, pair], wk, wk[:, pair]], axis=1)
    a["L0_attn_Wv"] = v["L0_attn_Wv"]
    a["L0_attn_Wo"] = v["L0_attn_Wo"].reshape(G, G, 8, D).transpose(0, 2, 1, 3).reshape(G * 8, G, D)
    a["L0_ffn_w_q"] = v["L0_ffn_w_q"]
    a["L0_ffn_w_q_T"] = v["L0_ffn_w_q"].T.reshape(16, P, D).transpose(1, 0, 2)
    a["L0_ffn_keys"] = v["L0_ffn_keys"].transpose(3, 2, 0, 1).reshape(P, 16, 32)
    a["L0_ffn_gamma"] = v["L0_ffn_bn_gamma"].reshape(16, P).T
    a["L0_ffn_beta"] = v["L0_ffn_bn_beta"].reshape(16, P).T
    a["L0_ffn_down_T"] = v["L0_ffn_down_embed"].T
    a["L0_ffn_up"] = v["L0_ffn_up_embed"].reshape(8, P, D).transpose(1, 0, 2)
    a["ctx_T"] = v["ctx_2048"].transpose(0, 2, 1)
    a["L1_xattn_w_qkv_T"] = v["L1_xattn_w_qkv"].T
    a["L1_xattn_w_proj_T"] = v["L1_xattn_w_proj"].T
    a["L1_xattn_b_proj"] = v["L1_xattn_b_proj"].reshape(1, D)
    halves = lambda t: t.reshape(2, P, -1).transpose(1, 0, 2)
    a["L1_attn_W_in"] = v["L1_attn_W_in"].reshape(D, 4, P)
    a["L1_attn_W_x"] = halves(v["L1_attn_W_x"])
    a["L1_attn_W_dt"] = v["L1_attn_W_dt"].reshape(16, 2, P)
    a["L1_attn_W_Bp"] = v["L1_attn_W_Bp"].reshape(16, 2, P)
    a["L1_attn_W_out"] = halves(v["L1_attn_W_out"])
    a["L1_attn_conv_w"] = halves(v["L1_attn_conv_w"].reshape(2 * P, 4))
    a["L1_attn_b_dt"] = v["L1_attn_b_dt"].reshape(2, P).T
    a["L1_attn_D_param"] = v["L1_attn_D_param"].reshape(2, P).T
    a["L1_ffn_W_fc_T"] = v["L1_ffn_W_fc"].T
    a["L1_ffn_W_proj_T"] = v["L1_ffn_W_proj"].T.reshape(4, P, D).transpose(1, 0, 2)
    a["L1_ffn_ln_w"] = v["L1_ffn_ln_w"].reshape(4, P).T
    a["L1_ffn_ln_b"] = v["L1_ffn_ln_b"].reshape(4, P).T
    F = 64
    heads = lambda w: w.reshape(-1, HEADS, F).transpose(2, 1, 0)
    a["L2_xattn_WqT"] = heads(v["L2_xattn_Wq"])
    a["L2_xattn_WkT"] = heads(v["L2_xattn_Wkv"][:, 0:HEADS * F])
    a["L2_xattn_WvT"] = heads(v["L2_xattn_Wkv"][:, HEADS * F:])
    a["L2_xattn_Wo"] = v["L2_xattn_Wout"].reshape(HEADS, F, D).transpose(1, 0, 2)
    a["L2_xattn_null_kv_T"] = v["L2_xattn_null_kv"].T
    a["L2_xattn_ln_scale"] = v["L2_xattn_ln_scale"].reshape(1, D)
    a["L2_xattn_ln_bias"] = v["L2_xattn_ln_bias"].reshape(1, D)
    a["L2_xattn_ctx_last_T"] = v["ctx_2048"][:, CTX - 1, :].T.reshape(2, P, B).transpose(1, 0, 2)
    a["L2_attn_Wqkv"] = np.concatenate([v[f"L2_attn_W{f}"] for f in "qkv"], axis=1)
    a["L2_attn_bqkv"] = np.concatenate([v[f"L2_attn_b{f}"] for f in "qkv"]).reshape(1, 3 * D)
    a["L2_attn_temp"] = np.repeat(v["L2_attn_temperature"].reshape(HEADS), 8).reshape(P, 1)
    a["L2_ffn_w1_T"] = v["L2_ffn_w1"].T
    a["L2_ffn_w2_T"] = v["L2_ffn_w2"].T.reshape(4, P, D).transpose(1, 0, 2)
    a["L2_ffn_b1"] = v["L2_ffn_b1"].reshape(1, -1)
    a["L2_ffn_b2"] = v["L2_ffn_b2"].reshape(1, -1)
    a["L3_attn_W"] = np.stack([v[f"L3_attn_W{f}"].reshape(D) for f in "fih"], axis=1)
    a["L3_ffn_W_lin_T"] = v["L3_ffn_W_lin"].T
    a["L3_ffn_gate_left"] = np.concatenate(
        [v["L3_ffn_gate_w"].T, v["L3_ffn_left"].transpose(1, 0, 2).reshape(D, -1)], axis=1)
    a["L3_ffn_right"] = v["L3_ffn_right"].reshape(-1, D)
    a["L3_ffn_b_lin"] = v["L3_ffn_b_lin"].reshape(1, D)
    return {k: np.ascontiguousarray(t) for k, t in a.items()}


def kernel(**inputs):
    import concourse.bacc as bacc
    from concourse.bass_utils import run_bass_kernel_spmd

    arrays = layouts({k: np.asarray(v) for k, v in inputs.items()})
    nc = bacc.Bacc("TRN2", target_bir_lowering=False, num_devices=1)
    dram = {k: nc.dram_tensor(f"{k}_dram", a.shape, mybir.dt.from_np(a.dtype), kind="ExternalInput").ap()
            for k, a in arrays.items()}
    dram["out"] = nc.dram_tensor("out_dram", (B * SEQ, D), F32, kind="ExternalOutput").ap()
    program(nc, dram)
    got = run_bass_kernel_spmd(nc, [{f"{k}_dram": a for k, a in arrays.items()}], core_ids=[0])
    return got.results[0]["out_dram"].reshape(B, SEQ, D)
```
